# Optimizing a Trainium2 kernel written in Bass

```python
import numpy as np
import jax
import jax.numpy as jnp

def _softmax(x, axis=-1):
    return jax.nn.softmax(x, axis=axis)

def _gelu(x):
    return jax.nn.gelu(x, approximate=True)

def _silu(x):
    return jax.nn.silu(x)

def _sigmoid(x):
    return jax.nn.sigmoid(x)

def _layernorm(x, axis=-1, eps=1e-05):
    m = jnp.mean(x, axis=axis, keepdims=True)
    v = jnp.var(x, axis=axis, keepdims=True)
    return (x - m) / jnp.sqrt(v + eps)

def _scatter_add(tgt, idx, src, axis=0):
    return tgt.at[idx].add(src)

def _segment_sum(src, seg, n):
    return jax.ops.segment_sum(src, seg, n)
kernel_name = 'mk_flamingo_gated_d2_seqx_r4_efabc9'

def setup_inputs(seed: int=0):
    np.random.seed(seed)
    _w = jnp.asarray

    def _rec_inputs():
        import jax
        import jax.numpy as jnp
        _rk = jax.random.key(seed)
        x = -0.0002928 + 1 * jax.random.normal(jax.random.fold_in(_rk, 1), (32, 112, 256), jnp.float32)
        _lenS = 112 - jax.random.randint(jax.random.fold_in(_rk, 7), (32,), 0, max(1, 112 // 4) + 1, jnp.int32)
        _lenS2 = 375 - jax.random.randint(jax.random.fold_in(_rk, 8), (32,), 0, max(1, 375 // 4) + 1, jnp.int32)
        _ctx_1024P = jax.random.normal(jax.random.fold_in(_rk, 11), (32, 16, 256), jnp.float32)
        _ctx_1024c = jax.random.dirichlet(jax.random.fold_in(_rk, 511), 0.3 * jnp.ones((16,), jnp.float32), (32, 375))
        _ctx_1024t = jnp.einsum('bsk,bkd->bsd', _ctx_1024c, _ctx_1024P)
        _ctx_1024t = _ctx_1024t * jax.lax.rsqrt(jnp.mean(jnp.square(_ctx_1024t)) + 1e-12) * 0.953939
        ctx_1024 = -1.39393e-06 + 0.999914 * (_ctx_1024t + 0.3 * jax.random.normal(jax.random.fold_in(_rk, 611), (32, 375, 256), jnp.float32))
        _validS = jnp.arange(112)[None, :] < _lenS[:, None]
        _validS2 = jnp.arange(375)[None, :] < _lenS2[:, None]
        _causal = jnp.tril(jnp.ones((112, 112), dtype=bool))
        mask_1x1xSxS2_ik1 = jnp.where(jnp.broadcast_to(_validS2[0:1, None, None, :], (1, 1, 112, 375)), 1, 0).astype(jnp.int32)
        mask_BxSxS2_if1 = jnp.where(jnp.ones((32, 112, 375), dtype=bool), 1, 0).astype(jnp.int32)
        _g = jax.random.normal(jax.random.fold_in(_rk, 9001), (2, 2), jnp.float32)
        _g = jnp.sign(_g) * jnp.maximum(jnp.abs(_g), 1.0) + (_g == 0) * 1.0
        g_xattn = _g[0]
        g_ffn = _g[1]
        return (x, ctx_1024, mask_1x1xSxS2_ik1, mask_BxSxS2_if1, g_xattn, g_ffn)
    x, ctx_1024, mask_1x1xSxS2_ik1, mask_BxSxS2_if1, g_xattn, g_ffn = _rec_inputs()

    def _L0_xattn_setup():
        import jax, jax.numpy as jnp
        import numpy as np
        D_MODEL = 256
        N_HEAD = 16
        D_K = D_MODEL // N_HEAD
        B, S = (2, 512)
        NEG = -1000000000.0
        key = jax.random.key(seed)
        ks = jax.random.split(key, 9)
        inp = {'input_q': jax.random.normal(ks[0], (B, S, D_MODEL), dtype=jnp.float32), 'input_k': jax.random.normal(ks[1], (B, S, D_MODEL), dtype=jnp.float32), 'input_v': jax.random.normal(ks[2], (B, S, D_MODEL), dtype=jnp.float32), 'mask': jax.random.randint(ks[3], (1, 1, S, S), 0, 2, dtype=jnp.int32), 'w_q': jax.random.normal(ks[4], (D_MODEL, D_MODEL), dtype=jnp.float32) / np.sqrt(D_MODEL), 'w_k': jax.random.normal(ks[5], (D_MODEL, D_MODEL), dtype=jnp.float32) / np.sqrt(D_MODEL), 'w_v': jax.random.normal(ks[6], (D_MODEL, D_MODEL), dtype=jnp.float32) / np.sqrt(D_MODEL), 'w_o': jax.random.normal(ks[7], (D_MODEL, D_MODEL), dtype=jnp.float32) / np.sqrt(D_MODEL), 'b_o': jax.random.normal(ks[8], (D_MODEL,), dtype=jnp.float32) * 0.01}
        return inp
    _L0_xattn_all = _L0_xattn_setup()
    _L0_xattn_in = {k: v for k, v in _L0_xattn_all.items() if k in ('w_q', 'w_k', 'w_v', 'w_o', 'b_o')}
    del _L0_xattn_all

    def _L0_ffn_setup():
        import jax, jax.numpy as jnp
        import numpy as np
        import math
        D_IN = 256
        FEATURES = (1024, 1024, 256)
        BATCH, SEQ = (8, 512)

        def _conn_dense(kernel_bool, x):
            w = jnp.where(kernel_bool, jnp.float32(1.0), jnp.float32(-1.0))
            return x @ w
        key = jax.random.key(seed)
        kx, kk0, kk1, kk2 = jax.random.split(key, 4)
        x = jax.random.normal(kx, (BATCH, SEQ, D_IN), dtype=jnp.float32)
        k0 = jax.random.randint(kk0, (2 * D_IN, FEATURES[0]), 0, 2).astype(jnp.bool_)
        k1 = jax.random.randint(kk1, (FEATURES[0], FEATURES[1]), 0, 2).astype(jnp.bool_)
        k2 = jax.random.randint(kk2, (FEATURES[1], FEATURES[2]), 0, 2).astype(jnp.bool_)
        s0 = jnp.asarray(1.0 / math.sqrt(2 * D_IN), dtype=jnp.float32)
        s1 = jnp.asarray(1.0 / math.sqrt(FEATURES[0]), dtype=jnp.float32)
        s2 = jnp.asarray(1.0 / math.sqrt(FEATURES[1]), dtype=jnp.float32)
        return {'x': x, 'k0': k0, 'k1': k1, 'k2': k2, 's0': s0, 's1': s1, 's2': s2}
    _L0_ffn_all = _L0_ffn_setup()
    _L0_ffn_in = {k: v for k, v in _L0_ffn_all.items() if k in ('k0', 'k1', 'k2', 's0', 's1', 's2')}
    del _L0_ffn_all

    def _L1_xattn_setup():
        import jax, jax.numpy as jnp
        import numpy as np
        H = 16
        key = jax.random.key(seed)
        ks = jax.random.split(key, 8)
        B, T, D = (4, 512, 256)
        s = 0.02
        return {'query': jax.random.normal(ks[0], (B, T, D), jnp.float32), 'key': jax.random.normal(ks[1], (B, T, D), jnp.float32), 'value': jax.random.normal(ks[2], (B, T, D), jnp.float32), 'mask': jnp.ones((B, T, T), jnp.int32), 'Wq': jax.random.normal(ks[3], (D, D), jnp.float32) * s, 'Wk': jax.random.normal(ks[4], (D, D), jnp.float32) * s, 'Wv': jax.random.normal(ks[5], (D, D), jnp.float32) * s, 'Wo': jax.random.normal(ks[6], (D, D), jnp.float32) * s, 'bo': jnp.zeros((D,), jnp.float32)}
    _L1_xattn_all = _L1_xattn_setup()
    _L1_xattn_in = {k: v for k, v in _L1_xattn_all.items() if k in ('Wq', 'Wk', 'Wv', 'Wo', 'bo')}
    del _L1_xattn_all

    def _L1_ffn_setup():
        import math
        import jax, jax.numpy as jnp
        import numpy as np
        B, S, D, F, E = (8, 512, 256, 1024, 8)
        CAPACITY_FACTOR = 1.0
        key = jax.random.key(seed)
        k1, k2, k3, k4 = jax.random.split(key, 4)
        x = jax.random.normal(k1, (B, S, D), dtype=jnp.float32)
        Wr = jax.random.normal(k2, (D, E), dtype=jnp.float32) * (1.0 / math.sqrt(D))
        W1 = jax.random.normal(k3, (E, D, F), dtype=jnp.float32) * (1.0 / math.sqrt(D))
        W2 = jax.random.normal(k4, (E, F, D), dtype=jnp.float32) * (1.0 / math.sqrt(F))
        return {'x': x, 'Wr': Wr, 'W1': W1, 'W2': W2}
    _L1_ffn_all = _L1_ffn_setup()
    _L1_ffn_in = {k: v for k, v in _L1_ffn_all.items() if k in ('Wr', 'W1', 'W2')}
    del _L1_ffn_all
    return {'x': x, 'ctx_1024': ctx_1024, 'mask_1x1xSxS2_ik1': mask_1x1xSxS2_ik1, 'mask_BxSxS2_if1': mask_BxSxS2_if1, 'g_xattn': g_xattn, 'g_ffn': g_ffn, 'L0_xattn_w_q': _L0_xattn_in['w_q'], 'L0_xattn_w_k': _L0_xattn_in['w_k'], 'L0_xattn_w_v': _L0_xattn_in['w_v'], 'L0_xattn_w_o': _L0_xattn_in['w_o'], 'L0_xattn_b_o': _L0_xattn_in['b_o'], 'L0_ffn_k0': _L0_ffn_in['k0'], 'L0_ffn_k1': _L0_ffn_in['k1'], 'L0_ffn_k2': _L0_ffn_in['k2'], 'L0_ffn_s0': _L0_ffn_in['s0'], 'L0_ffn_s1': _L0_ffn_in['s1'], 'L0_ffn_s2': _L0_ffn_in['s2'], 'L1_xattn_Wq': _L1_xattn_in['Wq'], 'L1_xattn_Wk': _L1_xattn_in['Wk'], 'L1_xattn_Wv': _L1_xattn_in['Wv'], 'L1_xattn_Wo': _L1_xattn_in['Wo'], 'L1_xattn_bo': _L1_xattn_in['bo'], 'L1_ffn_Wr': _L1_ffn_in['Wr'], 'L1_ffn_W1': _L1_ffn_in['W1'], 'L1_ffn_W2': _L1_ffn_in['W2']}

def reference(x, ctx_1024, mask_1x1xSxS2_ik1, mask_BxSxS2_if1, g_xattn, g_ffn, L0_xattn_w_q, L0_xattn_w_k, L0_xattn_w_v, L0_xattn_w_o, L0_xattn_b_o, L0_ffn_k0, L0_ffn_k1, L0_ffn_k2, L0_ffn_s0, L0_ffn_s1, L0_ffn_s2, L1_xattn_Wq, L1_xattn_Wk, L1_xattn_Wv, L1_xattn_Wo, L1_xattn_bo, L1_ffn_Wr, L1_ffn_W1, L1_ffn_W2):
    import jax
    import jax.numpy as jnp

    def _L0_xattn_ref(input_q, input_k, input_v, mask, w_q, w_k, w_v, w_o, b_o):
        import jax, jax.numpy as jnp
        import numpy as np
        D_MODEL = 256
        N_HEAD = 16
        D_K = D_MODEL // N_HEAD
        B, S = (2, 512)
        NEG = -1000000000.0
        b = input_q.shape[0]

        def split_heads(x):
            return x.reshape(b, -1, N_HEAD, D_K).transpose(0, 2, 1, 3)
        q = split_heads(input_q @ w_q)
        k = split_heads(input_k @ w_k)
        v = split_heads(input_v @ w_v)
        scores = jnp.einsum('bhqd,bhkd->bhqk', q, k) / jnp.sqrt(jnp.float32(D_K))
        scores = jnp.where(mask == 0, jnp.float32(NEG), scores)
        attn = jax.nn.softmax(scores, axis=-1)
        per_head = jnp.einsum('bhqk,bhkd->bhqd', attn, v)
        concat = per_head.transpose(0, 2, 1, 3).reshape(b, -1, N_HEAD * D_K)
        return concat @ w_o + b_o

    def _L0_ffn_ref(x, k0, k1, k2, s0, s1, s2):
        import jax, jax.numpy as jnp
        import numpy as np
        import math
        D_IN = 256
        FEATURES = (1024, 1024, 256)
        BATCH, SEQ = (8, 512)

        def _conn_dense(kernel_bool, x):
            w = jnp.where(kernel_bool, jnp.float32(1.0), jnp.float32(-1.0))
            return x @ w
        h = jnp.concatenate([x, -x], axis=-1)
        h = s0 * _conn_dense(k0, h)
        h = jax.nn.relu(h) * 2
        h = s1 * _conn_dense(k1, h)
        h = jax.nn.relu(h) * 2
        h = s2 * _conn_dense(k2, h)
        return h

    def _L1_xattn_ref(query, key, value, mask, Wq, Wk, Wv, Wo, bo):
        import jax, jax.numpy as jnp
        import numpy as np
        H = 16
        B, Tq, _ = query.shape
        Tk = key.shape[1]
        Dv = Wv.shape[0]
        Q = jnp.einsum('btd,ed->bte', query, Wq).reshape(B, Tq, H, -1).transpose(0, 2, 1, 3)
        K = jnp.einsum('btd,ed->bte', key, Wk).reshape(B, Tk, H, -1).transpose(0, 2, 1, 3)
        V = jnp.einsum('btd,ed->bte', value, Wv).reshape(B, Tk, H, -1).transpose(0, 2, 1, 3)
        d_k = K.shape[-1]
        scores = jnp.einsum('bhqd,bhkd->bhqk', Q, K) / jnp.sqrt(jnp.asarray(d_k, Q.dtype))
        scores = jnp.where(mask[:, None] == 0, jnp.asarray(-1000000000.0, scores.dtype), scores)
        attn = jax.nn.softmax(scores, axis=-1)
        Z = jnp.einsum('bhqk,bhkd->bhqd', attn, V)
        Zc = Z.transpose(0, 2, 1, 3).reshape(B, Tq, Dv)
        return jnp.einsum('btd,ed->bte', Zc, Wo) + bo

    def _L1_ffn_ref(x, Wr, W1, W2):
        import math
        import jax, jax.numpy as jnp
        import numpy as np
        B, S, D, F, E = (8, 512, 256, 1024, 8)
        CAPACITY_FACTOR = 1.0
        b, s, d = x.shape
        t = b * s
        cap = max(math.ceil(t * CAPACITY_FACTOR / E), 1)
        xf = x.reshape(t, d)
        probs = jax.nn.softmax(xf.astype(jnp.float32) @ Wr, axis=-1)
        eidx = jnp.argmax(probs, axis=-1)
        p_tok = jnp.take_along_axis(probs, eidx[:, None], axis=1)[:, 0]
        onehot = jax.nn.one_hot(eidx, E, dtype=jnp.int32)
        rank_all = jnp.cumsum(onehot, axis=0) - onehot
        rank = jnp.take_along_axis(rank_all, eidx[:, None], axis=1)[:, 0]
        keep = rank < cap
        slot = jnp.where(keep, rank, cap)
        dispatch = jnp.zeros((E, cap + 1), dtype=jnp.int32).at[eidx, slot].set(jnp.arange(t, dtype=jnp.int32))
        valid = jnp.zeros((E, cap + 1), dtype=bool).at[eidx, slot].set(keep)
        dispatch = dispatch[:, :cap]
        valid = valid[:, :cap]
        xe = xf[dispatch]
        h = jnp.maximum(jnp.einsum('ecd,edf->ecf', xe, W1), 0.0)
        ye = jnp.einsum('ecf,efd->ecd', h, W2)
        pe = p_tok[dispatch]
        ye = ye * (pe * valid.astype(ye.dtype))[:, :, None]
        y = jnp.zeros((t, d), dtype=x.dtype).at[dispatch.reshape(-1)].add(ye.reshape(E * cap, d).astype(x.dtype))
        return y.reshape(b, s, d)
    x = x + jnp.tanh(g_xattn[0]) * _L0_xattn_ref(_layernorm(x, axis=-1), ctx_1024, ctx_1024, mask_1x1xSxS2_ik1, L0_xattn_w_q, L0_xattn_w_k, L0_xattn_w_v, L0_xattn_w_o, L0_xattn_b_o)
    x = x + jnp.tanh(g_ffn[0]) * _L0_ffn_ref(_layernorm(x, axis=-1), L0_ffn_k0, L0_ffn_k1, L0_ffn_k2, L0_ffn_s0, L0_ffn_s1, L0_ffn_s2)
    x = x + jnp.tanh(g_xattn[1]) * _L1_xattn_ref(_layernorm(x, axis=-1), ctx_1024, ctx_1024, mask_BxSxS2_if1, L1_xattn_Wq, L1_xattn_Wk, L1_xattn_Wv, L1_xattn_Wo, L1_xattn_bo)
    x = x + jnp.tanh(g_ffn[1]) * _L1_ffn_ref(_layernorm(x, axis=-1), L1_ffn_Wr, L1_ffn_W1, L1_ffn_W2)
    return x

_drawn_inputs = setup_inputs


def setup_inputs(seed=0):
    import zlib

    import numpy as np

    out = dict(_drawn_inputs(seed))
    spreads = {'g_ffn': (-1.0, 0.6), 'L1_xattn_bo': (0.0, 0.1)}
    factors = {'L0_xattn_b_o': 5.7, 'L1_xattn_Wq': 8.0, 'L1_xattn_Wk': 8.0}
    for name, (base, spread) in spreads.items():
        noise = np.random.default_rng([zlib.crc32(name.encode()), seed]).standard_normal(out[name].shape)
        drawn = base * np.exp(spread * noise) if base else spread * noise
        out[name] = jnp.asarray(drawn.astype(out[name].dtype))
    for name, factor in factors.items():
        out[name] = (out[name] * factor).astype(out[name].dtype)
    return out
```

```python
from contextlib import ExitStack

import concourse.bass as bass
from concourse import mybir

F32 = mybir.dt.float32
F16 = mybir.dt.float16
BF16 = mybir.dt.bfloat16
I32 = mybir.dt.int32
U32 = mybir.dt.uint32
U8 = mybir.dt.uint8
ALU = mybir.AluOpType
ACT = mybir.ActivationFunctionType
AX = mybir.AxisListType

P = 128
B, S, D = 32, 112, 256
S2 = 375
H, DK = 16, 16
KC = D // P
CH = 3
CK = S2 // CH
NP = H // 2
QUAD = 32
NT = H // 4
UNITS = NT * CH
G = 4
NG = B // G
GT = G * S
F = 1024
FC = F // P
E = 8
CAP = B * S // E
STACK = 3 * QUAD
ROWS = STACK + 4
MASKED = float(2 ** 30)
EPS = 1e-5
LARGEST = 3.0e38


class Step:

    def __init__(self, pair, slot):
        self.pair, self.slot = pair, slot
        self.value = 2 * pair + slot

    def back(self, n):
        total = self.slot - n
        pairs = total // 2
        return Step(self.pair + pairs if pairs else self.pair, total % 2)

    def exists(self, count):
        return 0 <= self.value < count if isinstance(self.value, int) else count > 1


def run_steps(eng, count, lag, body):
    for s in range(4):
        body(Step(s // 2, s % 2))
    with eng.Fori(2, count // 2) as pair:
        for slot in range(2):
            body(Step(pair, slot))
    for s in range(count, count + lag):
        body(Step(s // 2, s % 2))


def wait(eng, sem, value):
    if not isinstance(value, int) or value > 0:
        eng.wait_ge(sem, value)


class Semaphores:

    def __init__(self, nc, stack):
        self.nc, self.stack, self.made = nc, stack, []

    def new(self, name):
        self.made.append(self.stack.enter_context(self.nc.semaphore(name)))
        return self.made[-1]

    def clear(self):
        with self.nc.Block() as block:
            @block.sync
            def _(sp):
                for s in self.made:
                    sp.sem_clear(s)


def flamingo_program(nc, a, out):
    def dram(name, shape, dt):
        return nc.dram_tensor(name, shape, dt, kind="Internal").ap()

    x1 = dram("x_after_attention_0", [B, S, D], F32)
    x2 = dram("x_after_ffn_0", [B, S, D], F32)
    x3 = dram("x_after_attention_1", [B, S, D], F32)
    x3_normed = dram("x_after_attention_1_normed", [B, S, D], F32)
    q_split = dram("q_split", [2, D, B * S], F16)
    k_split = dram("k_split", [2, 2, D, S2], F16)
    wo_turned = dram("wo_turned", [D, D], F32)
    expert_in = dram("expert_in", [E * CAP, D], F32)
    expert_out = dram("expert_out", [E * CAP, D], F32)

    with ExitStack() as ctx:
        def sb(name, shape, dt):
            return ctx.enter_context(nc.sbuf_tensor(name, shape, dt))

        m = {
            "bank": [ctx.enter_context(nc.psum_tensor(f"bank{i}", [P, 512], F32)) for i in range(8)],
            "ident": sb("ident", [P, P], F32),
            "ident_h": sb("ident_h", [P, P], F16),
            "ident_b": sb("ident_b", [P, P], BF16),
            "eps": sb("eps", [P, 1], F32),
            "gate": sb("gate", [P, 4], F32),
            "ffn_scale": sb("ffn_scale", [P, 1], F32),
            "sign": sb("sign", [P, 2], F32),
            "wq": [sb(f"wq{n}", [P, KC, D], F32) for n in range(2)],
            "wk": [sb(f"wk{n}", [P, KC, D], F32) for n in range(2)],
            "wv": [sb(f"wv{n}", [P, KC, D], F32) for n in range(2)],
            "wo": [sb(f"wo{n}", [P, NT, D], F32) for n in range(2)],
            "bo": [sb(f"bo{n}", [S, D], F32) for n in range(2)],
            "pick_sum": sb("pick_sum", [P, P], F32),
        }
        setup_phase(nc, m, a, wo_turned, expert_in)
        queries_phase(nc, m, 0, a["x"], a["mask_1x1xSxS2_ik1"], q_split)
        attention_phase(nc, m, 0, a["x"], x1, a["ctx_1024"], a["mask_1x1xSxS2_ik1"], q_split, k_split)
        ffn_phase(nc, m, a, x1, x2)
        queries_phase(nc, m, 1, x2, a["mask_BxSxS2_if1"], q_split)
        attention_phase(nc, m, 1, x2, x3, a["ctx_1024"], a["mask_BxSxS2_if1"], q_split, k_split)
        moe_phases(nc, m, a, x3, x3_normed, expert_in, expert_out, out)


def setup_phase(nc, m, a, wo_turned, expert_in):
    with ExitStack() as ctx:
        sems = Semaphores(nc, ctx)
        def sem(name):
            return sems.new(name)

        raw = [ctx.enter_context(nc.sbuf_tensor(f"raw_w{n}", [P, KC, D], F32)) for n in range(4)]
        turned_o = ctx.enter_context(nc.sbuf_tensor("turned_o", [P, KC, D], F32))
        zeros = ctx.enter_context(nc.sbuf_tensor("zeros", [P, CAP * E * D // P // 4], F32))
        gin = ctx.enter_context(nc.sbuf_tensor("gate_in", [P, 4], F32))
        sin = ctx.enter_context(nc.sbuf_tensor("scale_in", [P, 3], F32))
        mag = ctx.enter_context(nc.sbuf_tensor("scale_parts", [P, 4], F32))
        small_loaded, weights_loaded, raw_loaded = sem("small_loaded"), sem("weights_loaded"), sem("raw_loaded")
        cleared, made, turned, copied = sem("su_cleared"), sem("su_made"), sem("su_turned"), sem("su_copied")
        chain, gated, experts_cleared = sem("su_chain"), sem("su_gated"), sem("experts_cleared")
        wo_stored, wo_loaded, wo_zeroed = sem("wo_stored"), sem("wo_loaded"), sem("wo_zeroed")
        passed = sem("passed")
        ended = ExitStack()
        block = ended.enter_context(nc.Block())

        def chunked(w):
            return w.rearrange("(c p) n -> p c n", p=P)

        @block.sync
        def _(sp):
            for n, g in enumerate((a["g_xattn"], a["g_ffn"])):
                sp.dma_start(gin[:, 2 * n:2 * n + 2], g.partition_broadcast(P)).then_inc(small_loaded, 16)
            for n in range(3):
                s = a[f"L0_ffn_s{n}"]
                sp.dma_start(sin[:, n:n + 1], s.partition_broadcast(P)).then_inc(small_loaded, 16)
            for n, w in enumerate(("Wq", "Wk", "Wv", "Wo")):
                sp.dma_start(raw[n][:, :, :], chunked(a[f"L1_xattn_{w}"])).then_inc(raw_loaded, 16)
            for w in "qkv":
                sp.dma_start(m["w" + w][0][:, :, :], chunked(a[f"L0_xattn_w_{w}"])).then_inc(weights_loaded, 16)
            for n, b in enumerate((a["L0_xattn_b_o"], a["L1_xattn_bo"])):
                sp.dma_start(m["bo"][n][:, :], b.partition_broadcast(S)).then_inc(weights_loaded, 16)
            sp.wait_ge(wo_zeroed, 2)
            sp.wait_ge(copied, 16)
            sp.dma_start(chunked(wo_turned), turned_o[:, :, :]).then_inc(wo_stored, 16)
            sp.wait_ge(wo_stored, 16)
            for n, w in enumerate((a["L0_xattn_w_o"], wo_turned)):
                rows = w.rearrange("(t j r) n -> j r t n", j=4, r=DK)
                for j in range(4):
                    sp.dma_start(m["wo"][n][QUAD * j:QUAD * j + DK, :, :], rows[j]).then_inc(wo_loaded, 16)
            sp.wait_ge(cleared, 1)
            rows = expert_in.rearrange("(f p r) n -> f p (r n)", f=4, p=P)
            for f in range(4):
                sp.dma_start(rows[f], zeros[:, :]).then_inc(experts_cleared, 16)
            sp.wait_ge(experts_cleared, 64)
            sp.wait_ge(wo_loaded, 128)
            sp.wait_ge(weights_loaded, 80)

        @block.gpsimd
        def _(pool):
            for t in (m["ident"], m["ident_h"], m["ident_b"], m["pick_sum"]):
                pool.memset(t[:, :], 0.0).then_inc(made, 1)
            pool.wait_ge(made, 4)
            for t in (m["ident"], m["ident_h"], m["ident_b"]):
                pool.affine_select(out=t[:, :], in_=t[:, :], compare_op=ALU.not_equal, fill=1.0, base=0,
                                   pattern=[[-1, P]], channel_multiplier=1).then_inc(made, 1)
            pick = m["pick_sum"][:, :].rearrange("p (j r) -> p j r", j=4)
            pool.affine_select(out=pick, in_=pick, compare_op=ALU.not_equal, fill=1.0, base=-DK,
                               pattern=[[-QUAD, 4], [0, QUAD]], channel_multiplier=1).then_inc(made, 1)

        @block.tensor
        def _(pe):
            pe.wait_ge(made, 5)
            pe.wait_ge(raw_loaded, 64)
            n = 0
            for w in range(4):
                for r in range(KC):
                    for c in range(KC):
                        if n >= 4:
                            pe.wait_ge(copied, n - 3)
                        pe.transpose(m["bank"][n % 4][:, 0:P], raw[w][:, r, c * P:(c + 1) * P],
                                     m["ident"][:, :]).then_inc(turned, 1)
                        n += 1

        @block.vector
        def _(dve):
            dve.memset(zeros[:, :], 0.0).then_inc(cleared, 1)
            dve.memset(m["eps"][:, :], EPS)
            for n in range(2):
                dve.memset(m["wo"][n][:, :, :], 0.0).then_inc(wo_zeroed, 1)
            n = 0
            for w in (m["wq"][1], m["wk"][1], m["wv"][1], turned_o):
                for r in range(KC):
                    for c in range(KC):
                        dve.wait_ge(turned, n + 1)
                        dve.tensor_copy(w[:, c, r * P:(r + 1) * P], m["bank"][n % 4][:, 0:P]).then_inc(copied, 1)
                        n += 1
            dve.wait_ge(small_loaded, 80)
            steps = 0

            def link(ins):
                nonlocal steps
                steps += 1
                ins.then_inc(chain, 1)
                dve.wait_ge(chain, steps)

            link(dve.tensor_scalar(m["sign"][:, :], sin[:, 0:2], 0.0, None, ALU.is_ge))
            link(dve.tensor_scalar(m["sign"][:, :], m["sign"][:, :], 2.0, -1.0, ALU.mult, ALU.add))
            link(dve.tensor_tensor(mag[:, 0:2], sin[:, 0:2], m["sign"][:, :], ALU.mult))
            link(dve.tensor_tensor(mag[:, 2:3], mag[:, 0:1], mag[:, 1:2], ALU.mult))
            link(dve.tensor_tensor(mag[:, 3:4], mag[:, 2:3], sin[:, 2:3], ALU.mult))
            dve.wait_ge(gated, 1)
            link(dve.tensor_scalar(m["ffn_scale"][:, :], mag[:, 3:4], m["gate"][:, 2:3], 4.0 * 32.0,
                                   ALU.mult, ALU.mult))

        @block.scalar
        def _(act):
            act.wait_ge(small_loaded, 80)
            act.activation(m["gate"][:, :], gin[:, :], ACT.Tanh).then_inc(gated, 1)

        ended.close()
        sems.clear()


def queries_phase(nc, m, layer, x_in, mask, q_split):
    tag = f"_q{layer}"
    with ExitStack() as ctx:
        sems = Semaphores(nc, ctx)
        def sb(name, shape, dt):
            return ctx.enter_context(nc.sbuf_tensor(name + tag, shape, dt))

        def sem(name):
            return sems.new(name + tag)

        masks = G if layer else 1
        xg = [sb(f"xg{n}", [S, G, D], F32) for n in range(2)]
        mask_in = [sb(f"mask_in{n}", [S, masks, S2], I32) for n in range(2)]
        mask_f = sb("mask_f", [S, masks, S2], F32)
        seen = sb("seen", [S, masks], F32)
        stats = sb("stats", [S, G, 6], F32)
        mean_var = sb("mean_var", [S, G, 2], F32)
        dev = sb("dev", [S, G], F32)
        scale = sb("scale", [S, G], F32)
        xn = [sb(f"xn{n}", [S, G, D], F32) for n in range(2)]
        xt = [sb(f"xt{n}", [P, KC, GT], F32) for n in range(2)]
        high = [sb(f"high{n}", [P, KC, GT], F16) for n in range(2)]
        low = [sb(f"low{n}", [P, KC, GT], F16) for n in range(2)]
        x_loaded = [sem(f"x_loaded{n}") for n in range(2)]
        mask_loaded = [sem(f"mask_loaded{n}") for n in range(2)]
        dve_chain, var_ready, dev_ready, scaled = sem("dve_chain"), sem("var_ready"), sem("dev_ready"), sem("scaled")
        xn_ready, turned, xt_ready, q_ready = sem("xn_ready"), sem("turned"), sem("xt_ready"), sem("q_ready")
        high_ready, low_ready = sem("high_ready"), sem("low_ready")
        stored = [sem(f"stored{n}") for n in range(2)]
        passed = sem("passed")
        ended = ExitStack()
        block = ended.enter_context(nc.Block())
        turn_bank = [m["bank"][0:2], m["bank"][2:4]]
        q_bank = [m["bank"][4:6], m["bank"][6:8]]
        x_rows = x_in.rearrange("(g b) s d -> g s b d", b=G)
        q_out = q_split.rearrange("w (c p) (g t) -> w g p c t", p=P, t=GT)

        @block.sync
        def _(sp):
            if not layer:
                sp.dma_start(mask_in[0][:, 0, :], mask[0, 0, :, :]).then_inc(mask_loaded[0], 16)

            def body(s):
                if s.exists(NG):
                    wait(sp, xn_ready, s.back(2).value + 1 if s.back(2).exists(NG) else 0)
                    sp.dma_start(xg[s.slot][:, :, :], take(x_rows, s.value)).then_inc(x_loaded[s.slot], 16)
                    if layer:
                        rows = mask.rearrange("(g b) s k -> g s b k", b=G)
                        sp.dma_start(mask_in[s.slot][:, :, :],
                                     take(rows, s.value)).then_inc(mask_loaded[s.slot], 16)
                p = s.back(1)
                if p.exists(NG):
                    for part, (tile, ready) in enumerate(((high, high_ready), (low, low_ready))):
                        wait(sp, ready, 2 * (p.value + 1))
                        sp.dma_start(take(q_out[part], p.value), tile[p.slot][:, :, :]).then_inc(stored[p.slot], 16)

            run_steps(sp, NG, 1, body)
            for n in range(2):
                sp.wait_ge(stored[n], 32 * NG // 2)

        @block.vector
        def _(dve):
            def see(slot):
                dve.tensor_scalar(mask_f[:, :, :], mask_in[slot][:, :, :], 0.0, None,
                                  ALU.not_equal).then_inc(dve_chain, 1)

            if not layer:
                dve.wait_ge(mask_loaded[0], 16)
                see(0)
                dve.wait_ge(dve_chain, 1)
                dve.tensor_reduce(seen[:, :], mask_f[:, :, :], AX.X, ALU.max).then_inc(dve_chain, 1)
            per, first = (3, 0) if layer else (1, 2)

            def body(s):
                if s.exists(NG):
                    dve.wait_ge(x_loaded[s.slot], 16 * (s.pair + 1))
                    done = per * s.value + first
                    if layer:
                        dve.wait_ge(mask_loaded[s.slot], 16 * (s.pair + 1))
                        wait(dve, dve_chain, done)
                        see(s.slot)
                        dve.wait_ge(dve_chain, done + 1)
                        dve.tensor_reduce(seen[:, :], mask_f[:, :, :], AX.X, ALU.max).then_inc(dve_chain, 1)
                        done = done + 2
                    for b in range(G):
                        last = dve.bn_stats(stats[:, b, :], xg[s.slot][:, b, :])
                    last.then_inc(dve_chain, 1)
                    hold(dve, dve_chain, done + 1, passed)
                    for b in range(G):
                        last = dve.bn_aggr(mean_var[:, b, :], stats[:, b, :])
                    last.then_inc(var_ready, 1)
                    dve.wait_ge(dev_ready, s.value + 1)
                    dve.reciprocal(scale[:, :], dev[:, :]).then_inc(scaled, 1)
                    dve.wait_ge(scaled, 2 * s.value + 1)
                    seen_all = seen[:, :] if layer else seen[:, :].to_broadcast([S, G])
                    dve.tensor_tensor(scale[:, :], scale[:, :], seen_all, ALU.mult).then_inc(scaled, 1)
                    dve.wait_ge(scaled, 2 * s.value + 2)
                    wait(dve, turned, 2 * (s.back(2).value + 1) if s.back(2).exists(NG) else 0)
                    for b in range(G):
                        last = dve.tensor_scalar(xn[s.slot][:, b, :], xg[s.slot][:, b, :], mean_var[:, b, 0:1],
                                                 scale[:, b:b + 1], ALU.subtract, ALU.mult)
                    last.then_inc(xn_ready, 1)
                p = s.back(1)
                if p.exists(NG):
                    wait(dve, stored[p.slot], 32 * p.pair)
                    for c in range(KC):
                        dve.wait_ge(high_ready, 2 * p.value + c + 1)
                        dve.tensor_tensor(low[p.slot][:, c, :], q_bank[p.slot][c][:, 0:GT],
                                          high[p.slot][:, c, :], ALU.subtract).then_inc(low_ready, 1)

            run_steps(dve, NG, 1, body)

        @block.scalar
        def _(act):
            def body(s):
                if s.exists(NG):
                    act.wait_ge(var_ready, s.value + 1)
                    act.activation(dev[:, :], mean_var[:, :, 1], ACT.Sqrt, bias=m["eps"][0:S, :]).then_inc(dev_ready, 1)
                    wait(act, q_ready, 2 * (s.back(2).value + 1) if s.back(2).exists(NG) else 0)
                    for c in range(KC):
                        act.wait_ge(turned, 2 * s.value + c + 1)
                        act.activation(xt[s.slot][:, c, :], turn_bank[s.slot][c][:, 0:GT], ACT.Copy).then_inc(xt_ready, 1)
                p = s.back(1)
                if p.exists(NG):
                    wait(act, stored[p.slot], 32 * p.pair)
                    for c in range(KC):
                        act.wait_ge(q_ready, 2 * p.value + c + 1)
                        act.activation(high[p.slot][:, c, :], q_bank[p.slot][c][:, 0:GT], ACT.Copy).then_inc(high_ready, 1)

            run_steps(act, NG, 1, body)

        @block.tensor
        def _(pe):
            def body(s):
                if s.exists(NG):
                    pe.wait_ge(xn_ready, s.value + 1)
                    wait(pe, xt_ready, 2 * (s.back(2).value + 1) if s.back(2).exists(NG) else 0)
                    for c in range(KC):
                        for b in range(G):
                            last = pe.transpose(turn_bank[s.slot][c][:, b * S:(b + 1) * S],
                                                xn[s.slot][:, b, c * P:(c + 1) * P], m["ident"][0:S, 0:S])
                        last.then_inc(turned, 1)
                p = s.back(1)
                if p.exists(NG):
                    pe.wait_ge(xt_ready, 2 * (p.value + 1))
                    wait(pe, low_ready, 2 * (p.back(2).value + 1) if p.back(2).exists(NG) else 0)
                    for j in range(KC):
                        for c in range(KC):
                            last = pe.matmul(q_bank[p.slot][j][:, 0:GT], m["wq"][layer][:, c, j * P:(j + 1) * P],
                                             xt[p.slot][:, c, :], start=c == 0, stop=c == KC - 1)
                        last.then_inc(q_ready, 1)

            run_steps(pe, NG, 1, body)

        ended.close()
        sems.clear()


def hold(eng, sem, value, passed):
    if not isinstance(value, int) or value > 0:
        eng.wait_ge(sem, value)
        eng.sem_inc(passed, 1)


def take(ap, index):
    return ap[index] if isinstance(index, int) else ap[bass.ds(index, 1)].squeeze(0)


def attention_phase(nc, m, layer, x_in, x_out, context, mask, q_split, k_split):
    tag = f"_a{layer}"
    with ExitStack() as ctx:
        sems = Semaphores(nc, ctx)
        def sb(name, shape, dt):
            return ctx.enter_context(nc.sbuf_tensor(name + tag, shape, dt))

        def sem(name):
            return sems.new(name + tag)

        def two(make, name, *args):
            return [make(f"{name}{n}", *args) for n in range(2)]

        ctx_in = two(sb, "ctx_in", [CK, CH, D], F32)
        ctx_t = sb("ctx_t", [P, KC, S2], F32)
        k_high = sb("k_high", [P, KC, S2], F16)
        k_low = sb("k_low", [P, KC, S2], F16)
        k_stack = two(sb, "k_stack", [P, NP, S2], F16)
        q_stack = two(sb, "q_stack", [P, NP, 2 * S], F16)
        values = two(sb, "values", [CK, CH, H, QUAD], F32)
        mask_in = two(sb, "mask_in", [S, S2], I32)
        mask_f = sb("mask_f", [S, S2], F32)
        seen = sb("seen", [S, 2], F32)
        mask_add = sb("mask_add", [S, S2], F32)
        mask_b = sb("mask_b", [S, S2], BF16)
        mask_t = two(sb, "mask_t", [CK, CH, S], BF16)
        masked_scores = sb("masked_scores", [S, 2, S2], BF16)
        row_max = sb("row_max", [S, H], F32)
        max_parts = sb("max_parts", [S, 2 * H], F16)
        max_t = sb("max_t", [2 * H, S], F16)
        probs = sb("probs", [CK, CH, GT], F32)
        heads_t = sb("heads_t", [P, GT], F32)
        inverse = sb("inverse", [P, GT], F32)
        heads_n = sb("heads_n", [P, GT], F32)
        x_old = two(sb, "x_old", [S, D], F32)
        attended = sb("attended", [S, D], F32)
        x_new = two(sb, "x_new", [S, D], F32)

        ctx_loaded, q_loaded, k_loaded = two(sem, "ctx_loaded"), two(sem, "q_loaded"), two(sem, "k_loaded")
        mask_loaded, max_loaded, x_loaded = two(sem, "mask_loaded"), two(sem, "max_loaded"), two(sem, "x_loaded")
        k_stored, x_stored = sem("k_stored"), two(sem, "x_stored")
        stacks_set = sem("stacks_set")
        ctx_turned, ctx_copied = sem("ctx_turned"), sem("ctx_copied")
        k_made, k_high_ready, k_low_ready = sem("k_made"), sem("k_high_ready"), sem("k_low_ready")
        v_made, v_ready = sem("v_made"), sem("v_ready")
        mask_step, mask_made, mask_turned, mask_ready = (sem("mask_step"), sem("mask_made"), sem("mask_turned"),
                                                         sem("mask_ready"))
        rows_scored, rows_maxed = sem("rows_scored"), sem("rows_maxed")
        parts_ready, max_turned, max_ready = sem("parts_ready"), sem("max_turned"), sem("max_ready")
        scored, exped, weighted = sem("scored"), sem("exped"), sem("weighted")
        heads_ready, sums_ready, inverted = sem("heads_ready"), sem("sums_ready"), sem("inverted")
        normed, projected, biased, added = sem("normed"), sem("projected"), sem("biased"), sem("added")
        passed = sem("passed")
        ended = ExitStack()
        block = ended.enter_context(nc.Block())

        row_bank = m["bank"][0:2]
        score_bank = m["bank"][2:5]
        head_bank = m["bank"][5]
        prep_bank = m["bank"][6:8]
        sudbank, out_bank = score_bank[0], score_bank[1]
        max_t_ps = row_bank[0][:, :].bitcast(F16)[0:2 * H, 0:S]
        mask_t_ps = row_bank[1][:, :].bitcast(BF16)[0:CK, 0:CH * S]
        masks = B if layer else 1

        ctx_rows = context.rearrange("b (c p) d -> b p c d", p=CK)
        mask_rows = mask if layer else mask[0]
        q_rows = q_split.rearrange("w (p e r) (b t) -> w e b r p t", e=2, r=DK, t=S)
        k_rows = k_split.rearrange("s w (p r) k -> s w r p k", r=QUAD)
        k_save = k_split.rearrange("s w (c p) k -> s w p c k", p=P)

        @block.sync
        def _(sp):
            def body(s):
                d = s.back(2)
                if s.exists(B):
                    wait(sp, ctx_turned, KC * (s.back(2).value + 1) if s.back(2).exists(B) else 0)
                    sp.dma_start(ctx_in[s.slot][:, :, :], take(ctx_rows, s.value)).then_inc(ctx_loaded[s.slot], 16)
                if s.exists(masks):
                    wait(sp, mask_step, 3 * (s.back(2).value + 1) if s.back(2).exists(masks) else 0)
                    sp.dma_start(mask_in[s.slot][:, :], take(mask_rows, s.value)).then_inc(mask_loaded[s.slot], 16)
                if d.exists(B):
                    wait(sp, added, d.back(2).value + 1 if d.back(2).exists(B) else 0)
                    sp.dma_start(x_old[d.slot][:, :], take(x_in, d.value)).then_inc(x_loaded[d.slot], 16)
                if s.exists(B):
                    if isinstance(s.value, int):
                        sp.wait_ge(stacks_set, 4)
                    wait(sp, scored, UNITS * (d.value + 1) if d.exists(B) else 0)
                    for e in range(2):
                        for g, part in enumerate((0, 0, 1)):
                            src = q_rows[part, e]
                            first = QUAD * g + DK * e
                            dst = q_stack[s.slot][first:first + DK, :, e * S:(e + 1) * S]
                            sp.dma_start(dst, take(src, s.value)).then_inc(q_loaded[s.slot], 16)
                x = s.back(1)
                if x.exists(B):
                    sp.wait_ge(max_ready, x.value + 1)
                    for part in range(2):
                        for e in range(2):
                            row = STACK + 2 * part + e
                            dst = q_stack[x.slot][row:row + 1, :, e * S:(e + 1) * S]
                            src = max_t[part * H + e:(part + 1) * H:2, :]
                            sp.dma_start(dst, src).then_inc(max_loaded[x.slot], 16)

            run_steps(sp, B, 2, body)

        @block.gpsimd
        def _(pool):
            def body(s):
                if s.exists(B):
                    wait(pool, k_loaded[s.slot], 48 * s.pair)
                    for part, (tile, ready) in enumerate(((k_high, k_high_ready), (k_low, k_low_ready))):
                        hold(pool, ready, 2 * (s.value + 1), passed)
                        pool.dma_start(k_save[s.slot, part], tile[:, :, :]).then_inc(k_stored, 16)
                    pool.wait_ge(k_stored, 32 * (s.value + 1))
                    pool.wait_ge(stacks_set, 4)
                    hold(pool, scored, UNITS * (s.back(2).value + 1) if s.back(2).exists(B) else 0, passed)
                    for g, part in enumerate((0, 1, 0)):
                        pool.dma_start(k_stack[s.slot][QUAD * g:QUAD * (g + 1), :, :],
                                       k_rows[s.slot, part]).then_inc(k_loaded[s.slot], 16)
                d = s.back(2)
                if d.exists(B):
                    hold(pool, added, d.value + 1, passed)
                    pool.dma_start(take(x_out, d.value), x_new[d.slot][:, :]).then_inc(x_stored[d.slot], 16)

            run_steps(pool, B, 2, body)
            for n in range(2):
                pool.wait_ge(x_stored[n], 16 * B // 2)

        @block.tensor
        def _(pe):
            ident, ident_h, ident_b = m["ident"], m["ident_h"], m["ident_b"]

            def turn_context(s, c):
                if c == 0:
                    pe.wait_ge(ctx_loaded[s.slot], 16 * (s.pair + 1))
                    wait(pe, v_ready, CH * s.value)
                for k in range(CH):
                    last = pe.transpose(prep_bank[c][:, k * CK:(k + 1) * CK],
                                        ctx_in[s.slot][:, k, c * P:(c + 1) * P], ident[0:CK, 0:CK])
                last.then_inc(ctx_turned, 1)

            def make_keys(s, j):
                pe.wait_ge(ctx_copied, KC * (s.value + 1))
                for c in range(KC):
                    last = pe.matmul(prep_bank[j][:, 0:S2], m["wk"][layer][:, c, j * P:(j + 1) * P],
                                     ctx_t[:, c, :], start=c == 0, stop=c == KC - 1)
                last.then_inc(k_made, 1)

            def make_values(s, k):
                if k < 2:
                    pe.wait_ge(k_low_ready, KC * s.value + k + 1)
                else:
                    pe.wait_ge(v_ready, CH * s.value + 1)
                for c in range(KC):
                    last = pe.matmul(prep_bank[k % 2][0:CK, 0:D], ctx_t[:, c, k * CK:(k + 1) * CK],
                                     m["wv"][layer][:, c, :], start=c == 0, stop=c == KC - 1)
                last.then_inc(v_made, 1)

            def turn_mask(x):
                pe.wait_ge(mask_step, 3 * (x.value + 1))
                wait(pe, rows_maxed, H * x.value)
                for k in range(CH):
                    last = pe.transpose(mask_t_ps[:, k * S:(k + 1) * S], mask_b[:, k * CK:(k + 1) * CK],
                                        ident_b[0:S, 0:S])
                last.then_inc(mask_turned, 1)

            def score_rows(x, h):
                if h == 0:
                    pe.wait_ge(q_loaded[x.slot], 96 * (x.pair + 1))
                    pe.wait_ge(k_loaded[x.slot], 48 * (x.pair + 1))
                    wait(pe, max_ready, x.value)
                elif h == 1 and layer:
                    pe.wait_ge(mask_ready, x.value + 1)
                elif h == 1:
                    wait(pe, rows_maxed, H * x.value)
                    if isinstance(x.value, int) and x.value == 0:
                        pe.wait_ge(mask_ready, 1)
                else:
                    pe.wait_ge(rows_maxed, H * x.value + h - 1)
                e = h % 2
                pe.matmul(row_bank[h % 2][0:S, 0:S2], q_stack[x.slot][0:STACK, h // 2, e * S:(e + 1) * S],
                          k_stack[x.slot][0:STACK, h // 2, :], start=True, stop=True).then_inc(rows_scored, 1)

            def turn_maxima(x):
                pe.wait_ge(parts_ready, 2 * (x.value + 1))
                pe.transpose(max_t_ps, max_parts[:, :], ident_h[0:S, 0:S]).then_inc(max_turned, 1)

            def score_unit(d, i):
                if i == 0:
                    pe.wait_ge(max_loaded[d.slot], 64 * (d.pair + 1))
                    wait(pe, inverted, d.value)
                    if layer:
                        pe.wait_ge(mask_ready, d.value + 1)
                elif i == 1:
                    wait(pe, biased, d.value)
                elif i == 2:
                    wait(pe, exped, UNITS * d.value)
                else:
                    pe.wait_ge(exped, UNITS * d.value + i - 2)
                t, k = divmod(i, CH)
                bank = score_bank[i % 3]
                mask_cols = mask_t[d.slot if layer else 0][:, k, :]
                pe.matmul(bank[0:CK, 0:GT], ident_b[0:CK, 0:CK], mask_cols.unsqueeze(1).to_broadcast([CK, 4, S]),
                          start=True, stop=True)
                for half in range(2):
                    last = pe.matmul(bank[0:CK, half * 2 * S:(half + 1) * 2 * S],
                                     k_stack[d.slot][0:ROWS, 2 * t + half, k * CK:(k + 1) * CK],
                                     q_stack[d.slot][0:ROWS, 2 * t + half, :], start=False, stop=True,
                                     skip_group_check=True)
                last.then_inc(scored, 1)

            def weigh_unit(d, i):
                t, k = divmod(i, CH)
                if i == 0:
                    pe.wait_ge(v_ready, CH * (d.value + 1))
                    wait(pe, heads_ready, d.value)
                pe.wait_ge(exped, UNITS * d.value + i + 1)
                for j in range(4):
                    last = pe.matmul(head_bank[QUAD * j:QUAD * (j + 1), t * S:(t + 1) * S],
                                     values[d.slot][:, k, 4 * t + j, :], probs[:, k, j * S:(j + 1) * S],
                                     start=k == 0, stop=k == CH - 1, tile_position=(0, QUAD * j))
                last.then_inc(weighted, 1)

            def body(s):
                x, d = s.back(1), s.back(2)
                for i in range(UNITS):
                    if d.exists(B):
                        score_unit(d, i)
                        if i >= 2:
                            weigh_unit(d, i - 2)
                    if s.exists(B) and i in (5, 6):
                        turn_context(s, i - 5)
                    if x.exists(masks) and i == 3:
                        turn_mask(x)
                    if x.exists(B) and i >= 4:
                        score_rows(x, 2 * (i - 4))
                        score_rows(x, 2 * (i - 4) + 1)
                if d.exists(B):
                    weigh_unit(d, UNITS - 2)
                    weigh_unit(d, UNITS - 1)
                if s.exists(B):
                    for j in range(KC):
                        make_keys(s, j)
                if x.exists(B):
                    turn_maxima(x)
                if s.exists(B):
                    for k in range(CH):
                        make_values(s, k)
                if d.exists(B):
                    pe.wait_ge(heads_ready, d.value + 1)
                    pe.matmul(sudbank[:, 0:GT], m["pick_sum"][:, :], heads_t[:, :],
                              start=True, stop=True).then_inc(sums_ready, 1)
                    pe.wait_ge(normed, d.value + 1)
                    for t in range(NT):
                        last = pe.matmul(out_bank[0:S, 0:D], heads_n[:, t * S:(t + 1) * S], m["wo"][layer][:, t, :],
                                         start=t == 0, stop=t == NT - 1)
                    last.then_inc(projected, 1)

            run_steps(pe, B, 2, body)

        @block.scalar
        def _(act):
            def copy_context(s, c):
                act.wait_ge(ctx_turned, KC * s.value + c + 1)
                act.activation(ctx_t[:, c, :], prep_bank[c][:, 0:S2], ACT.Copy).then_inc(ctx_copied, 1)

            def body(s):
                x, d = s.back(1), s.back(2)
                for i in range(UNITS):
                    if d.exists(B):
                        act.wait_ge(scored, UNITS * d.value + i + 1)
                        wait(act, weighted, UNITS * d.value + i - 2)
                        act.activation(probs[:, i % CH, :], score_bank[i % 3][0:CK, 0:GT], ACT.Exp,
                                       scale=DK ** -0.5).then_inc(exped, 1)
                    if s.exists(B) and i in (5, 6):
                        copy_context(s, i - 5)
                if d.exists(B):
                    act.wait_ge(weighted, UNITS * (d.value + 1))
                    act.activation(heads_t[:, :], head_bank[:, 0:GT], ACT.Copy).then_inc(heads_ready, 1)
                if s.exists(B):
                    wait(act, k_stored, 32 * s.value)
                    for j in range(KC):
                        act.wait_ge(k_made, KC * s.value + j + 1)
                        act.activation(k_high[:, j, :], prep_bank[j][:, 0:S2], ACT.Copy).then_inc(k_high_ready, 1)
                if x.exists(B):
                    act.wait_ge(max_turned, x.value + 1)
                    p = x.back(1)
                    if p.exists(B):
                        act.wait_ge(max_loaded[p.slot], 64 * (p.pair + 1))
                    act.activation(max_t[:, :], max_t_ps, ACT.Copy).then_inc(max_ready, 1)
                if s.exists(B):
                    for k in range(CH):
                        act.wait_ge(v_made, CH * s.value + k + 1)
                        if isinstance(s.value, int):
                            act.wait_ge(stacks_set, 6)
                        act.activation(values[s.slot][:, k, :, 0:DK],
                                       prep_bank[k % 2][0:CK, 0:D].rearrange("p (h r) -> p h r", r=DK),
                                       ACT.Copy).then_inc(v_ready, 1)

            run_steps(act, B, 2, body)

        @block.vector
        def _(dve):
            for n in range(2):
                dve.memset(q_stack[n][:, :, :], 0.0).then_inc(stacks_set, 1)
                dve.memset(k_stack[n][STACK:P, :, :], 1.0).then_inc(stacks_set, 1)
            for n in range(2):
                dve.memset(values[n][:, :, :, DK:QUAD], 1.0).then_inc(stacks_set, 1)

            def split_mask(x):
                dve.wait_ge(mask_loaded[x.slot], 16 * (x.pair + 1))
                dve.tensor_scalar(mask_f[:, :], mask_in[x.slot][:, :], 0.0, None, ALU.not_equal).then_inc(mask_step, 1)
                dve.wait_ge(mask_step, 3 * x.value + 1)
                dve.tensor_reduce(seen[:, 0:1], mask_f[:, :], AX.X, ALU.max).then_inc(mask_step, 1)
                dve.wait_ge(mask_step, 3 * x.value + 2)
                dve.tensor_scalar(seen[:, 1:2], seen[:, 0:1], MASKED, None, ALU.mult).then_inc(mask_made, 1)
                dve.wait_ge(mask_made, 2 * x.value + 1)
                dve.tensor_scalar(mask_add[:, :], mask_f[:, :], 1.0, seen[:, 1:2], ALU.subtract,
                                  ALU.mult).then_inc(mask_made, 1)
                wait(dve, mask_turned, x.value)
                dve.wait_ge(mask_made, 2 * x.value + 2)
                dve.tensor_copy(mask_b[:, :], mask_add[:, :]).then_inc(mask_step, 1)

            def copy_mask(x):
                dve.wait_ge(mask_turned, x.value + 1)
                p = x.back(2)
                wait(dve, scored, UNITS * (p.value + 1) if p.exists(B) else 0)
                dve.tensor_copy(mask_t[x.slot][:, :, :], mask_t_ps.rearrange("p (k q) -> p k q", k=CH)).then_inc(mask_ready, 1)

            def body(s):
                x, d = s.back(1), s.back(2)
                if x.exists(masks):
                    split_mask(x)
                    copy_mask(x)
                if x.exists(B):
                    for h in range(H):
                        hold(dve, rows_scored, H * x.value + h + 1, passed)
                        dve.tensor_tensor_reduce(masked_scores[:, h % 2, :], row_bank[h % 2][0:S, 0:S2], mask_add[:, :],
                                                 1.0, -LARGEST, ALU.add, ALU.max,
                                                 row_max[:, h:h + 1]).then_inc(rows_maxed, 1)
                    dve.wait_ge(rows_maxed, H * (x.value + 1))
                    wait(dve, max_turned, x.value)
                    dve.tensor_scalar(max_parts[:, 0:H], row_max[:, :], -1.0, None, ALU.mult).then_inc(parts_ready, 1)
                    dve.wait_ge(parts_ready, 2 * x.value + 1)
                    dve.scalar_tensor_tensor(out=max_parts[:, H:2 * H], in0=row_max[:, :], scalar=-1.0,
                                             in1=max_parts[:, 0:H], op0=ALU.mult, op1=ALU.subtract).then_inc(parts_ready, 1)
                if s.exists(B):
                    wait(dve, k_stored, 32 * s.value)
                    for j in range(KC):
                        dve.wait_ge(k_high_ready, KC * s.value + j + 1)
                        dve.tensor_tensor(k_low[:, j, :], prep_bank[j][:, 0:S2], k_high[:, j, :],
                                          ALU.subtract).then_inc(k_low_ready, 1)
                if d.exists(B):
                    dve.wait_ge(sums_ready, d.value + 1)
                    dve.reciprocal(inverse[:, :], sudbank[:, 0:GT]).then_inc(inverted, 1)
                    dve.wait_ge(inverted, d.value + 1)
                    dve.tensor_tensor(heads_n[:, :], heads_t[:, :], inverse[:, :], ALU.mult).then_inc(normed, 1)
                    dve.wait_ge(projected, d.value + 1)
                    dve.tensor_tensor(attended[:, :], out_bank[0:S, 0:D], m["bo"][layer][:, :], ALU.add).then_inc(biased, 1)
                    dve.wait_ge(biased, d.value + 1)
                    dve.wait_ge(x_loaded[d.slot], 16 * (d.pair + 1))
                    wait(dve, x_stored[d.slot], 16 * d.pair)
                    dve.scalar_tensor_tensor(out=x_new[d.slot][:, :], in0=attended[:, :],
                                             scalar=m["gate"][0:S, layer:layer + 1], in1=x_old[d.slot][:, :],
                                             op0=ALU.mult, op1=ALU.add).then_inc(added, 1)

            run_steps(dve, B, 2, body)

        ended.close()
        sems.clear()


def ffn_phase(nc, m, a, x_in, x_out):
    with ExitStack() as ctx:
        sems = Semaphores(nc, ctx)
        def sb(name, shape, dt):
            return ctx.enter_context(nc.sbuf_tensor(name + "_f", shape, dt))

        def sem(name):
            return sems.new(name + "_f")

        def two(make, name, *args):
            return [make(f"{name}{n}", *args) for n in range(2)]

        k_in = [sb("k0_in", [P, 2 * KC, F], U8), sb("k1_in", [P, FC, F], U8), sb("k2_in", [P, FC, D], U8)]
        w0_parts = sb("w0_parts", [P, 2 * KC, F], F16)
        w = [sb("w0", [P, KC, F], F16), sb("w1", [P, FC, F], F16), sb("w2", [P, FC, D], F16)]
        factors = sb("factors", [P, 4], F32)
        xg = two(sb, "xg", [S, G, D], F32)
        stats = sb("stats", [S, G, 6], F32)
        mean_var = sb("mean_var", [S, G, 2], F32)
        dev = sb("dev", [S, G], F32)
        scale = sb("scale", [S, G], F32)
        xn = sb("xn", [S, G, D], F32)
        xh, xl = two(sb, "xh", [P, KC, GT], F16), two(sb, "xl", [P, KC, GT], F16)
        h = [[sb(f"h{n}{part}", [P, FC, GT], F16) for part in "hl"] for n in range(2)]
        y = two(sb, "y", [S, G, D], F32)

        k_loaded, w_step, w_ready = sem("k_loaded"), sem("w_step"), sem("w_ready")
        x_loaded, stored = two(sem, "x_loaded"), two(sem, "stored")
        stats_ready, var_ready, dev_ready, scaled = sem("stats_ready"), sem("var_ready"), sem("dev_ready"), sem("scaled")
        xn_ready, turned, xh_ready, xl_ready = sem("xn_ready"), sem("turned"), sem("xh_ready"), sem("xl_ready")
        z_made, h_high_ready, h_low_ready = sem("z_made"), sem("h_high_ready"), sem("h_low_ready")
        y_made, y_ready = sem("y_made"), sem("y_ready")
        passed = sem("passed")
        ended = ExitStack()
        block = ended.enter_context(nc.Block())

        z_bank, y_bank, turn_bank = m["bank"][0:4], m["bank"][4:6], m["bank"][6:8]
        x_rows = x_in.rearrange("(g b) s d -> g s b d", b=G)
        out_rows = x_out.rearrange("(g b) s d -> g s b d", b=G)
        ZS = 2 * FC

        @block.sync
        def _(sp):
            def body(s):
                if s.exists(NG):
                    wait(sp, y_ready, G * (s.back(2).value + 1) if s.back(2).exists(NG) else 0)
                    sp.dma_start(xg[s.slot][:, :, :], take(x_rows, s.value)).then_inc(x_loaded[s.slot], 16)
                if isinstance(s.value, int) and s.value == 0:
                    for n in range(3):
                        sp.dma_start(k_in[n][:, :, :], a[f"L0_ffn_k{n}"].rearrange("(c p) n -> p c n", p=P)).then_inc(k_loaded, 16)

            run_steps(sp, NG, 1, body)

        @block.gpsimd
        def _(pool):
            def body(s):
                p = s.back(1)
                if p.exists(NG):
                    hold(pool, y_ready, G * (p.value + 1), passed)
                    pool.dma_start(take(out_rows, p.value), y[p.slot][:, :, :]).then_inc(stored[p.slot], 16)

            run_steps(pool, NG, 1, body)
            for n in range(2):
                pool.wait_ge(stored[n], 16 * NG // 2)

        @block.vector
        def _(dve):
            def weights():
                dve.wait_ge(k_loaded, 48)
                for n, size in enumerate((1.0, 2.0 ** -5)):
                    dve.tensor_scalar(factors[:, 2 * n:2 * n + 1], m["sign"][:, n:n + 1], 2.0 * size, None,
                                      ALU.mult).then_inc(w_step, 1)
                    dve.tensor_scalar(factors[:, 2 * n + 1:2 * n + 2], m["sign"][:, n:n + 1], size, None,
                                      ALU.mult).then_inc(w_step, 1)
                dve.wait_ge(w_step, 4)
                dve.tensor_scalar(w0_parts[:, :, :], k_in[0][:, :, :], factors[:, 0:1], factors[:, 1:2],
                                  ALU.mult, ALU.subtract).then_inc(w_step, 1)
                dve.tensor_scalar(w[1][:, :, :], k_in[1][:, :, :], factors[:, 2:3], factors[:, 3:4],
                                  ALU.mult, ALU.subtract).then_inc(w_ready, 1)
                dve.tensor_scalar(w[2][:, :, :], k_in[2][:, :, :], 2.0, -1.0, ALU.mult, ALU.add).then_inc(w_ready, 1)
                dve.wait_ge(w_step, 5)
                dve.tensor_tensor(w[0][:, :, :], w0_parts[:, 0:KC, :], w0_parts[:, KC:2 * KC, :],
                                  ALU.subtract).then_inc(w_ready, 1)

            def normalise(s):
                dve.wait_ge(x_loaded[s.slot], 16 * (s.pair + 1))
                for b in range(G):
                    last = dve.bn_stats(stats[:, b, :], xg[s.slot][:, b, :])
                last.then_inc(stats_ready, 1)
                hold(dve, stats_ready, s.value + 1, passed)
                for b in range(G):
                    last = dve.bn_aggr(mean_var[:, b, :], stats[:, b, :])
                last.then_inc(var_ready, 1)

            def normalise_end(s):
                dve.wait_ge(dev_ready, s.value + 1)
                dve.reciprocal(scale[:, :], dev[:, :]).then_inc(scaled, 1)
                dve.wait_ge(scaled, s.value + 1)
                wait(dve, turned, KC * s.value)
                for b in range(G):
                    last = dve.tensor_scalar(xn[:, b, :], xg[s.slot][:, b, :], mean_var[:, b, 0:1],
                                             scale[:, b:b + 1], ALU.subtract, ALU.mult)
                last.then_inc(xn_ready, 1)

            def low_rows(s):
                for c in range(KC):
                    dve.wait_ge(xh_ready, KC * s.value + c + 1)
                    dve.tensor_tensor(xl[s.slot][:, c, :], turn_bank[c][:, 0:GT], xh[s.slot][:, c, :],
                                      ALU.subtract).then_inc(xl_ready, 1)

            def low_hidden(p, z):
                dve.wait_ge(h_high_ready, ZS * p.value + z + 1)
                layer, j = divmod(z, FC)
                high, low = h[layer]
                dve.scalar_tensor_tensor(out=low[:, j, :], in0=z_bank[z % 4][:, 0:GT], scalar=0.0,
                                         in1=high[:, j, :], op0=ALU.max, op1=ALU.subtract).then_inc(h_low_ready, 1)

            def add(p, b):
                dve.wait_ge(y_made, G * p.value + b + 1)
                if b == 0:
                    wait(dve, stored[p.slot], 16 * p.pair)
                dve.scalar_tensor_tensor(out=y[p.slot][:, b, :], in0=y_bank[b % 2][0:S, 0:D],
                                         scalar=m["ffn_scale"][0:S, 0:1], in1=xg[p.slot][:, b, :],
                                         op0=ALU.mult, op1=ALU.add).then_inc(y_ready, 1)

            def body(s):
                p = s.back(1)
                for z in range(ZS):
                    if p.exists(NG):
                        low_hidden(p, z)
                    if s.exists(NG):
                        if z == 4:
                            normalise(s)
                        if z == 6:
                            normalise_end(s)
                        if z == 12:
                            low_rows(s)
                if p.exists(NG):
                    for b in range(G):
                        add(p, b)

            weights()
            run_steps(dve, NG, 1, body)

        @block.scalar
        def _(act):
            def body(s):
                p = s.back(1)
                for z in range(ZS):
                    if p.exists(NG):
                        act.wait_ge(z_made, ZS * p.value + z + 1)
                        layer, j = divmod(z, FC)
                        act.activation(h[layer][0][:, j, :], z_bank[z % 4][:, 0:GT], ACT.Relu).then_inc(h_high_ready, 1)
                    if s.exists(NG):
                        if z == 5:
                            act.wait_ge(var_ready, s.value + 1)
                            act.activation(dev[:, :], mean_var[:, :, 1], ACT.Sqrt, bias=m["eps"][0:S, :]).then_inc(dev_ready, 1)
                        if z == 12:
                            for c in range(KC):
                                act.wait_ge(turned, KC * s.value + c + 1)
                                act.activation(xh[s.slot][:, c, :], turn_bank[c][:, 0:GT], ACT.Copy).then_inc(xh_ready, 1)

            run_steps(act, NG, 1, body)

        @block.tensor
        def _(pe):
            def turn(s):
                pe.wait_ge(xn_ready, s.value + 1)
                wait(pe, xl_ready, KC * s.value)
                for c in range(KC):
                    for b in range(G):
                        last = pe.transpose(turn_bank[c][:, b * S:(b + 1) * S], xn[:, b, c * P:(c + 1) * P],
                                            m["ident"][0:S, 0:S])
                    last.then_inc(turned, 1)

            def hidden(p, z):
                layer, j = divmod(z, FC)
                wait(pe, h_low_ready, ZS * p.value + z - 3)
                if z == 0:
                    pe.wait_ge(xl_ready, KC * (p.value + 1))
                parts = h[0] if layer else [xh[p.slot], xl[p.slot]]
                chunks = FC if layer else KC
                for c in range(chunks):
                    if z == FC:
                        pe.wait_ge(h_low_ready, ZS * p.value + c + 1)
                    for n, part in enumerate(parts):
                        last = pe.matmul(z_bank[z % 4][:, 0:GT], w[layer][:, c, j * P:(j + 1) * P], part[:, c, :],
                                         start=c == 0 and n == 0, stop=c == chunks - 1 and n == 1)
                last.then_inc(z_made, 1)

            def output(p, b):
                wait(pe, y_ready, G * p.value + b - 1)
                for c in range(FC):
                    if b == 0:
                        pe.wait_ge(h_low_ready, ZS * p.value + FC + c + 1)
                    for n, part in enumerate(h[1]):
                        last = pe.matmul(y_bank[b % 2][0:S, 0:D], part[:, c, b * S:(b + 1) * S], w[2][:, c, :],
                                         start=c == 0 and n == 0, stop=c == FC - 1 and n == 1)
                last.then_inc(y_made, 1)

            def body(s):
                p = s.back(1)
                for z in range(ZS):
                    if p.exists(NG):
                        hidden(p, z)
                    if s.exists(NG) and z == 11:
                        turn(s)
                if p.exists(NG):
                    for b in range(G):
                        output(p, b)

            pe.wait_ge(w_ready, 3)
            run_steps(pe, NG, 1, body)

        ended.close()
        sems.clear()


def moe_phases(nc, m, a, x_in, x_normed, expert_in, expert_out, out):
    with ExitStack() as ctx:
        def sb(name, shape, dt):
            return ctx.enter_context(nc.sbuf_tensor(name + "_r", shape, dt))

        route = {
            "logits": sb("logits", [S, B, E], F32),
            "put": sb("put", [S, B], U32),
            "get": sb("get", [S, B], U32),
            "weight": sb("weight", [S, B], F32),
        }
        logits_phase(nc, m, a, x_in, x_normed, route)
        ranks_phase(nc, m, route)
        dispatch_phase(nc, route, x_normed, expert_in)
        experts_phase(nc, m, a, expert_in, expert_out)
        combine_phase(nc, route, x_in, expert_out, out)


def logits_phase(nc, m, a, x_in, x_normed, route):
    with ExitStack() as ctx:
        sems = Semaphores(nc, ctx)
        def sb(name, shape, dt):
            return ctx.enter_context(nc.sbuf_tensor(name + "_l", shape, dt))

        def sem(name):
            return sems.new(name + "_l")

        def two(make, name, *args):
            return [make(f"{name}{n}", *args) for n in range(2)]

        wr = sb("wr", [P, KC, E], F32)
        xg = two(sb, "xg", [S, G, D], F32)
        xn = two(sb, "xn", [S, G, D], F32)
        stats = sb("stats", [S, G, 6], F32)
        mean_var = sb("mean_var", [S, G, 2], F32)
        dev = sb("dev", [S, G], F32)
        scale = sb("scale", [S, G], F32)
        xt = two(sb, "xt", [P, KC, GT], F32)
        wr_loaded, x_loaded = sem("wr_loaded"), two(sem, "x_loaded")
        stats_ready, var_ready, dev_ready, scaled = sem("stats_ready"), sem("var_ready"), sem("dev_ready"), sem("scaled")
        xn_ready, stored = sem("xn_ready"), two(sem, "stored")
        turned, xt_ready, made, kept = sem("turned"), sem("xt_ready"), sem("made"), sem("kept")
        passed = sem("passed")
        ended = ExitStack()
        block = ended.enter_context(nc.Block())
        turn_bank = [m["bank"][0:2], m["bank"][2:4]]
        logit_bank = m["bank"][4:6]
        x_rows = x_in.rearrange("(g b) s d -> g s b d", b=G)
        normed_rows = x_normed.rearrange("(g b) s d -> g s b d", b=G)

        @block.sync
        def _(sp):
            sp.dma_start(wr[:, :, :], a["L1_ffn_Wr"].rearrange("(c p) e -> p c e", p=P)).then_inc(wr_loaded, 16)

            def body(s):
                if s.exists(NG):
                    wait(sp, xn_ready, s.back(2).value + 1 if s.back(2).exists(NG) else 0)
                    sp.dma_start(xg[s.slot][:, :, :], take(x_rows, s.value)).then_inc(x_loaded[s.slot], 16)
                p = s.back(1)
                if p.exists(NG):
                    sp.wait_ge(xn_ready, p.value + 1)
                    sp.dma_start(take(normed_rows, p.value), xn[p.slot][:, :, :]).then_inc(stored[p.slot], 16)

            run_steps(sp, NG, 1, body)
            for n in range(2):
                sp.wait_ge(stored[n], 16 * NG // 2)

        @block.tensor
        def _(pe):
            pe.wait_ge(wr_loaded, 16)

            def body(s):
                p = s.back(1)
                if s.exists(NG):
                    pe.wait_ge(xn_ready, s.value + 1)
                    wait(pe, xt_ready, KC * (s.back(2).value + 1) if s.back(2).exists(NG) else 0)
                    for c in range(KC):
                        for b in range(G):
                            last = pe.transpose(turn_bank[s.slot][c][:, b * S:(b + 1) * S],
                                                xn[s.slot][:, b, c * P:(c + 1) * P], m["ident"][0:S, 0:S])
                        last.then_inc(turned, 1)
                if p.exists(NG):
                    pe.wait_ge(xt_ready, KC * (p.value + 1))
                    wait(pe, kept, p.back(2).value + 1 if p.back(2).exists(NG) else 0)
                    for b in range(G):
                        for c in range(KC):
                            last = pe.matmul(logit_bank[p.slot][0:S, b * E:(b + 1) * E], xt[p.slot][:, c, b * S:(b + 1) * S],
                                             wr[:, c, :], start=c == 0, stop=c == KC - 1)
                    last.then_inc(made, 1)

            run_steps(pe, NG, 1, body)

        @block.scalar
        def _(act):
            def body(s):
                if s.exists(NG):
                    act.wait_ge(var_ready, s.value + 1)
                    act.activation(dev[:, :], mean_var[:, :, 1], ACT.Sqrt, bias=m["eps"][0:S, :]).then_inc(dev_ready, 1)
                    wait(act, made, s.back(2).value + 1 if s.back(2).exists(NG) else 0)
                    for c in range(KC):
                        act.wait_ge(turned, KC * s.value + c + 1)
                        act.activation(xt[s.slot][:, c, :], turn_bank[s.slot][c][:, 0:GT], ACT.Copy).then_inc(xt_ready, 1)

            run_steps(act, NG, 1, body)

        @block.vector
        def _(dve):
            def body(s):
                if s.exists(NG):
                    dve.wait_ge(x_loaded[s.slot], 16 * (s.pair + 1))
                    for b in range(G):
                        last = dve.bn_stats(stats[:, b, :], xg[s.slot][:, b, :])
                    last.then_inc(stats_ready, 1)
                    hold(dve, stats_ready, s.value + 1, passed)
                    for b in range(G):
                        last = dve.bn_aggr(mean_var[:, b, :], stats[:, b, :])
                    last.then_inc(var_ready, 1)
                    dve.wait_ge(dev_ready, s.value + 1)
                    dve.reciprocal(scale[:, :], dev[:, :]).then_inc(scaled, 1)
                    dve.wait_ge(scaled, s.value + 1)
                    wait(dve, turned, KC * (s.back(2).value + 1) if s.back(2).exists(NG) else 0)
                    wait(dve, stored[s.slot], 16 * s.pair)
                    for b in range(G):
                        last = dve.tensor_scalar(xn[s.slot][:, b, :], xg[s.slot][:, b, :], mean_var[:, b, 0:1],
                                                 scale[:, b:b + 1], ALU.subtract, ALU.mult)
                    last.then_inc(xn_ready, 1)
                p = s.back(1)
                if p.exists(NG):
                    dve.wait_ge(made, p.value + 1)
                    dst = route["logits"][:, :, :].rearrange("s (g b) e -> s g (b e)", b=G)
                    at = dst[:, p.value, :] if isinstance(p.value, int) else dst[:, bass.ds(p.value, 1), :].squeeze(1)
                    dve.tensor_scalar(at, logit_bank[p.slot][0:S, 0:G * E], 1.0, None, ALU.mult).then_inc(kept, 1)

            run_steps(dve, NG, 1, body)

        ended.close()
        sems.clear()


def ranks_phase(nc, m, route):
    with ExitStack() as ctx:
        sems = Semaphores(nc, ctx)
        def sb(name, shape=(S, B, E), dt=F32):
            return ctx.enter_context(nc.sbuf_tensor(name + "_k", list(shape), dt))

        def sem(name):
            return sems.new(name + "_k")

        before = sb("before", (S, S))
        ones = sb("ones", (S, S))
        number = sb("number")
        top, first, prob, rank, kept, base = (sb(n, (S, B)) for n in ("top", "first", "prob", "rank", "kept", "base"))
        shifted, power, equal, chosen, counts, total = (sb(n) for n in ("shifted", "power", "equal", "chosen", "counts", "total"))
        sums = [sb(f"sums{n}") for n in range(2)]
        step, made, product, powered = sem("step"), sem("made"), sem("product"), sem("powered")
        passed = sem("passed")
        ended = ExitStack()
        block = ended.enter_context(nc.Block())
        rank_bank, count_bank = m["bank"][0], m["bank"][1]

        @block.gpsimd
        def _(pool):
            pool.memset(before[:, :], 0.0).then_inc(made, 1)
            pool.memset(ones[:, :], 1.0).then_inc(made, 1)
            pool.wait_ge(made, 2)
            pool.affine_select(out=before[:, :], in_=before[:, :], compare_op=ALU.is_ge, fill=1.0, base=0,
                               pattern=[[-1, S]], channel_multiplier=1).then_inc(made, 1)
            for e in range(E):
                pool.memset(number[:, :, e], float(e - E)).then_inc(made, 1)

        @block.scalar
        def _(act):
            act.wait_ge(step, 2)
            act.activation(power[:, :, :], shifted[:, :, :], ACT.Exp).then_inc(powered, 1)

        @block.tensor
        def _(pe):
            pe.wait_ge(made, 3)
            pe.wait_ge(step, 6)
            pe.matmul(rank_bank[0:S, 0:B * E], before[:, :], chosen[:, :, :].rearrange("s b e -> s (b e)"),
                      start=True, stop=True).then_inc(product, 1)
            pe.matmul(count_bank[0:S, 0:B * E], ones[:, :], chosen[:, :, :].rearrange("s b e -> s (b e)"),
                      start=True, stop=True).then_inc(product, 1)

        @block.vector
        def _(dve):
            done = 0

            def link(ins):
                nonlocal done
                done += 1
                ins.then_inc(step, 1)
                dve.wait_ge(step, done)

            def wide(t):
                return t[:, :].unsqueeze(2).to_broadcast([S, B, E])

            logits = route["logits"]
            link(dve.tensor_reduce(top[:, :], logits[:, :, :], AX.X, ALU.max))
            link(dve.tensor_tensor(shifted[:, :, :], logits[:, :, :], wide(top), ALU.subtract))
            link(dve.tensor_scalar(equal[:, :, :], shifted[:, :, :], 0.0, None, ALU.is_equal))
            dve.wait_ge(made, 3 + E)
            link(dve.tensor_tensor(equal[:, :, :], equal[:, :, :], number[:, :, :], ALU.mult))
            link(dve.tensor_reduce(first[:, :], equal[:, :, :], AX.X, ALU.min))
            link(dve.tensor_tensor(chosen[:, :, :], number[:, :, :], wide(first), ALU.is_equal))
            dve.wait_ge(powered, 1)
            link(dve.tensor_reduce(prob[:, :], power[:, :, :], AX.X, ALU.add))
            link(dve.reciprocal(prob[:, :], prob[:, :]))
            dve.wait_ge(product, 2)
            link(dve.tensor_copy(counts[:, :, :].rearrange("s b e -> s (b e)"), count_bank[0:S, 0:B * E]))
            old = counts
            shift, turn = 1, 0
            while shift < B:
                new = sums[turn]
                link(dve.tensor_copy(new[:, 0:shift, :], old[:, 0:shift, :]))
                link(dve.tensor_tensor(new[:, shift:B, :], old[:, shift:B, :], old[:, 0:B - shift, :], ALU.add))
                old, shift, turn = new, 2 * shift, 1 - turn
            link(dve.tensor_tensor(total[:, :, :], old[:, :, :], counts[:, :, :], ALU.subtract))
            link(dve.tensor_tensor(total[:, :, :].rearrange("s b e -> s (b e)"), rank_bank[0:S, 0:B * E],
                                   total[:, :, :].rearrange("s b e -> s (b e)"), ALU.add))
            link(dve.tensor_tensor(total[:, :, :], total[:, :, :], chosen[:, :, :], ALU.mult))
            link(dve.tensor_reduce(rank[:, :], total[:, :, :], AX.X, ALU.add))
            link(dve.tensor_scalar(kept[:, :], rank[:, :], float(CAP), None, ALU.is_lt))
            link(dve.tensor_scalar(base[:, :], first[:, :], float(CAP), float(E * CAP), ALU.mult, ALU.add))
            link(dve.tensor_scalar(rank[:, :], rank[:, :], float(CAP - 1), None, ALU.min))
            link(dve.tensor_tensor(base[:, :], base[:, :], rank[:, :], ALU.add))
            link(dve.tensor_copy(route["get"][:, :], base[:, :]))
            link(dve.tensor_scalar(rank[:, :], kept[:, :], -float(2 * E * CAP), float(2 * E * CAP), ALU.mult, ALU.add))
            link(dve.tensor_tensor(route["put"][:, :], base[:, :], rank[:, :], ALU.add))
            link(dve.tensor_tensor(prob[:, :], prob[:, :], kept[:, :], ALU.mult))
            link(dve.tensor_scalar(route["weight"][:, :], prob[:, :], m["gate"][0:S, 3:4], None, ALU.mult))

        ended.close()
        sems.clear()


def dispatch_phase(nc, route, x_in, expert_in):
    with ExitStack() as ctx:
        sems = Semaphores(nc, ctx)
        def sem(name):
            return sems.new(name + "_d")

        xg = [ctx.enter_context(nc.sbuf_tensor(f"xg{n}_d", [S, G, D], F32)) for n in range(2)]
        index = [ctx.enter_context(nc.sbuf_tensor(f"index{n}_d", [S, G], U32)) for n in range(2)]
        x_loaded, put = [sem(f"x_loaded{n}") for n in range(2)], [sem(f"put{n}") for n in range(2)]
        index_ready = sem("index_ready")
        passed = sem("passed")
        ended = ExitStack()
        block = ended.enter_context(nc.Block())
        x_rows = x_in.rearrange("(g b) s d -> g s b d", b=G)

        @block.sync
        def _(sp):
            def body(s):
                if s.exists(NG):
                    wait(sp, put[s.slot], 16 * G * s.pair)
                    sp.dma_start(xg[s.slot][:, :, :], take(x_rows, s.value)).then_inc(x_loaded[s.slot], 16)

            run_steps(sp, NG, 0, body)

        @block.vector
        def _(dve):
            def body(s):
                wait(dve, put[s.slot], 16 * G * s.pair)
                copy_index(dve, index[s.slot], route["put"], s).then_inc(index_ready, 1)

            run_steps(dve, NG, 0, body)

        @block.gpsimd
        def _(pool):
            def body(s):
                pool.wait_ge(x_loaded[s.slot], 16 * (s.pair + 1))
                hold(pool, index_ready, s.value + 1, passed)
                for b in range(G):
                    pool.indirect_dma_start(expert_in[:, :], bass.IndirectOffsetOnAxis(index[s.slot][:, b:b + 1], 0),
                                            xg[s.slot][:, b, :], None, bounds_check=E * CAP - 1,
                                            oob_is_err=False).then_inc(put[s.slot], 16)

            run_steps(pool, NG, 0, body)
            for n in range(2):
                pool.wait_ge(put[n], 16 * G * NG // 2)

        ended.close()
        sems.clear()


def copy_index(dve, slot, table, s):
    groups = table[:, :].rearrange("s (g b) -> s g b", b=G)
    at = groups[:, s.value, :] if isinstance(s.value, int) else groups[:, bass.ds(s.value, 1), :].squeeze(1)
    return dve.tensor_scalar(slot[:, :], at, 0.0, None, ALU.add)


def experts_phase(nc, m, a, expert_in, expert_out):
    with ExitStack() as ctx:
        sems = Semaphores(nc, ctx)
        def sb(name, shape, dt):
            return ctx.enter_context(nc.sbuf_tensor(name + "_e", shape, dt))

        def sem(name):
            return sems.new(name + "_e")

        def two(make, name, *args):
            return [make(f"{name}{n}", *args) for n in range(2)]

        w1 = two(sb, "w1", [P, KC, F], F32)
        w2 = two(sb, "w2", [P, FC, D], F32)
        xg = two(sb, "xg", [S, G, D], F32)
        xt = two(sb, "xt", [P, KC, GT], F32)
        h = sb("h", [P, FC, GT], F32)
        y = two(sb, "y", [S, G, D], F32)
        x_loaded, w_loaded, stored = two(sem, "x_loaded"), two(sem, "w_loaded"), two(sem, "stored")
        turned, xt_ready, z_made = sem("turned"), sem("xt_ready"), sem("z_made")
        h_even_ready, h_odd_ready, y_made = sem("h_even_ready"), sem("h_odd_ready"), sem("y_made")
        y_even_ready, y_odd_ready = sem("y_even_ready"), sem("y_odd_ready")
        passed = sem("passed")
        ended = ExitStack()
        block = ended.enter_context(nc.Block())
        z_bank, y_bank, turn_bank = m["bank"][0:4], m["bank"][4:6], m["bank"][6:8]
        in_rows = expert_in.rearrange("(e t s) d -> e s t d", e=E, s=S)
        out_rows = expert_out.rearrange("(e t s) d -> e s t d", e=E, s=S)
        w1_rows = a["L1_ffn_W1"].rearrange("e (c p) f -> e p c f", p=P)
        w2_rows = a["L1_ffn_W2"].rearrange("e (c p) d -> e p c d", p=P)
        HC, HG = FC // 2, G // 2

        @block.sync
        def _(sp):
            def body(s):
                if s.exists(E):
                    wait(sp, turned, KC * (s.back(2).value + 1) if s.back(2).exists(E) else 0)
                    sp.dma_start(xg[s.slot][:, :, :], take(in_rows, s.value)).then_inc(x_loaded[s.slot], 16)
                    wait(sp, y_made, G * (s.back(2).value + 1) if s.back(2).exists(E) else 0)
                    sp.dma_start(w1[s.slot][:, :, :], take(w1_rows, s.value)).then_inc(w_loaded[s.slot], 16)
                    sp.dma_start(w2[s.slot][:, :, :], take(w2_rows, s.value)).then_inc(w_loaded[s.slot], 16)

            run_steps(sp, E, 1, body)

        @block.gpsimd
        def _(pool):
            def body(s):
                p = s.back(1)
                if p.exists(E):
                    pool.wait_ge(y_even_ready, HG * (p.value + 1))
                    hold(pool, y_odd_ready, HG * (p.value + 1), passed)
                    pool.dma_start(take(out_rows, p.value), y[p.slot][:, :, :]).then_inc(stored[p.slot], 16)

            run_steps(pool, E, 1, body)
            for n in range(2):
                pool.wait_ge(stored[n], 16 * E // 2)

        @block.tensor
        def _(pe):
            def turn(s):
                pe.wait_ge(x_loaded[s.slot], 16 * (s.pair + 1))
                wait(pe, xt_ready, KC * s.value)
                for c in range(KC):
                    for b in range(G):
                        last = pe.transpose(turn_bank[c][:, b * S:(b + 1) * S], xg[s.slot][:, b, c * P:(c + 1) * P],
                                            m["ident"][0:S, 0:S])
                    last.then_inc(turned, 1)

            def body(s):
                p = s.back(1)
                for j in range(FC):
                    if p.exists(E):
                        if j == 0:
                            pe.wait_ge(w_loaded[p.slot], 32 * (p.pair + 1))
                            pe.wait_ge(xt_ready, KC * (p.value + 1))
                        ready = (h_even_ready, h_odd_ready)[j % 2]
                        wait(pe, ready, HC * p.value + j // 2 - 1)
                        for c in range(KC):
                            last = pe.matmul(z_bank[j % 4][:, 0:GT], w1[p.slot][:, c, j * P:(j + 1) * P],
                                             xt[p.slot][:, c, :], start=c == 0, stop=c == KC - 1)
                        last.then_inc(z_made, 1)
                    if s.exists(E) and j == FC - 1:
                        turn(s)
                if p.exists(E):
                    for b in range(G):
                        wait(pe, (y_even_ready, y_odd_ready)[b % 2], HG * p.value + b // 2)
                        for c in range(FC):
                            if b == 0:
                                pe.wait_ge((h_even_ready, h_odd_ready)[c % 2], HC * p.value + c // 2 + 1)
                            last = pe.matmul(y_bank[b % 2][0:S, 0:D], h[:, c, b * S:(b + 1) * S], w2[p.slot][:, c, :],
                                             start=c == 0, stop=c == FC - 1)
                        last.then_inc(y_made, 1)

            run_steps(pe, E, 1, body)

        @block.scalar
        def _(act):
            def body(s):
                p = s.back(1)
                if p.exists(E):
                    wait(act, y_made, G * p.value)
                    for j in range(0, FC, 2):
                        act.wait_ge(z_made, FC * p.value + j + 1)
                        act.activation(h[:, j, :], z_bank[j % 4][:, 0:GT], ACT.Relu).then_inc(h_even_ready, 1)
                if s.exists(E):
                    for c in range(KC):
                        act.wait_ge(turned, KC * s.value + c + 1)
                        act.activation(xt[s.slot][:, c, :], turn_bank[c][:, 0:GT], ACT.Copy).then_inc(xt_ready, 1)
                if p.exists(E):
                    wait(act, stored[p.slot], 16 * p.pair)
                    for b in range(0, G, 2):
                        act.wait_ge(y_made, G * p.value + b + 1)
                        act.activation(y[p.slot][:, b, :], y_bank[0][0:S, 0:D], ACT.Copy).then_inc(y_even_ready, 1)

            run_steps(act, E, 1, body)

        @block.vector
        def _(dve):
            def body(s):
                p = s.back(1)
                if p.exists(E):
                    wait(dve, y_made, G * p.value)
                    for j in range(1, FC, 2):
                        dve.wait_ge(z_made, FC * p.value + j + 1)
                        dve.tensor_scalar(h[:, j, :], z_bank[j % 4][:, 0:GT], 0.0, None, ALU.max).then_inc(h_odd_ready, 1)
                    wait(dve, stored[p.slot], 16 * p.pair)
                    for b in range(1, G, 2):
                        dve.wait_ge(y_made, G * p.value + b + 1)
                        dve.tensor_copy(y[p.slot][:, b, :], y_bank[1][0:S, 0:D]).then_inc(y_odd_ready, 1)

            run_steps(dve, E, 1, body)

        ended.close()
        sems.clear()


def combine_phase(nc, route, x_in, expert_out, out):
    with ExitStack() as ctx:
        sems = Semaphores(nc, ctx)
        def sb(name, shape, dt):
            return ctx.enter_context(nc.sbuf_tensor(name + "_c", shape, dt))

        def sem(name):
            return sems.new(name + "_c")

        def two(make, name, *args):
            return [make(f"{name}{n}", *args) for n in range(2)]

        xg, y, total = (two(sb, name, [S, G, D], F32) for name in ("xg", "y", "total"))
        index = two(sb, "index", [S, G], U32)
        weight = sb("weight", [S, G], F32)
        x_loaded, got, stored = two(sem, "x_loaded"), two(sem, "got"), two(sem, "stored")
        index_ready, weight_ready, added = sem("index_ready"), sem("weight_ready"), sem("added")
        passed = sem("passed")
        ended = ExitStack()
        block = ended.enter_context(nc.Block())
        x_rows = x_in.rearrange("(g b) s d -> g s b d", b=G)
        out_rows = out.rearrange("(g b) s d -> g s b d", b=G)

        @block.sync
        def _(sp):
            def body(s):
                p = s.back(1)
                if s.exists(NG):
                    wait(sp, added, s.back(2).value + 1 if s.back(2).exists(NG) else 0)
                    sp.dma_start(xg[s.slot][:, :, :], take(x_rows, s.value)).then_inc(x_loaded[s.slot], 16)
                if p.exists(NG):
                    sp.wait_ge(added, p.value + 1)
                    sp.dma_start(take(out_rows, p.value), total[p.slot][:, :, :]).then_inc(stored[p.slot], 16)

            run_steps(sp, NG, 1, body)
            for n in range(2):
                sp.wait_ge(stored[n], 16 * NG // 2)

        @block.gpsimd
        def _(pool):
            def body(s):
                if s.exists(NG):
                    pool.wait_ge(index_ready, s.value + 1)
                    hold(pool, added, s.back(2).value + 1 if s.back(2).exists(NG) else 0, passed)
                    for b in range(G):
                        pool.indirect_dma_start(y[s.slot][:, b, :], None, expert_out[:, :],
                                                bass.IndirectOffsetOnAxis(index[s.slot][:, b:b + 1], 0)
                                                ).then_inc(got[s.slot], 16)

            run_steps(pool, NG, 1, body)

        @block.vector
        def _(dve):
            def body(s):
                p = s.back(1)
                if s.exists(NG):
                    wait(dve, got[s.slot], 16 * G * s.pair)
                    copy_index(dve, index[s.slot], route["get"], s).then_inc(index_ready, 1)
                if p.exists(NG):
                    wait(dve, added, p.value)
                    copy_index(dve, weight, route["weight"], p).then_inc(weight_ready, 1)
                    dve.wait_ge(weight_ready, p.value + 1)
                    dve.wait_ge(x_loaded[p.slot], 16 * (p.pair + 1))
                    dve.wait_ge(got[p.slot], 16 * G * (p.pair + 1))
                    wait(dve, stored[p.slot], 16 * p.pair)
                    for b in range(G):
                        last = dve.scalar_tensor_tensor(out=total[p.slot][:, b, :], in0=y[p.slot][:, b, :],
                                                        scalar=weight[:, b:b + 1], in1=xg[p.slot][:, b, :],
                                                        op0=ALU.mult, op1=ALU.add)
                    last.then_inc(added, 1)

            run_steps(dve, NG, 1, body)

        ended.close()
        sems.clear()


_INS = ["x", "ctx_1024", "mask_1x1xSxS2_ik1", "mask_BxSxS2_if1", "g_xattn", "g_ffn",
        "L0_xattn_w_q", "L0_xattn_w_k", "L0_xattn_w_v", "L0_xattn_w_o", "L0_xattn_b_o",
        "L0_ffn_k0", "L0_ffn_k1", "L0_ffn_k2", "L0_ffn_s0", "L0_ffn_s1", "L0_ffn_s2",
        "L1_xattn_Wq", "L1_xattn_Wk", "L1_xattn_Wv", "L1_xattn_Wo", "L1_xattn_bo",
        "L1_ffn_Wr", "L1_ffn_W1", "L1_ffn_W2"]


def kernel(**inputs):
    import numpy as _np
    import concourse.bacc as _bacc
    from concourse import mybir as _mybir
    from concourse.bass_utils import run_bass_kernel_spmd as _run

    nc = _bacc.Bacc("TRN2", target_bir_lowering=False, num_devices=1)
    arrays, args = {}, {}
    for name in _INS:
        a = _np.ascontiguousarray(inputs[name])
        if a.ndim == 0:
            a = a.reshape(1)
        arrays[f"in_{name}_dram"] = a
        args[name] = nc.dram_tensor(f"in_{name}_dram", a.shape, _mybir.dt.from_np(a.dtype), kind="ExternalInput").ap()
    out = nc.dram_tensor("out_0_dram", (B, S, D), F32, kind="ExternalOutput").ap()
    flamingo_program(nc, args, out)
    r = _run(nc, [arrays], core_ids=[0])
    return r.results[0]["out_0_dram"]
```

```python
from contextlib import ExitStack

import concourse.bass as bass
from concourse import mybir

F32 = mybir.dt.float32
F16 = mybir.dt.float16
BF16 = mybir.dt.bfloat16
I32 = mybir.dt.int32
U32 = mybir.dt.uint32
U8 = mybir.dt.uint8
ALU = mybir.AluOpType
ACT = mybir.ActivationFunctionType
AX = mybir.AxisListType

P = 128
B, S, D = 32, 112, 256
S2 = 375
H, DK = 16, 16
KC = D // P
CH = 3
CK = S2 // CH
NP = H // 2
QUAD = 32
NT = H // 4
UNITS = NT * CH
G = 4
NG = B // G
GT = G * S
F = 1024
FC = F // P
E = 8
CAP = B * S // E
STACK = 3 * QUAD
ROWS = STACK + 2
MASKED = float(2 ** 30)
EPS = 1e-5
LARGEST = 3.0e38


class Step:

    def __init__(self, pair, slot):
        self.pair, self.slot = pair, slot
        self.value = 2 * pair + slot

    def back(self, n):
        total = self.slot - n
        pairs = total // 2
        return Step(self.pair + pairs if pairs else self.pair, total % 2)

    def exists(self, count):
        return 0 <= self.value < count if isinstance(self.value, int) else count > 1


def run_steps(eng, count, lag, body, head=4):
    for s in range(head):
        body(Step(s // 2, s % 2))
    with eng.Fori(head // 2, count // 2) as pair:
        for slot in range(2):
            body(Step(pair, slot))
    for s in range(count, count + lag):
        body(Step(s // 2, s % 2))


def wait(eng, sem, value):
    if not isinstance(value, int) or value > 0:
        eng.wait_ge(sem, value)


class Semaphores:

    def __init__(self, nc, stack):
        self.nc, self.stack, self.made = nc, stack, []

    def new(self, name):
        self.made.append(self.stack.enter_context(self.nc.semaphore(name)))
        return self.made[-1]

    def clear(self):
        with self.nc.Block() as block:
            @block.sync
            def _(sp):
                for s in self.made:
                    sp.sem_clear(s)


def flamingo_program(nc, a, out):
    def dram(name, shape, dt):
        return nc.dram_tensor(name, shape, dt, kind="Internal").ap()

    x1 = dram("x_after_attention_0", [B, S, D], F32)
    x2 = dram("x_after_ffn_0", [B, S, D], F32)
    x3 = dram("x_after_attention_1", [B, S, D], F32)
    x3_normed = dram("x_after_attention_1_normed", [B, S, D], F32)
    q_split = dram("q_split", [2, 3, P, B * S], F16) 
    k_split = dram("k_split", [2, 2, 3, P, S2], F16)
    expert_in = dram("expert_in", [E * CAP, D], F32)
    expert_out = dram("expert_out", [E * CAP, D], F32)

    with ExitStack() as ctx:
        def sb(name, shape, dt):
            return ctx.enter_context(nc.sbuf_tensor(name, shape, dt))

        m = {
            "bank": [ctx.enter_context(nc.psum_tensor(f"bank{i}", [P, 512], F32)) for i in range(8)],
            "ident": sb("ident", [P, P], F32),
            "ident_h": sb("ident_h", [P, P], F16),
            "ident_b": sb("ident_b", [P, P], BF16),
            "eps": sb("eps", [P, 1], F32),
            "gate": sb("gate", [P, 4], F32),
            "ffn_scale": sb("ffn_scale", [P, 1], F32),
            "sign": sb("sign", [P, 2], F32),
            "wq": [sb(f"wq{n}", [P, KC, D], F32) for n in range(2)],
            "wk": [sb(f"wk{n}", [P, KC, D], F32) for n in range(2)],
            "wv": [sb(f"wv{n}", [P, KC, D], F32) for n in range(2)],
            "wo": [sb(f"wo{n}", [P, KC, D], F32) for n in range(2)],
            "bo": [sb(f"bo{n}", [S, D], F32) for n in range(2)],
        }
        setup_phase(nc, m, a, expert_in)
        queries_phase(nc, m, 0, a["x"], a["mask_1x1xSxS2_ik1"], q_split)
        attention_phase(nc, m, 0, a["x"], x1, a["ctx_1024"], a["mask_1x1xSxS2_ik1"], q_split, k_split)
        ffn_phase(nc, m, a, x1, x2)
        queries_phase(nc, m, 1, x2, a["mask_BxSxS2_if1"], q_split)
        attention_phase(nc, m, 1, x2, x3, a["ctx_1024"], a["mask_BxSxS2_if1"], q_split, k_split)
        moe_phases(nc, m, a, x3, x3_normed, expert_in, expert_out, out)


def setup_phase(nc, m, a, expert_in):
    with ExitStack() as ctx:
        sems = Semaphores(nc, ctx)
        def sem(name):
            return sems.new(name)

        zeros = ctx.enter_context(nc.sbuf_tensor("zeros", [P, CAP * E * D // P // 4], F32))
        gin = ctx.enter_context(nc.sbuf_tensor("gate_in", [P, 4], F32))
        sin = ctx.enter_context(nc.sbuf_tensor("scale_in", [P, 3], F32))
        mag = ctx.enter_context(nc.sbuf_tensor("scale_parts", [P, 4], F32))
        small_loaded, weights_loaded = sem("small_loaded"), sem("weights_loaded")
        cleared, made = sem("su_cleared"), sem("su_made")
        chain, gated, experts_cleared = sem("su_chain"), sem("su_gated"), sem("experts_cleared")
        passed = sem("passed")
        ended = ExitStack()
        block = ended.enter_context(nc.Block())

        def chunked(w):
            return w.rearrange("(c p) n -> p c n", p=P)

        @block.sync
        def _(sp):
            for n, g in enumerate((a["g_xattn"], a["g_ffn"])):
                sp.dma_start(gin[:, 2 * n:2 * n + 2], g.partition_broadcast(P)).then_inc(small_loaded, 16)
            for n in range(3):
                s = a[f"L0_ffn_s{n}"]
                sp.dma_start(sin[:, n:n + 1], s.partition_broadcast(P)).then_inc(small_loaded, 16)
            for w in "qkvo":
                for n, name in enumerate((f"L0_xattn_w_{w}", f"L1_xattn_W{w}")):
                    sp.dma_start(m["w" + w][n][:, :, :], chunked(a[name])).then_inc(weights_loaded, 16)
            for n, b in enumerate((a["L0_xattn_b_o"], a["L1_xattn_bo"])):
                sp.dma_start(m["bo"][n][:, :], b.partition_broadcast(S)).then_inc(weights_loaded, 16)
            sp.wait_ge(cleared, 1)
            rows = expert_in.rearrange("(f p r) n -> f p (r n)", f=4, p=P)
            for f in range(4):
                sp.dma_start(rows[f], zeros[:, :]).then_inc(experts_cleared, 16)
            sp.wait_ge(experts_cleared, 64)
            sp.wait_ge(weights_loaded, 160)

        @block.gpsimd
        def _(pool):
            for t in (m["ident"], m["ident_h"], m["ident_b"]):
                pool.memset(t[:, :], 0.0).then_inc(made, 1)
            pool.wait_ge(made, 3)
            for t in (m["ident"], m["ident_h"], m["ident_b"]):
                pool.affine_select(out=t[:, :], in_=t[:, :], compare_op=ALU.not_equal, fill=1.0, base=0,
                                   pattern=[[-1, P]], channel_multiplier=1).then_inc(made, 1)

        @block.vector
        def _(dve):
            dve.memset(zeros[:, :], 0.0).then_inc(cleared, 1)
            dve.memset(m["eps"][:, :], EPS)
            dve.wait_ge(small_loaded, 80)
            steps = 0

            def link(ins):
                nonlocal steps
                steps += 1
                ins.then_inc(chain, 1)
                dve.wait_ge(chain, steps)

            link(dve.tensor_scalar(m["sign"][:, :], sin[:, 0:2], 0.0, None, ALU.is_ge))
            link(dve.tensor_scalar(m["sign"][:, :], m["sign"][:, :], 2.0, -1.0, ALU.mult, ALU.add))
            link(dve.tensor_tensor(mag[:, 0:2], sin[:, 0:2], m["sign"][:, :], ALU.mult))
            link(dve.tensor_tensor(mag[:, 2:3], mag[:, 0:1], mag[:, 1:2], ALU.mult))
            link(dve.tensor_tensor(mag[:, 3:4], mag[:, 2:3], sin[:, 2:3], ALU.mult))
            dve.wait_ge(gated, 1)
            link(dve.tensor_scalar(m["ffn_scale"][:, :], mag[:, 3:4], m["gate"][:, 2:3], 4.0 * 32.0,
                                   ALU.mult, ALU.mult))

        @block.scalar
        def _(act):
            act.wait_ge(small_loaded, 80)
            act.activation(m["gate"][:, :], gin[:, :], ACT.Tanh).then_inc(gated, 1)

        ended.close()
        sems.clear()


def queries_phase(nc, m, layer, x_in, mask, q_split):
    tag = f"_q{layer}"
    with ExitStack() as ctx:
        sems = Semaphores(nc, ctx)
        def sb(name, shape, dt):
            return ctx.enter_context(nc.sbuf_tensor(name + tag, shape, dt))

        def sem(name):
            return sems.new(name + tag)

        masks = G if layer else 1
        xg = [sb(f"xg{n}", [S, G, D], F32) for n in range(2)]
        mask_in = [sb(f"mask_in{n}", [S, masks, S2], I32) for n in range(2)]
        mask_f = sb("mask_f", [S, masks, S2], F32)
        seen = sb("seen", [S, masks], F32)
        stats = sb("stats", [S, G, 6], F32)
        mean_var = sb("mean_var", [S, G, 2], F32)
        dev = sb("dev", [S, G], F32)
        scale = sb("scale", [S, G], F32)
        xn = [sb(f"xn{n}", [S, G, D], F32) for n in range(2)]
        xt = [sb(f"xt{n}", [P, KC, GT], F32) for n in range(2)]
        high = [sb(f"high{n}", [P, KC, GT], F16) for n in range(2)]
        low = [sb(f"low{n}", [P, KC, GT], F16) for n in range(2)]
        x_loaded = [sem(f"x_loaded{n}") for n in range(2)]
        mask_loaded = [sem(f"mask_loaded{n}") for n in range(2)]
        dve_chain, var_ready, dev_ready, scaled = sem("dve_chain"), sem("var_ready"), sem("dev_ready"), sem("scaled")
        xn_ready, turned, xt_ready, q_ready = sem("xn_ready"), sem("turned"), sem("xt_ready"), sem("q_ready")
        high_ready, low_ready = sem("high_ready"), sem("low_ready")
        stored = [sem(f"stored{n}") for n in range(2)]
        passed = sem("passed")
        ended = ExitStack()
        block = ended.enter_context(nc.Block())
        turn_bank = [m["bank"][0:2], m["bank"][2:4]]
        q_bank = [m["bank"][4:6], m["bank"][6:8]]
        x_rows = x_in.rearrange("(g b) s d -> g s b d", b=G)
        q_out = q_split.rearrange("e w p (g t) -> w g p e t", t=GT)

        @block.sync
        def _(sp):
            if not layer:
                sp.dma_start(mask_in[0][:, 0, :], mask[0, 0, :, :]).then_inc(mask_loaded[0], 16)

            def body(s):
                if s.exists(NG):
                    wait(sp, xn_ready, s.back(2).value + 1 if s.back(2).exists(NG) else 0)
                    sp.dma_start(xg[s.slot][:, :, :], take(x_rows, s.value)).then_inc(x_loaded[s.slot], 16)
                    if layer:
                        rows = mask.rearrange("(g b) s k -> g s b k", b=G)
                        sp.dma_start(mask_in[s.slot][:, :, :],
                                     take(rows, s.value)).then_inc(mask_loaded[s.slot], 16)
                p = s.back(1)
                if p.exists(NG):
                    for g, (tile, ready) in enumerate(((high, high_ready), (high, high_ready), (low, low_ready))):
                        wait(sp, ready, 2 * (p.value + 1))
                        sp.dma_start(take(q_out[g], p.value), tile[p.slot][:, :, :]).then_inc(stored[p.slot], 16)

            run_steps(sp, NG, 1, body)
            for n in range(2):
                sp.wait_ge(stored[n], 48 * NG // 2)

        @block.vector
        def _(dve):
            def see(slot):
                dve.tensor_scalar(mask_f[:, :, :], mask_in[slot][:, :, :], 0.0, None,
                                  ALU.not_equal).then_inc(dve_chain, 1)

            if not layer:
                dve.wait_ge(mask_loaded[0], 16)
                see(0)
                dve.wait_ge(dve_chain, 1)
                dve.tensor_reduce(seen[:, :], mask_f[:, :, :], AX.X, ALU.max).then_inc(dve_chain, 1)
            per, first = (3, 0) if layer else (1, 2)

            def body(s):
                if s.exists(NG):
                    dve.wait_ge(x_loaded[s.slot], 16 * (s.pair + 1))
                    done = per * s.value + first
                    if layer:
                        dve.wait_ge(mask_loaded[s.slot], 16 * (s.pair + 1))
                        wait(dve, dve_chain, done)
                        see(s.slot)
                        dve.wait_ge(dve_chain, done + 1)
                        dve.tensor_reduce(seen[:, :], mask_f[:, :, :], AX.X, ALU.max).then_inc(dve_chain, 1)
                        done = done + 2
                    for b in range(G):
                        last = dve.bn_stats(stats[:, b, :], xg[s.slot][:, b, :])
                    last.then_inc(dve_chain, 1)
                    hold(dve, dve_chain, done + 1, passed)
                    for b in range(G):
                        last = dve.bn_aggr(mean_var[:, b, :], stats[:, b, :])
                    last.then_inc(var_ready, 1)
                    dve.wait_ge(dev_ready, s.value + 1)
                    dve.reciprocal(scale[:, :], dev[:, :]).then_inc(scaled, 1)
                    dve.wait_ge(scaled, 2 * s.value + 1)
                    seen_all = seen[:, :] if layer else seen[:, :].to_broadcast([S, G])
                    dve.tensor_tensor(scale[:, :], scale[:, :], seen_all, ALU.mult).then_inc(scaled, 1)
                    dve.wait_ge(scaled, 2 * s.value + 2)
                    wait(dve, turned, 2 * (s.back(2).value + 1) if s.back(2).exists(NG) else 0)
                    for b in range(G):
                        last = dve.tensor_scalar(xn[s.slot][:, b, :], xg[s.slot][:, b, :], mean_var[:, b, 0:1],
                                                 scale[:, b:b + 1], ALU.subtract, ALU.mult)
                    last.then_inc(xn_ready, 1)
                p = s.back(1)
                if p.exists(NG):
                    wait(dve, stored[p.slot], 48 * p.pair)
                    for c in range(KC):
                        dve.wait_ge(high_ready, 2 * p.value + c + 1)
                        dve.tensor_tensor(low[p.slot][:, c, :], q_bank[p.slot][c][:, 0:GT],
                                          high[p.slot][:, c, :], ALU.subtract).then_inc(low_ready, 1)

            run_steps(dve, NG, 1, body)

        @block.scalar
        def _(act):
            def body(s):
                if s.exists(NG):
                    act.wait_ge(var_ready, s.value + 1)
                    act.activation(dev[:, :], mean_var[:, :, 1], ACT.Sqrt, bias=m["eps"][0:S, :]).then_inc(dev_ready, 1)
                    wait(act, q_ready, 2 * (s.back(2).value + 1) if s.back(2).exists(NG) else 0)
                    for c in range(KC):
                        act.wait_ge(turned, 2 * s.value + c + 1)
                        act.activation(xt[s.slot][:, c, :], turn_bank[s.slot][c][:, 0:GT], ACT.Copy).then_inc(xt_ready, 1)
                p = s.back(1)
                if p.exists(NG):
                    wait(act, stored[p.slot], 48 * p.pair)
                    for c in range(KC):
                        act.wait_ge(q_ready, 2 * p.value + c + 1)
                        act.activation(high[p.slot][:, c, :], q_bank[p.slot][c][:, 0:GT], ACT.Copy).then_inc(high_ready, 1)

            run_steps(act, NG, 1, body)

        @block.tensor
        def _(pe):
            def body(s):
                if s.exists(NG):
                    pe.wait_ge(xn_ready, s.value + 1)
                    wait(pe, xt_ready, 2 * (s.back(2).value + 1) if s.back(2).exists(NG) else 0)
                    for c in range(KC):
                        for b in range(G):
                            last = pe.transpose(turn_bank[s.slot][c][:, b * S:(b + 1) * S],
                                                xn[s.slot][:, b, c * P:(c + 1) * P], m["ident"][0:S, 0:S])
                        last.then_inc(turned, 1)
                p = s.back(1)
                if p.exists(NG):
                    pe.wait_ge(xt_ready, 2 * (p.value + 1))
                    wait(pe, low_ready, 2 * (p.back(2).value + 1) if p.back(2).exists(NG) else 0)
                    for j in range(KC):
                        for c in range(KC):
                            last = pe.matmul(q_bank[p.slot][j][:, 0:GT], m["wq"][layer][:, c, j * P:(j + 1) * P],
                                             xt[p.slot][:, c, :], start=c == 0, stop=c == KC - 1)
                        last.then_inc(q_ready, 1)

            run_steps(pe, NG, 1, body)

        ended.close()
        sems.clear()


def hold(eng, sem, value, passed):
    if not isinstance(value, int) or value > 0:
        eng.wait_ge(sem, value)
        eng.sem_inc(passed, 1)


def take(ap, index):
    return ap[index] if isinstance(index, int) else ap[bass.ds(index, 1)].squeeze(0)


def attention_phase(nc, m, layer, x_in, x_out, context, mask, q_split, k_split):
    tag = f"_a{layer}"
    with ExitStack() as ctx:
        sems = Semaphores(nc, ctx)
        def sb(name, shape, dt):
            return ctx.enter_context(nc.sbuf_tensor(name + tag, shape, dt))

        def sem(name):
            return sems.new(name + tag)

        def two(make, name, *args):
            return [make(f"{name}{n}", *args) for n in range(2)]

        ctx_in = two(sb, "ctx_in", [CK, CH, D], F32)
        ctx_t = two(sb, "ctx_t", [P, KC, S2], F32)
        k_high = sb("k_high", [P, KC, S2], F16)
        k_low = sb("k_low", [P, KC, S2], F16)
        k_stack = two(sb, "k_stack", [P, NP, S2], F16)
        q_stack = two(sb, "q_stack", [P, NP, 2 * S], F16)
        values = two(sb, "values", [CK, CH, H, QUAD], F32)
        mask_in = two(sb, "mask_in", [S, S2], I32)
        mask_f = sb("mask_f", [S, S2], F32)
        seen = sb("seen", [S, 2], F32)
        mask_add = sb("mask_add", [S, S2], F32)
        mask_b = sb("mask_b", [S, S2], BF16)
        mask_t = two(sb, "mask_t", [CK, CH, S], BF16)
        masked_scores = sb("masked_scores", [S, 2, S2], BF16)
        row_max = sb("row_max", [S, H], F32)
        max_parts = sb("max_parts", [S, 2 * H], F16)
        max_t = sb("max_t", [2 * H, S], F16)
        probs = sb("probs", [CK, CH, GT], F32)
        heads_t = sb("heads_t", [P, GT], F32)
        inverse = sb("inverse", [S, H], F32)
        heads_q = sb("heads_q", [S, H, DK], F32)
        heads_n = sb("heads_n", [P, KC, S], F32)
        x_old = two(sb, "x_old", [S, D], F32)
        attended = sb("attended", [S, D], F32)
        x_new = two(sb, "x_new", [S, D], F32)

        def halves(name):
            return [two(sem, f"{name}_{half}_") for half in ("first", "second")]

        ctx_loaded, q_loaded, k_loaded = two(sem, "ctx_loaded"), halves("q_loaded"), halves("k_loaded")
        mask_loaded, max_loaded, x_loaded = two(sem, "mask_loaded"), two(sem, "max_loaded"), two(sem, "x_loaded")
        k_stored, x_stored = sem("k_stored"), two(sem, "x_stored")
        stacks_set = sem("stacks_set")
        ctx_turned, ctx_copied = sem("ctx_turned"), sem("ctx_copied")
        k_made, k_high_ready, k_low_ready = sem("k_made"), sem("k_high_ready"), sem("k_low_ready")
        v_made, v_ready = sem("v_made"), sem("v_ready")
        mask_step, mask_made, mask_turned, mask_ready = (sem("mask_step"), sem("mask_made"), sem("mask_turned"),
                                                         sem("mask_ready"))
        rows_scored, rows_maxed = sem("rows_scored"), sem("rows_maxed")
        parts_ready, max_turned, max_ready = sem("parts_ready"), sem("max_turned"), sem("max_ready")
        scored, exped, weighted = sem("scored"), sem("exped"), sem("weighted")
        heads_ready, heads_turned, inverted, normed = (sem("heads_ready"), sem("heads_turned"), sem("inverted"),
                                                       sem("normed"))
        turned_back, back_ready = sem("turned_back"), sem("back_ready")
        projected, biased, added = sem("projected"), sem("biased"), sem("added")
        passed = sem("passed")
        ended = ExitStack()
        block = ended.enter_context(nc.Block())

        row_bank = m["bank"][0:2]
        score_bank = m["bank"][2:5]
        head_bank = m["bank"][5]
        bank_a = m["bank"][6]
        bank_b = m["bank"][7]
        prep_bank = (bank_a, bank_b)
        max_t_ps = row_bank[0][:, :].bitcast(F16)[0:2 * H, 0:S]
        mask_t_ps = bank_b[:, :].bitcast(BF16)[0:CK, 0:CH * S]
        masks = B if layer else 1
        HALF_UNITS, HALF_PAIRS = UNITS // 2, NP // 2

        ctx_rows = context.rearrange("b (c p) d -> b p c d", p=CK)
        mask_rows = mask if layer else mask[0]
        q_rows = q_split.rearrange("e g (r p) (b t) -> e b (g r) p t", p=NP, t=S)
        k_rows = k_split.rearrange("s e g (r p) k -> s (e g r) p k", p=NP)
        k_save = k_split.rearrange("s e g p k -> s g p e k")
        SIDE = STACK // 2

        def load_queries(p, half):
            pairs = slice(HALF_PAIRS * half, HALF_PAIRS * (half + 1))
            for e in range(2):
                dst = q_stack[p.slot][SIDE * e:SIDE * (e + 1), pairs, e * S:(e + 1) * S]
                nc.sync.dma_start(dst, take(q_rows[e], p.value)[:, pairs, :]).then_inc(q_loaded[half][p.slot], 16)

        def load_keys(p, half):
            pairs = slice(HALF_PAIRS * half, HALF_PAIRS * (half + 1))
            nc.gpsimd.dma_start(k_stack[p.slot][0:STACK, pairs, :],
                                k_rows[p.slot][:, pairs, :]).then_inc(k_loaded[half][p.slot], 16)

        @block.sync
        def _(sp):
            def body(s):
                p, x, d, e = s.back(1), s.back(2), s.back(3), s.back(4)
                if e.exists(B):
                    wait(sp, added, e.back(2).value + 1 if e.back(2).exists(B) else 0)
                    sp.dma_start(x_old[e.slot][:, :], take(x_in, e.value)).then_inc(x_loaded[e.slot], 16)
                if s.exists(B):
                    wait(sp, ctx_turned, KC * (s.back(2).value + 1) if s.back(2).exists(B) else 0)
                    sp.dma_start(ctx_in[s.slot][:, :, :], take(ctx_rows, s.value)).then_inc(ctx_loaded[s.slot], 16)
                if p.exists(masks):
                    wait(sp, mask_step, 3 * (p.back(2).value + 1) if p.back(2).exists(masks) else 0)
                    sp.dma_start(mask_in[p.slot][:, :], take(mask_rows, p.value)).then_inc(mask_loaded[p.slot], 16)
                if p.exists(B):
                    for half in range(2):
                        hold(sp, k_loaded[half][p.slot], 16 * p.pair, passed)
                    for g, (tile, ready) in enumerate(((k_high, k_high_ready), (k_low, k_low_ready),
                                                       (k_high, k_high_ready))):
                        sp.wait_ge(ready, 2 * (p.value + 1))
                        sp.dma_start(k_save[p.slot, g], tile[:, :, :]).then_inc(k_stored, 16)
                    if isinstance(p.value, int) and p.value == 0:
                        sp.wait_ge(stacks_set, 2)
                    hold(sp, scored, UNITS * d.value + HALF_UNITS if d.exists(B) else 0, passed)
                    load_queries(p, 0)
                if x.exists(B):
                    sp.wait_ge(max_ready, x.value + 1)
                    dst = q_stack[x.slot][STACK:ROWS, :, :].rearrange("w p t -> w (p t)")
                    sp.dma_start(dst, max_t[:, :]).then_inc(max_loaded[x.slot], 16)
                if p.exists(B):
                    hold(sp, scored, UNITS * (d.value + 1) if d.exists(B) else 0, passed)
                    load_queries(p, 1)

            run_steps(sp, B, 4, body, 6)

        @block.gpsimd
        def _(pool):
            def body(s):
                p, d, e = s.back(1), s.back(3), s.back(4)
                if p.exists(B):
                    wait(pool, scored, UNITS * d.value + HALF_UNITS if d.exists(B) else 0)
                    hold(pool, k_stored, 48 * (p.value + 1), passed)
                    load_keys(p, 0)
                if e.exists(B):
                    hold(pool, added, e.value + 1, passed)
                    pool.dma_start(take(x_out, e.value), x_new[e.slot][:, :]).then_inc(x_stored[e.slot], 16)
                if p.exists(B):
                    hold(pool, scored, UNITS * (d.value + 1) if d.exists(B) else 0, passed)
                    load_keys(p, 1)

            run_steps(pool, B, 4, body, 6)
            for n in range(2):
                pool.wait_ge(x_stored[n], 16 * B // 2)

        @block.tensor
        def _(pe):
            ident, ident_h, ident_b = m["ident"], m["ident_h"], m["ident_b"]

            def turn_context(s, c):
                p, x, e = s.back(1), s.back(2), s.back(4)
                if c == 0:
                    pe.wait_ge(ctx_loaded[s.slot], 16 * (s.pair + 1))
                if c == 0 and x.exists(B):
                    pe.wait_ge(v_ready, CH * (x.value + 1))
                elif c == 1 and x.exists(masks):
                    pe.wait_ge(mask_ready, x.value + 1)
                elif c == 1 and e.exists(B):
                    pe.wait_ge(biased, e.value + 1)
                elif p.exists(B):
                    pe.wait_ge(k_low_ready, KC * p.value + c + 1)
                for k in range(CH):
                    last = pe.transpose(prep_bank[c][:, k * CK:(k + 1) * CK],
                                        ctx_in[s.slot][:, k, c * P:(c + 1) * P], ident[0:CK, 0:CK])
                last.then_inc(ctx_turned, 1)

            def make_keys(s, j):
                pe.wait_ge(ctx_copied, KC * (s.value + 1))
                for c in range(KC):
                    last = pe.matmul(prep_bank[j][:, 0:S2], m["wk"][layer][:, c, j * P:(j + 1) * P],
                                     ctx_t[s.slot][:, c, :], start=c == 0, stop=c == KC - 1)
                last.then_inc(k_made, 1)

            def make_values(x, p, k):
                if k:
                    pe.wait_ge(v_ready, CH * x.value + k)
                elif p.exists(B):
                    pe.wait_ge(k_low_ready, KC * p.value + 1)
                else:
                    wait(pe, v_ready, CH * x.value)
                for c in range(KC):
                    last = pe.matmul(bank_a[0:CK, 0:D], ctx_t[x.slot][:, c, k * CK:(k + 1) * CK],
                                     m["wv"][layer][:, c, :], start=c == 0, stop=c == KC - 1)
                last.then_inc(v_made, 1)

            def turn_mask(x, p, e):
                pe.wait_ge(mask_step, 3 * (x.value + 1))
                if e.exists(B):
                    pe.wait_ge(biased, e.value + 1)
                elif p.exists(B):
                    pe.wait_ge(k_low_ready, KC * (p.value + 1))
                for k in range(CH):
                    last = pe.transpose(mask_t_ps[:, k * S:(k + 1) * S], mask_b[:, k * CK:(k + 1) * CK],
                                        ident_b[0:S, 0:S])
                last.then_inc(mask_turned, 1)

            def score_rows(x, h):
                if h % (H // 2) == 0:
                    half = h // (H // 2)
                    pe.wait_ge(q_loaded[half][x.slot], 32 * (x.pair + 1))
                    pe.wait_ge(k_loaded[half][x.slot], 16 * (x.pair + 1))
                if h == 0 and isinstance(x.value, int) and x.value == 0:
                    pe.wait_ge(stacks_set, 6)
                if h == 0:
                    wait(pe, max_ready, x.value)
                elif h == 1:
                    wait(pe, rows_maxed, H * x.value)
                else:
                    pe.wait_ge(rows_maxed, H * x.value + h - 1)
                e = h % 2
                pe.matmul(row_bank[h % 2][0:S, 0:S2], q_stack[x.slot][0:STACK, h // 2, e * S:(e + 1) * S],
                          k_stack[x.slot][0:STACK, h // 2, :], start=True, stop=True).then_inc(rows_scored, 1)

            def turn_maxima(x):
                pe.wait_ge(parts_ready, 2 * (x.value + 1))
                pe.transpose(max_t_ps, max_parts[:, :], ident_h[0:S, 0:S]).then_inc(max_turned, 1)

            def score_unit(d, i):
                if i == 0:
                    pe.wait_ge(max_loaded[d.slot], 16 * (d.pair + 1))
                    if layer:
                        pe.wait_ge(mask_ready, d.value + 1)
                    elif isinstance(d.value, int) and d.value == 0:
                        pe.wait_ge(mask_ready, 1)
                wait(pe, exped, UNITS * d.value + i - 2)
                t, k = divmod(i, CH)
                bank = score_bank[i % 3]
                mask_cols = mask_t[d.slot if layer else 0][:, k, :]
                pe.matmul(bank[0:CK, 0:GT], ident_b[0:CK, 0:CK], mask_cols.unsqueeze(1).to_broadcast([CK, 4, S]),
                          start=True, stop=True)
                for half in range(2):
                    last = pe.matmul(bank[0:CK, half * 2 * S:(half + 1) * 2 * S],
                                     k_stack[d.slot][0:ROWS, 2 * t + half, k * CK:(k + 1) * CK],
                                     q_stack[d.slot][0:ROWS, 2 * t + half, :], start=False, stop=True,
                                     skip_group_check=True)
                last.then_inc(scored, 1)

            def weigh_unit(d, i):
                t, k = divmod(i, CH)
                if i == 0:
                    pe.wait_ge(v_ready, CH * (d.value + 1))
                    wait(pe, heads_ready, d.value)
                pe.wait_ge(exped, UNITS * d.value + i + 1)
                for j in range(4):
                    last = pe.matmul(head_bank[QUAD * j:QUAD * (j + 1), t * S:(t + 1) * S],
                                     values[d.slot][:, k, 4 * t + j, :], probs[:, k, j * S:(j + 1) * S],
                                     start=k == 0, stop=k == CH - 1, tile_position=(0, QUAD * j))
                last.then_inc(weighted, 1)

            def turn_heads(e, p):
                pe.wait_ge(heads_ready, e.value + 1)
                if p.exists(B):
                    pe.wait_ge(k_low_ready, KC * (p.value + 1))
                else:
                    wait(pe, biased, e.value)
                for t in range(NT):
                    last = pe.transpose(bank_b[0:S, t * P:(t + 1) * P], heads_t[:, t * S:(t + 1) * S], ident[:, :])
                last.then_inc(heads_turned, 1)

            def turn_heads_back(e):
                pe.wait_ge(normed, e.value + 1)
                for c in range(KC):
                    last = pe.transpose(bank_b[:, c * S:(c + 1) * S],
                                        heads_q[:, :, :].rearrange("q h r -> q (h r)")[:, c * P:(c + 1) * P],
                                        ident[0:S, 0:S])
                last.then_inc(turned_back, 1)

            def project(e):
                pe.wait_ge(back_ready, e.value + 1)
                for c in range(KC):
                    last = pe.matmul(bank_b[0:S, 0:D], heads_n[:, c, :], m["wo"][layer][:, c, :],
                                     start=c == 0, stop=c == KC - 1)
                last.then_inc(projected, 1)

            def body(s):
                p, x, d, e = (s.back(n) for n in range(1, 5))
                for i in range(UNITS):
                    if d.exists(B):
                        score_unit(d, i)
                    if x.exists(B) and i < H // 2:
                        score_rows(x, 2 * i)
                    if d.exists(B) and i >= 2:
                        weigh_unit(d, i - 2)
                    if x.exists(B) and i < H // 2:
                        score_rows(x, 2 * i + 1)
                    if e.exists(B):
                        if i == 1:
                            turn_heads(e, p)
                        if i == 3:
                            turn_heads_back(e)
                        if i == 5:
                            project(e)
                    if x.exists(B) and i in (2, 4, 6):
                        make_values(x, p, i // 2 - 1)
                    if x.exists(masks) and i == 7:
                        turn_mask(x, p, e)
                    if s.exists(B) and i in (8, 9):
                        turn_context(s, i - 8)
                    if x.exists(B) and i == 9:
                        turn_maxima(x)
                    if s.exists(B) and i in (10, 11):
                        make_keys(s, i - 10)
                if d.exists(B):
                    weigh_unit(d, UNITS - 2)
                    weigh_unit(d, UNITS - 1)

            run_steps(pe, B, 4, body, 6)

        @block.scalar
        def _(act):
            def body(s):
                p, x, d, e = (s.back(n) for n in range(1, 5))
                if e.exists(B):
                    act.wait_ge(weighted, UNITS * (e.value + 1))
                    wait(act, heads_turned, e.value)
                    act.activation(heads_t[:, :], head_bank[:, 0:GT], ACT.Copy).then_inc(heads_ready, 1)
                for i in range(UNITS):
                    if d.exists(B):
                        act.wait_ge(scored, UNITS * d.value + i + 1)
                        wait(act, weighted, UNITS * d.value + i - 2)
                        act.activation(probs[:, i % CH, :], score_bank[i % 3][0:CK, 0:GT], ACT.Exp,
                                       scale=DK ** -0.5).then_inc(exped, 1)
                    if e.exists(B) and i == 3:
                        act.wait_ge(turned_back, e.value + 1)
                        wait(act, projected, e.value)
                        act.activation(heads_n[:, :, :], bank_b[:, 0:KC * S].rearrange("p (c t) -> p c t", c=KC),
                                       ACT.Copy).then_inc(back_ready, 1)
                    if x.exists(B) and i in (2, 4, 6):
                        k = i // 2 - 1
                        act.wait_ge(v_made, CH * x.value + k + 1)
                        act.activation(values[x.slot][:, k, :, 0:DK],
                                       bank_a[0:CK, 0:D].rearrange("p (h r) -> p h r", r=DK),
                                       ACT.Copy).then_inc(v_ready, 1)
                    if s.exists(B) and i in (8, 9):
                        c = i - 8
                        act.wait_ge(ctx_turned, KC * s.value + c + 1)
                        act.activation(ctx_t[s.slot][:, c, :], prep_bank[c][:, 0:S2], ACT.Copy).then_inc(ctx_copied, 1)
                    if x.exists(B) and i == 9:
                        act.wait_ge(max_turned, x.value + 1)
                        w = x.back(1)
                        if w.exists(B):
                            act.wait_ge(max_loaded[w.slot], 16 * (w.pair + 1))
                        act.activation(max_t[:, :], max_t_ps, ACT.Copy).then_inc(max_ready, 1)
                    if s.exists(B) and i in (10, 11):
                        wait(act, k_stored, 48 * s.value)
                        j = i - 10
                        act.wait_ge(k_made, KC * s.value + j + 1)
                        act.activation(k_high[:, j, :], prep_bank[j][:, 0:S2], ACT.Copy).then_inc(k_high_ready, 1)

            run_steps(act, B, 4, body, 6)

        @block.vector
        def _(dve):
            for n in range(2):
                dve.memset(q_stack[n][0:STACK, :, :], 0.0).then_inc(stacks_set, 1)
            for n in range(2):
                dve.memset(k_stack[n][STACK:P, :, :], 1.0).then_inc(stacks_set, 1)
                dve.memset(values[n][:, :, :, DK:QUAD], 1.0).then_inc(stacks_set, 1)

            def split_mask(p):
                dve.wait_ge(mask_loaded[p.slot], 16 * (p.pair + 1))
                dve.tensor_scalar(mask_f[:, :], mask_in[p.slot][:, :], 0.0, None, ALU.not_equal).then_inc(mask_step, 1)
                dve.wait_ge(mask_step, 3 * p.value + 1)
                dve.tensor_reduce(seen[:, 0:1], mask_f[:, :], AX.X, ALU.max).then_inc(mask_step, 1)
                dve.wait_ge(mask_step, 3 * p.value + 2)
                dve.tensor_scalar(seen[:, 1:2], seen[:, 0:1], MASKED, None, ALU.mult).then_inc(mask_made, 1)
                dve.wait_ge(mask_made, 2 * p.value + 1)
                dve.tensor_scalar(mask_add[:, :], mask_f[:, :], 1.0, seen[:, 1:2], ALU.subtract,
                                  ALU.mult).then_inc(mask_made, 1)
                wait(dve, mask_turned, p.value)
                dve.wait_ge(mask_made, 2 * p.value + 2)
                dve.tensor_copy(mask_b[:, :], mask_add[:, :]).then_inc(mask_step, 1)

            def copy_mask(x):
                dve.wait_ge(mask_turned, x.value + 1)
                w = x.back(2)
                wait(dve, scored, UNITS * (w.value + 1) if w.exists(B) else 0)
                dve.tensor_copy(mask_t[x.slot][:, :, :],
                                mask_t_ps.rearrange("p (k q) -> p k q", k=CH)).then_inc(mask_ready, 1)

            def reduce_row(x, h):
                hold(dve, rows_scored, H * x.value + h + 1, passed)
                dve.tensor_tensor_reduce(masked_scores[:, h % 2, :], row_bank[h % 2][0:S, 0:S2], mask_add[:, :],
                                         1.0, -LARGEST, ALU.add, ALU.max,
                                         row_max[:, h:h + 1]).then_inc(rows_maxed, 1)

            def split_maxima(x):
                dve.wait_ge(rows_maxed, H * (x.value + 1))
                wait(dve, max_turned, x.value)
                dve.tensor_scalar(max_parts[:, 0:H], row_max[:, :], -1.0, None, ALU.mult).then_inc(parts_ready, 1)
                dve.wait_ge(parts_ready, 2 * x.value + 1)
                dve.scalar_tensor_tensor(out=max_parts[:, H:2 * H], in0=row_max[:, :], scalar=-1.0,
                                         in1=max_parts[:, 0:H], op0=ALU.mult, op1=ALU.subtract).then_inc(parts_ready, 1)

            def normalise(e):
                dve.wait_ge(heads_turned, e.value + 1)
                heads = bank_b[0:S, 0:H * QUAD].rearrange("q (h r) -> q h r", r=QUAD)
                dve.reciprocal(inverse[:, :], heads[:, :, DK]).then_inc(inverted, 1)
                dve.wait_ge(inverted, e.value + 1)
                wait(dve, turned_back, e.value)
                dve.tensor_tensor(heads_q[:, :, :], heads[:, :, 0:DK],
                                  inverse[:, :].unsqueeze(2).to_broadcast([S, H, DK]), ALU.mult).then_inc(normed, 1)

            def add_output(e):
                dve.wait_ge(projected, e.value + 1)
                dve.tensor_tensor(attended[:, :], bank_b[0:S, 0:D], m["bo"][layer][:, :], ALU.add).then_inc(biased, 1)
                dve.wait_ge(biased, e.value + 1)
                dve.wait_ge(x_loaded[e.slot], 16 * (e.pair + 1))
                wait(dve, x_stored[e.slot], 16 * e.pair)
                dve.scalar_tensor_tensor(out=x_new[e.slot][:, :], in0=attended[:, :],
                                         scalar=m["gate"][0:S, layer:layer + 1], in1=x_old[e.slot][:, :],
                                         op0=ALU.mult, op1=ALU.add).then_inc(added, 1)

            def low_keys(s, j):
                wait(dve, k_stored, 48 * s.value)
                dve.wait_ge(k_high_ready, KC * s.value + j + 1)
                dve.tensor_tensor(k_low[:, j, :], prep_bank[j][:, 0:S2], k_high[:, j, :],
                                  ALU.subtract).then_inc(k_low_ready, 1)

            def body(s):
                p, x, e = s.back(1), s.back(2), s.back(4)
                for i in range(H // 2):
                    if x.exists(B):
                        reduce_row(x, 2 * i)
                        reduce_row(x, 2 * i + 1)
                    if e.exists(B) and i == 1:
                        normalise(e)
                    if e.exists(B) and i == 5:
                        add_output(e)
                if x.exists(masks):
                    copy_mask(x)
                if x.exists(B):
                    split_maxima(x)
                if p.exists(masks):
                    split_mask(p)
                if s.exists(B):
                    for j in range(KC):
                        low_keys(s, j)

            run_steps(dve, B, 4, body, 6)

        ended.close()
        sems.clear()


def ffn_phase(nc, m, a, x_in, x_out):
    with ExitStack() as ctx:
        sems = Semaphores(nc, ctx)
        def sb(name, shape, dt):
            return ctx.enter_context(nc.sbuf_tensor(name + "_f", shape, dt))

        def sem(name):
            return sems.new(name + "_f")

        def two(make, name, *args):
            return [make(f"{name}{n}", *args) for n in range(2)]

        k_in = [sb("k0_in", [P, 2 * KC, F], U8), sb("k1_in", [P, FC, F], U8), sb("k2_in", [P, FC, D], U8)]
        w0_parts = sb("w0_parts", [P, 2 * KC, F], F16)
        w = [sb("w0", [P, KC, F], F16), sb("w1", [P, FC, F], F16), sb("w2", [P, FC, D], F16)]
        factors = sb("factors", [P, 4], F32)
        xg = two(sb, "xg", [S, G, D], F32)
        stats = sb("stats", [S, G, 6], F32)
        mean_var = sb("mean_var", [S, G, 2], F32)
        dev = sb("dev", [S, G], F32)
        scale = sb("scale", [S, G], F32)
        xn = sb("xn", [S, G, D], F32)
        xh, xl = two(sb, "xh", [P, KC, GT], F16), two(sb, "xl", [P, KC, GT], F16)
        h = [[sb(f"h{n}{part}", [P, FC, GT], F16) for part in "hl"] for n in range(2)]
        y = two(sb, "y", [S, G, D], F32)

        k_loaded, w_step, w_ready = sem("k_loaded"), sem("w_step"), sem("w_ready")
        x_loaded, stored = two(sem, "x_loaded"), two(sem, "stored")
        stats_ready, var_ready, dev_ready, scaled = sem("stats_ready"), sem("var_ready"), sem("dev_ready"), sem("scaled")
        xn_ready, turned, xh_ready, xl_ready = sem("xn_ready"), sem("turned"), sem("xh_ready"), sem("xl_ready")
        z_made, h_high_ready, h_low_ready = sem("z_made"), sem("h_high_ready"), sem("h_low_ready")
        y_made, y_ready = sem("y_made"), sem("y_ready")
        passed = sem("passed")
        ended = ExitStack()
        block = ended.enter_context(nc.Block())

        z_bank, y_bank, turn_bank = m["bank"][0:4], m["bank"][4:6], m["bank"][6:8]
        x_rows = x_in.rearrange("(g b) s d -> g s b d", b=G)
        out_rows = x_out.rearrange("(g b) s d -> g s b d", b=G)
        ZS = 2 * FC

        @block.sync
        def _(sp):
            def body(s):
                if s.exists(NG):
                    wait(sp, y_ready, G * (s.back(2).value + 1) if s.back(2).exists(NG) else 0)
                    sp.dma_start(xg[s.slot][:, :, :], take(x_rows, s.value)).then_inc(x_loaded[s.slot], 16)
                if isinstance(s.value, int) and s.value == 0:
                    for n in range(3):
                        sp.dma_start(k_in[n][:, :, :], a[f"L0_ffn_k{n}"].rearrange("(c p) n -> p c n", p=P)).then_inc(k_loaded, 16)

            run_steps(sp, NG, 1, body)

        @block.gpsimd
        def _(pool):
            def body(s):
                p = s.back(1)
                if p.exists(NG):
                    hold(pool, y_ready, G * (p.value + 1), passed)
                    pool.dma_start(take(out_rows, p.value), y[p.slot][:, :, :]).then_inc(stored[p.slot], 16)

            run_steps(pool, NG, 1, body)
            for n in range(2):
                pool.wait_ge(stored[n], 16 * NG // 2)

        @block.vector
        def _(dve):
            def weights():
                dve.wait_ge(k_loaded, 48)
                for n, size in enumerate((1.0, 2.0 ** -5)):
                    dve.tensor_scalar(factors[:, 2 * n:2 * n + 1], m["sign"][:, n:n + 1], 2.0 * size, None,
                                      ALU.mult).then_inc(w_step, 1)
                    dve.tensor_scalar(factors[:, 2 * n + 1:2 * n + 2], m["sign"][:, n:n + 1], size, None,
                                      ALU.mult).then_inc(w_step, 1)
                dve.wait_ge(w_step, 4)
                dve.tensor_scalar(w0_parts[:, :, :], k_in[0][:, :, :], factors[:, 0:1], factors[:, 1:2],
                                  ALU.mult, ALU.subtract).then_inc(w_step, 1)
                dve.tensor_scalar(w[1][:, :, :], k_in[1][:, :, :], factors[:, 2:3], factors[:, 3:4],
                                  ALU.mult, ALU.subtract).then_inc(w_ready, 1)
                dve.tensor_scalar(w[2][:, :, :], k_in[2][:, :, :], 2.0, -1.0, ALU.mult, ALU.add).then_inc(w_ready, 1)
                dve.wait_ge(w_step, 5)
                dve.tensor_tensor(w[0][:, :, :], w0_parts[:, 0:KC, :], w0_parts[:, KC:2 * KC, :],
                                  ALU.subtract).then_inc(w_ready, 1)

            def normalise(s):
                dve.wait_ge(x_loaded[s.slot], 16 * (s.pair + 1))
                for b in range(G):
                    last = dve.bn_stats(stats[:, b, :], xg[s.slot][:, b, :])
                last.then_inc(stats_ready, 1)
                hold(dve, stats_ready, s.value + 1, passed)
                for b in range(G):
                    last = dve.bn_aggr(mean_var[:, b, :], stats[:, b, :])
                last.then_inc(var_ready, 1)

            def normalise_end(s):
                dve.wait_ge(dev_ready, s.value + 1)
                dve.reciprocal(scale[:, :], dev[:, :]).then_inc(scaled, 1)
                dve.wait_ge(scaled, s.value + 1)
                wait(dve, turned, KC * s.value)
                for b in range(G):
                    last = dve.tensor_scalar(xn[:, b, :], xg[s.slot][:, b, :], mean_var[:, b, 0:1],
                                             scale[:, b:b + 1], ALU.subtract, ALU.mult)
                last.then_inc(xn_ready, 1)

            def low_rows(s):
                for c in range(KC):
                    dve.wait_ge(xh_ready, KC * s.value + c + 1)
                    dve.tensor_tensor(xl[s.slot][:, c, :], turn_bank[c][:, 0:GT], xh[s.slot][:, c, :],
                                      ALU.subtract).then_inc(xl_ready, 1)

            def low_hidden(p, z):
                dve.wait_ge(h_high_ready, ZS * p.value + z + 1)
                layer, j = divmod(z, FC)
                high, low = h[layer]
                dve.scalar_tensor_tensor(out=low[:, j, :], in0=z_bank[z % 4][:, 0:GT], scalar=0.0,
                                         in1=high[:, j, :], op0=ALU.max, op1=ALU.subtract).then_inc(h_low_ready, 1)

            def add(p, b):
                dve.wait_ge(y_made, G * p.value + b + 1)
                if b == 0:
                    wait(dve, stored[p.slot], 16 * p.pair)
                dve.scalar_tensor_tensor(out=y[p.slot][:, b, :], in0=y_bank[b % 2][0:S, 0:D],
                                         scalar=m["ffn_scale"][0:S, 0:1], in1=xg[p.slot][:, b, :],
                                         op0=ALU.mult, op1=ALU.add).then_inc(y_ready, 1)

            def body(s):
                p = s.back(1)
                for z in range(ZS):
                    if p.exists(NG):
                        low_hidden(p, z)
                    if s.exists(NG):
                        if z == 4:
                            normalise(s)
                        if z == 6:
                            normalise_end(s)
                        if z == 12:
                            low_rows(s)
                if p.exists(NG):
                    for b in range(G):
                        add(p, b)

            weights()
            run_steps(dve, NG, 1, body)

        @block.scalar
        def _(act):
            def body(s):
                p = s.back(1)
                for z in range(ZS):
                    if p.exists(NG):
                        act.wait_ge(z_made, ZS * p.value + z + 1)
                        layer, j = divmod(z, FC)
                        act.activation(h[layer][0][:, j, :], z_bank[z % 4][:, 0:GT], ACT.Relu).then_inc(h_high_ready, 1)
                    if s.exists(NG):
                        if z == 5:
                            act.wait_ge(var_ready, s.value + 1)
                            act.activation(dev[:, :], mean_var[:, :, 1], ACT.Sqrt, bias=m["eps"][0:S, :]).then_inc(dev_ready, 1)
                        if z == 12:
                            for c in range(KC):
                                act.wait_ge(turned, KC * s.value + c + 1)
                                act.activation(xh[s.slot][:, c, :], turn_bank[c][:, 0:GT], ACT.Copy).then_inc(xh_ready, 1)

            run_steps(act, NG, 1, body)

        @block.tensor
        def _(pe):
            def turn(s):
                pe.wait_ge(xn_ready, s.value + 1)
                wait(pe, xl_ready, KC * s.value)
                for c in range(KC):
                    for b in range(G):
                        last = pe.transpose(turn_bank[c][:, b * S:(b + 1) * S], xn[:, b, c * P:(c + 1) * P],
                                            m["ident"][0:S, 0:S])
                    last.then_inc(turned, 1)

            def hidden(p, z):
                layer, j = divmod(z, FC)
                wait(pe, h_low_ready, ZS * p.value + z - 3)
                if z == 0:
                    pe.wait_ge(xl_ready, KC * (p.value + 1))
                parts = h[0] if layer else [xh[p.slot], xl[p.slot]]
                chunks = FC if layer else KC
                for c in range(chunks):
                    if z == FC:
                        pe.wait_ge(h_low_ready, ZS * p.value + c + 1)
                    for n, part in enumerate(parts):
                        last = pe.matmul(z_bank[z % 4][:, 0:GT], w[layer][:, c, j * P:(j + 1) * P], part[:, c, :],
                                         start=c == 0 and n == 0, stop=c == chunks - 1 and n == 1)
                last.then_inc(z_made, 1)

            def output(p, b):
                wait(pe, y_ready, G * p.value + b - 1)
                for c in range(FC):
                    if b == 0:
                        pe.wait_ge(h_low_ready, ZS * p.value + FC + c + 1)
                    for n, part in enumerate(h[1]):
                        last = pe.matmul(y_bank[b % 2][0:S, 0:D], part[:, c, b * S:(b + 1) * S], w[2][:, c, :],
                                         start=c == 0 and n == 0, stop=c == FC - 1 and n == 1)
                last.then_inc(y_made, 1)

            def body(s):
                p = s.back(1)
                for z in range(ZS):
                    if p.exists(NG):
                        hidden(p, z)
                    if s.exists(NG) and z == 11:
                        turn(s)
                if p.exists(NG):
                    for b in range(G):
                        output(p, b)

            pe.wait_ge(w_ready, 3)
            run_steps(pe, NG, 1, body)

        ended.close()
        sems.clear()


def moe_phases(nc, m, a, x_in, x_normed, expert_in, expert_out, out):
    with ExitStack() as ctx:
        def sb(name, shape, dt):
            return ctx.enter_context(nc.sbuf_tensor(name + "_r", shape, dt))

        route = {
            "logits": sb("logits", [S, B, E], F32),
            "put": sb("put", [S, B], U32),
            "get": sb("get", [S, B], U32),
            "weight": sb("weight", [S, B], F32),
        }
        logits_phase(nc, m, a, x_in, x_normed, route)
        ranks_phase(nc, m, route)
        dispatch_phase(nc, route, x_normed, expert_in)
        experts_phase(nc, m, a, expert_in, expert_out)
        combine_phase(nc, route, x_in, expert_out, out)


def logits_phase(nc, m, a, x_in, x_normed, route):
    with ExitStack() as ctx:
        sems = Semaphores(nc, ctx)
        def sb(name, shape, dt):
            return ctx.enter_context(nc.sbuf_tensor(name + "_l", shape, dt))

        def sem(name):
            return sems.new(name + "_l")

        def two(make, name, *args):
            return [make(f"{name}{n}", *args) for n in range(2)]

        wr = sb("wr", [P, KC, E], F32)
        xg = two(sb, "xg", [S, G, D], F32)
        xn = two(sb, "xn", [S, G, D], F32)
        stats = sb("stats", [S, G, 6], F32)
        mean_var = sb("mean_var", [S, G, 2], F32)
        dev = sb("dev", [S, G], F32)
        scale = sb("scale", [S, G], F32)
        xt = two(sb, "xt", [P, KC, GT], F32)
        wr_loaded, x_loaded = sem("wr_loaded"), two(sem, "x_loaded")
        stats_ready, var_ready, dev_ready, scaled = sem("stats_ready"), sem("var_ready"), sem("dev_ready"), sem("scaled")
        xn_ready, stored = sem("xn_ready"), two(sem, "stored")
        turned, xt_ready, made, kept = sem("turned"), sem("xt_ready"), sem("made"), sem("kept")
        passed = sem("passed")
        ended = ExitStack()
        block = ended.enter_context(nc.Block())
        turn_bank = [m["bank"][0:2], m["bank"][2:4]]
        logit_bank = m["bank"][4:6]
        x_rows = x_in.rearrange("(g b) s d -> g s b d", b=G)
        normed_rows = x_normed.rearrange("(g b) s d -> g s b d", b=G)

        @block.sync
        def _(sp):
            sp.dma_start(wr[:, :, :], a["L1_ffn_Wr"].rearrange("(c p) e -> p c e", p=P)).then_inc(wr_loaded, 16)

            def body(s):
                if s.exists(NG):
                    wait(sp, xn_ready, s.back(2).value + 1 if s.back(2).exists(NG) else 0)
                    sp.dma_start(xg[s.slot][:, :, :], take(x_rows, s.value)).then_inc(x_loaded[s.slot], 16)
                p = s.back(1)
                if p.exists(NG):
                    sp.wait_ge(xn_ready, p.value + 1)
                    sp.dma_start(take(normed_rows, p.value), xn[p.slot][:, :, :]).then_inc(stored[p.slot], 16)

            run_steps(sp, NG, 1, body)
            for n in range(2):
                sp.wait_ge(stored[n], 16 * NG // 2)

        @block.tensor
        def _(pe):
            pe.wait_ge(wr_loaded, 16)

            def body(s):
                p = s.back(1)
                if s.exists(NG):
                    pe.wait_ge(xn_ready, s.value + 1)
                    wait(pe, xt_ready, KC * (s.back(2).value + 1) if s.back(2).exists(NG) else 0)
                    for c in range(KC):
                        for b in range(G):
                            last = pe.transpose(turn_bank[s.slot][c][:, b * S:(b + 1) * S],
                                                xn[s.slot][:, b, c * P:(c + 1) * P], m["ident"][0:S, 0:S])
                        last.then_inc(turned, 1)
                if p.exists(NG):
                    pe.wait_ge(xt_ready, KC * (p.value + 1))
                    wait(pe, kept, p.back(2).value + 1 if p.back(2).exists(NG) else 0)
                    for b in range(G):
                        for c in range(KC):
                            last = pe.matmul(logit_bank[p.slot][0:S, b * E:(b + 1) * E], xt[p.slot][:, c, b * S:(b + 1) * S],
                                             wr[:, c, :], start=c == 0, stop=c == KC - 1)
                    last.then_inc(made, 1)

            run_steps(pe, NG, 1, body)

        @block.scalar
        def _(act):
            def body(s):
                if s.exists(NG):
                    act.wait_ge(var_ready, s.value + 1)
                    act.activation(dev[:, :], mean_var[:, :, 1], ACT.Sqrt, bias=m["eps"][0:S, :]).then_inc(dev_ready, 1)
                    wait(act, made, s.back(2).value + 1 if s.back(2).exists(NG) else 0)
                    for c in range(KC):
                        act.wait_ge(turned, KC * s.value + c + 1)
                        act.activation(xt[s.slot][:, c, :], turn_bank[s.slot][c][:, 0:GT], ACT.Copy).then_inc(xt_ready, 1)

            run_steps(act, NG, 1, body)

        @block.vector
        def _(dve):
            def body(s):
                if s.exists(NG):
                    dve.wait_ge(x_loaded[s.slot], 16 * (s.pair + 1))
                    for b in range(G):
                        last = dve.bn_stats(stats[:, b, :], xg[s.slot][:, b, :])
                    last.then_inc(stats_ready, 1)
                    hold(dve, stats_ready, s.value + 1, passed)
                    for b in range(G):
                        last = dve.bn_aggr(mean_var[:, b, :], stats[:, b, :])
                    last.then_inc(var_ready, 1)
                    dve.wait_ge(dev_ready, s.value + 1)
                    dve.reciprocal(scale[:, :], dev[:, :]).then_inc(scaled, 1)
                    dve.wait_ge(scaled, s.value + 1)
                    wait(dve, turned, KC * (s.back(2).value + 1) if s.back(2).exists(NG) else 0)
                    wait(dve, stored[s.slot], 16 * s.pair)
                    for b in range(G):
                        last = dve.tensor_scalar(xn[s.slot][:, b, :], xg[s.slot][:, b, :], mean_var[:, b, 0:1],
                                                 scale[:, b:b + 1], ALU.subtract, ALU.mult)
                    last.then_inc(xn_ready, 1)
                p = s.back(1)
                if p.exists(NG):
                    dve.wait_ge(made, p.value + 1)
                    dst = route["logits"][:, :, :].rearrange("s (g b) e -> s g (b e)", b=G)
                    at = dst[:, p.value, :] if isinstance(p.value, int) else dst[:, bass.ds(p.value, 1), :].squeeze(1)
                    dve.tensor_scalar(at, logit_bank[p.slot][0:S, 0:G * E], 1.0, None, ALU.mult).then_inc(kept, 1)

            run_steps(dve, NG, 1, body)

        ended.close()
        sems.clear()


def ranks_phase(nc, m, route):
    with ExitStack() as ctx:
        sems = Semaphores(nc, ctx)
        def sb(name, shape=(S, B, E), dt=F32):
            return ctx.enter_context(nc.sbuf_tensor(name + "_k", list(shape), dt))

        def sem(name):
            return sems.new(name + "_k")

        before = sb("before", (S, S))
        ones = sb("ones", (S, S))
        number = sb("number")
        top, first, prob, rank, kept, base = (sb(n, (S, B)) for n in ("top", "first", "prob", "rank", "kept", "base"))
        shifted, power, equal, chosen, counts, total = (sb(n) for n in ("shifted", "power", "equal", "chosen", "counts", "total"))
        sums = [sb(f"sums{n}") for n in range(2)]
        step, made, product, powered = sem("step"), sem("made"), sem("product"), sem("powered")
        passed = sem("passed")
        ended = ExitStack()
        block = ended.enter_context(nc.Block())
        rank_bank, count_bank = m["bank"][0], m["bank"][1]

        @block.gpsimd
        def _(pool):
            pool.memset(before[:, :], 0.0).then_inc(made, 1)
            pool.memset(ones[:, :], 1.0).then_inc(made, 1)
            pool.wait_ge(made, 2)
            pool.affine_select(out=before[:, :], in_=before[:, :], compare_op=ALU.is_ge, fill=1.0, base=0,
                               pattern=[[-1, S]], channel_multiplier=1).then_inc(made, 1)
            for e in range(E):
                pool.memset(number[:, :, e], float(e - E)).then_inc(made, 1)

        @block.scalar
        def _(act):
            act.wait_ge(step, 2)
            act.activation(power[:, :, :], shifted[:, :, :], ACT.Exp).then_inc(powered, 1)

        @block.tensor
        def _(pe):
            pe.wait_ge(made, 3)
            pe.wait_ge(step, 6)
            pe.matmul(rank_bank[0:S, 0:B * E], before[:, :], chosen[:, :, :].rearrange("s b e -> s (b e)"),
                      start=True, stop=True).then_inc(product, 1)
            pe.matmul(count_bank[0:S, 0:B * E], ones[:, :], chosen[:, :, :].rearrange("s b e -> s (b e)"),
                      start=True, stop=True).then_inc(product, 1)

        @block.vector
        def _(dve):
            done = 0

            def link(ins):
                nonlocal done
                done += 1
                ins.then_inc(step, 1)
                dve.wait_ge(step, done)

            def wide(t):
                return t[:, :].unsqueeze(2).to_broadcast([S, B, E])

            logits = route["logits"]
            link(dve.tensor_reduce(top[:, :], logits[:, :, :], AX.X, ALU.max))
            link(dve.tensor_tensor(shifted[:, :, :], logits[:, :, :], wide(top), ALU.subtract))
            link(dve.tensor_scalar(equal[:, :, :], shifted[:, :, :], 0.0, None, ALU.is_equal))
            dve.wait_ge(made, 3 + E)
            link(dve.tensor_tensor(equal[:, :, :], equal[:, :, :], number[:, :, :], ALU.mult))
            link(dve.tensor_reduce(first[:, :], equal[:, :, :], AX.X, ALU.min))
            link(dve.tensor_tensor(chosen[:, :, :], number[:, :, :], wide(first), ALU.is_equal))
            dve.wait_ge(powered, 1)
            link(dve.tensor_reduce(prob[:, :], power[:, :, :], AX.X, ALU.add))
            link(dve.reciprocal(prob[:, :], prob[:, :]))
            dve.wait_ge(product, 2)
            link(dve.tensor_copy(counts[:, :, :].rearrange("s b e -> s (b e)"), count_bank[0:S, 0:B * E]))
            old = counts
            shift, turn = 1, 0
            while shift < B:
                new = sums[turn]
                link(dve.tensor_copy(new[:, 0:shift, :], old[:, 0:shift, :]))
                link(dve.tensor_tensor(new[:, shift:B, :], old[:, shift:B, :], old[:, 0:B - shift, :], ALU.add))
                old, shift, turn = new, 2 * shift, 1 - turn
            link(dve.tensor_tensor(total[:, :, :], old[:, :, :], counts[:, :, :], ALU.subtract))
            link(dve.tensor_tensor(total[:, :, :].rearrange("s b e -> s (b e)"), rank_bank[0:S, 0:B * E],
                                   total[:, :, :].rearrange("s b e -> s (b e)"), ALU.add))
            link(dve.tensor_tensor(total[:, :, :], total[:, :, :], chosen[:, :, :], ALU.mult))
            link(dve.tensor_reduce(rank[:, :], total[:, :, :], AX.X, ALU.add))
            link(dve.tensor_scalar(kept[:, :], rank[:, :], float(CAP), None, ALU.is_lt))
            link(dve.tensor_scalar(base[:, :], first[:, :], float(CAP), float(E * CAP), ALU.mult, ALU.add))
            link(dve.tensor_scalar(rank[:, :], rank[:, :], float(CAP - 1), None, ALU.min))
            link(dve.tensor_tensor(base[:, :], base[:, :], rank[:, :], ALU.add))
            link(dve.tensor_copy(route["get"][:, :], base[:, :]))
            link(dve.tensor_scalar(rank[:, :], kept[:, :], -float(2 * E * CAP), float(2 * E * CAP), ALU.mult, ALU.add))
            link(dve.tensor_tensor(route["put"][:, :], base[:, :], rank[:, :], ALU.add))
            link(dve.tensor_tensor(prob[:, :], prob[:, :], kept[:, :], ALU.mult))
            link(dve.tensor_scalar(route["weight"][:, :], prob[:, :], m["gate"][0:S, 3:4], None, ALU.mult))

        ended.close()
        sems.clear()


def dispatch_phase(nc, route, x_in, expert_in):
    with ExitStack() as ctx:
        sems = Semaphores(nc, ctx)
        def sem(name):
            return sems.new(name + "_d")

        xg = [ctx.enter_context(nc.sbuf_tensor(f"xg{n}_d", [S, G, D], F32)) for n in range(2)]
        index = [ctx.enter_context(nc.sbuf_tensor(f"index{n}_d", [S, G], U32)) for n in range(2)]
        x_loaded, put = [sem(f"x_loaded{n}") for n in range(2)], [sem(f"put{n}") for n in range(2)]
        index_ready = sem("index_ready")
        passed = sem("passed")
        ended = ExitStack()
        block = ended.enter_context(nc.Block())
        x_rows = x_in.rearrange("(g b) s d -> g s b d", b=G)

        @block.sync
        def _(sp):
            def body(s):
                if s.exists(NG):
                    wait(sp, put[s.slot], 16 * G * s.pair)
                    sp.dma_start(xg[s.slot][:, :, :], take(x_rows, s.value)).then_inc(x_loaded[s.slot], 16)

            run_steps(sp, NG, 0, body)

        @block.vector
        def _(dve):
            def body(s):
                wait(dve, put[s.slot], 16 * G * s.pair)
                copy_index(dve, index[s.slot], route["put"], s).then_inc(index_ready, 1)

            run_steps(dve, NG, 0, body)

        @block.gpsimd
        def _(pool):
            def body(s):
                pool.wait_ge(x_loaded[s.slot], 16 * (s.pair + 1))
                hold(pool, index_ready, s.value + 1, passed)
                for b in range(G):
                    pool.indirect_dma_start(expert_in[:, :], bass.IndirectOffsetOnAxis(index[s.slot][:, b:b + 1], 0),
                                            xg[s.slot][:, b, :], None, bounds_check=E * CAP - 1,
                                            oob_is_err=False).then_inc(put[s.slot], 16)

            run_steps(pool, NG, 0, body)
            for n in range(2):
                pool.wait_ge(put[n], 16 * G * NG // 2)

        ended.close()
        sems.clear()


def copy_index(dve, slot, table, s):
    groups = table[:, :].rearrange("s (g b) -> s g b", b=G)
    at = groups[:, s.value, :] if isinstance(s.value, int) else groups[:, bass.ds(s.value, 1), :].squeeze(1)
    return dve.tensor_scalar(slot[:, :], at, 0.0, None, ALU.add)


def experts_phase(nc, m, a, expert_in, expert_out):
    with ExitStack() as ctx:
        sems = Semaphores(nc, ctx)
        def sb(name, shape, dt):
            return ctx.enter_context(nc.sbuf_tensor(name + "_e", shape, dt))

        def sem(name):
            return sems.new(name + "_e")

        def two(make, name, *args):
            return [make(f"{name}{n}", *args) for n in range(2)]

        w1 = two(sb, "w1", [P, KC, F], F32)
        w2 = two(sb, "w2", [P, FC, D], F32)
        xg = two(sb, "xg", [S, G, D], F32)
        xt = two(sb, "xt", [P, KC, GT], F32)
        h = sb("h", [P, FC, GT], F32)
        y = two(sb, "y", [S, G, D], F32)
        x_loaded, w_loaded, stored = two(sem, "x_loaded"), two(sem, "w_loaded"), two(sem, "stored")
        turned, xt_ready, z_made = sem("turned"), sem("xt_ready"), sem("z_made")
        h_even_ready, h_odd_ready, y_made = sem("h_even_ready"), sem("h_odd_ready"), sem("y_made")
        y_even_ready, y_odd_ready = sem("y_even_ready"), sem("y_odd_ready")
        passed = sem("passed")
        ended = ExitStack()
        block = ended.enter_context(nc.Block())
        z_bank, y_bank, turn_bank = m["bank"][0:4], m["bank"][4:6], m["bank"][6:8]
        in_rows = expert_in.rearrange("(e t s) d -> e s t d", e=E, s=S)
        out_rows = expert_out.rearrange("(e t s) d -> e s t d", e=E, s=S)
        w1_rows = a["L1_ffn_W1"].rearrange("e (c p) f -> e p c f", p=P)
        w2_rows = a["L1_ffn_W2"].rearrange("e (c p) d -> e p c d", p=P)
        HC, HG = FC // 2, G // 2

        @block.sync
        def _(sp):
            def body(s):
                if s.exists(E):
                    wait(sp, turned, KC * (s.back(2).value + 1) if s.back(2).exists(E) else 0)
                    sp.dma_start(xg[s.slot][:, :, :], take(in_rows, s.value)).then_inc(x_loaded[s.slot], 16)
                    wait(sp, y_made, G * (s.back(2).value + 1) if s.back(2).exists(E) else 0)
                    sp.dma_start(w1[s.slot][:, :, :], take(w1_rows, s.value)).then_inc(w_loaded[s.slot], 16)
                    sp.dma_start(w2[s.slot][:, :, :], take(w2_rows, s.value)).then_inc(w_loaded[s.slot], 16)

            run_steps(sp, E, 1, body)

        @block.gpsimd
        def _(pool):
            def body(s):
                p = s.back(1)
                if p.exists(E):
                    pool.wait_ge(y_even_ready, HG * (p.value + 1))
                    hold(pool, y_odd_ready, HG * (p.value + 1), passed)
                    pool.dma_start(take(out_rows, p.value), y[p.slot][:, :, :]).then_inc(stored[p.slot], 16)

            run_steps(pool, E, 1, body)
            for n in range(2):
                pool.wait_ge(stored[n], 16 * E // 2)

        @block.tensor
        def _(pe):
            def turn(s):
                pe.wait_ge(x_loaded[s.slot], 16 * (s.pair + 1))
                wait(pe, xt_ready, KC * s.value)
                for c in range(KC):
                    for b in range(G):
                        last = pe.transpose(turn_bank[c][:, b * S:(b + 1) * S], xg[s.slot][:, b, c * P:(c + 1) * P],
                                            m["ident"][0:S, 0:S])
                    last.then_inc(turned, 1)

            def body(s):
                p = s.back(1)
                for j in range(FC):
                    if p.exists(E):
                        if j == 0:
                            pe.wait_ge(w_loaded[p.slot], 32 * (p.pair + 1))
                            pe.wait_ge(xt_ready, KC * (p.value + 1))
                        ready = (h_even_ready, h_odd_ready)[j % 2]
                        wait(pe, ready, HC * p.value + j // 2 - 1)
                        for c in range(KC):
                            last = pe.matmul(z_bank[j % 4][:, 0:GT], w1[p.slot][:, c, j * P:(j + 1) * P],
                                             xt[p.slot][:, c, :], start=c == 0, stop=c == KC - 1)
                        last.then_inc(z_made, 1)
                    if s.exists(E) and j == FC - 1:
                        turn(s)
                if p.exists(E):
                    for b in range(G):
                        wait(pe, (y_even_ready, y_odd_ready)[b % 2], HG * p.value + b // 2)
                        for c in range(FC):
                            if b == 0:
                                pe.wait_ge((h_even_ready, h_odd_ready)[c % 2], HC * p.value + c // 2 + 1)
                            last = pe.matmul(y_bank[b % 2][0:S, 0:D], h[:, c, b * S:(b + 1) * S], w2[p.slot][:, c, :],
                                             start=c == 0, stop=c == FC - 1)
                        last.then_inc(y_made, 1)

            run_steps(pe, E, 1, body)

        @block.scalar
        def _(act):
            def body(s):
                p = s.back(1)
                if p.exists(E):
                    wait(act, y_made, G * p.value)
                    for j in range(0, FC, 2):
                        act.wait_ge(z_made, FC * p.value + j + 1)
                        act.activation(h[:, j, :], z_bank[j % 4][:, 0:GT], ACT.Relu).then_inc(h_even_ready, 1)
                if s.exists(E):
                    for c in range(KC):
                        act.wait_ge(turned, KC * s.value + c + 1)
                        act.activation(xt[s.slot][:, c, :], turn_bank[c][:, 0:GT], ACT.Copy).then_inc(xt_ready, 1)
                if p.exists(E):
                    wait(act, stored[p.slot], 16 * p.pair)
                    for b in range(0, G, 2):
                        act.wait_ge(y_made, G * p.value + b + 1)
                        act.activation(y[p.slot][:, b, :], y_bank[0][0:S, 0:D], ACT.Copy).then_inc(y_even_ready, 1)

            run_steps(act, E, 1, body)

        @block.vector
        def _(dve):
            def body(s):
                p = s.back(1)
                if p.exists(E):
                    wait(dve, y_made, G * p.value)
                    for j in range(1, FC, 2):
                        dve.wait_ge(z_made, FC * p.value + j + 1)
                        dve.tensor_scalar(h[:, j, :], z_bank[j % 4][:, 0:GT], 0.0, None, ALU.max).then_inc(h_odd_ready, 1)
                    wait(dve, stored[p.slot], 16 * p.pair)
                    for b in range(1, G, 2):
                        dve.wait_ge(y_made, G * p.value + b + 1)
                        dve.tensor_copy(y[p.slot][:, b, :], y_bank[1][0:S, 0:D]).then_inc(y_odd_ready, 1)

            run_steps(dve, E, 1, body)

        ended.close()
        sems.clear()


def combine_phase(nc, route, x_in, expert_out, out):
    with ExitStack() as ctx:
        sems = Semaphores(nc, ctx)
        def sb(name, shape, dt):
            return ctx.enter_context(nc.sbuf_tensor(name + "_c", shape, dt))

        def sem(name):
            return sems.new(name + "_c")

        def two(make, name, *args):
            return [make(f"{name}{n}", *args) for n in range(2)]

        xg, y, total = (two(sb, name, [S, G, D], F32) for name in ("xg", "y", "total"))
        index = two(sb, "index", [S, G], U32)
        weight = sb("weight", [S, G], F32)
        x_loaded, got, stored = two(sem, "x_loaded"), two(sem, "got"), two(sem, "stored")
        index_ready, weight_ready, added = sem("index_ready"), sem("weight_ready"), sem("added")
        passed = sem("passed")
        ended = ExitStack()
        block = ended.enter_context(nc.Block())
        x_rows = x_in.rearrange("(g b) s d -> g s b d", b=G)
        out_rows = out.rearrange("(g b) s d -> g s b d", b=G)

        @block.sync
        def _(sp):
            def body(s):
                p = s.back(1)
                if s.exists(NG):
                    wait(sp, added, s.back(2).value + 1 if s.back(2).exists(NG) else 0)
                    sp.dma_start(xg[s.slot][:, :, :], take(x_rows, s.value)).then_inc(x_loaded[s.slot], 16)
                if p.exists(NG):
                    sp.wait_ge(added, p.value + 1)
                    sp.dma_start(take(out_rows, p.value), total[p.slot][:, :, :]).then_inc(stored[p.slot], 16)

            run_steps(sp, NG, 1, body)
            for n in range(2):
                sp.wait_ge(stored[n], 16 * NG // 2)

        @block.gpsimd
        def _(pool):
            def body(s):
                if s.exists(NG):
                    pool.wait_ge(index_ready, s.value + 1)
                    hold(pool, added, s.back(2).value + 1 if s.back(2).exists(NG) else 0, passed)
                    for b in range(G):
                        pool.indirect_dma_start(y[s.slot][:, b, :], None, expert_out[:, :],
                                                bass.IndirectOffsetOnAxis(index[s.slot][:, b:b + 1], 0)
                                                ).then_inc(got[s.slot], 16)

            run_steps(pool, NG, 1, body)

        @block.vector
        def _(dve):
            def body(s):
                p = s.back(1)
                if s.exists(NG):
                    wait(dve, got[s.slot], 16 * G * s.pair)
                    copy_index(dve, index[s.slot], route["get"], s).then_inc(index_ready, 1)
                if p.exists(NG):
                    wait(dve, added, p.value)
                    copy_index(dve, weight, route["weight"], p).then_inc(weight_ready, 1)
                    dve.wait_ge(weight_ready, p.value + 1)
                    dve.wait_ge(x_loaded[p.slot], 16 * (p.pair + 1))
                    dve.wait_ge(got[p.slot], 16 * G * (p.pair + 1))
                    wait(dve, stored[p.slot], 16 * p.pair)
                    for b in range(G):
                        last = dve.scalar_tensor_tensor(out=total[p.slot][:, b, :], in0=y[p.slot][:, b, :],
                                                        scalar=weight[:, b:b + 1], in1=xg[p.slot][:, b, :],
                                                        op0=ALU.mult, op1=ALU.add)
                    last.then_inc(added, 1)

            run_steps(dve, NG, 1, body)

        ended.close()
        sems.clear()


_INS = ["x", "ctx_1024", "mask_1x1xSxS2_ik1", "mask_BxSxS2_if1", "g_xattn", "g_ffn",
        "L0_xattn_w_q", "L0_xattn_w_k", "L0_xattn_w_v", "L0_xattn_w_o", "L0_xattn_b_o",
        "L0_ffn_k0", "L0_ffn_k1", "L0_ffn_k2", "L0_ffn_s0", "L0_ffn_s1", "L0_ffn_s2",
        "L1_xattn_Wq", "L1_xattn_Wk", "L1_xattn_Wv", "L1_xattn_Wo", "L1_xattn_bo",
        "L1_ffn_Wr", "L1_ffn_W1", "L1_ffn_W2"]


def laid_out(name, a):
    if name.startswith("L1_xattn_W"):
        a = a.T
    if name[-1] in "qk" and "xattn" in name and a.ndim == 2:
        a = a.reshape(D, NP, 2, DK).transpose(0, 2, 3, 1).reshape(D, D)
    return a


def kernel(**inputs):
    import numpy as _np
    import concourse.bacc as _bacc
    from concourse import mybir as _mybir
    from concourse.bass_utils import run_bass_kernel_spmd as _run

    nc = _bacc.Bacc("TRN2", target_bir_lowering=False, num_devices=1)
    arrays, args = {}, {}
    for name in _INS:
        a = _np.ascontiguousarray(laid_out(name, _np.asarray(inputs[name])))
        if a.ndim == 0:
            a = a.reshape(1)
        arrays[f"in_{name}_dram"] = a
        args[name] = nc.dram_tensor(f"in_{name}_dram", a.shape, _mybir.dt.from_np(a.dtype), kind="ExternalInput").ap()
    out = nc.dram_tensor("out_0_dram", (B, S, D), F32, kind="ExternalOutput").ap()
    flamingo_program(nc, args, out)
    r = _run(nc, [arrays], core_ids=[0])
    return r.results[0]["out_0_dram"]
```

```python
from contextlib import ExitStack

import concourse.bass as bass
from concourse import mybir

F32 = mybir.dt.float32
F16 = mybir.dt.float16
BF16 = mybir.dt.bfloat16
I32 = mybir.dt.int32
U32 = mybir.dt.uint32
U8 = mybir.dt.uint8
ALU = mybir.AluOpType
ACT = mybir.ActivationFunctionType
AX = mybir.AxisListType

P = 128
B, S, D = 32, 112, 256
S2 = 375
H, DK = 16, 16
KC = D // P
CH = 3
CK = S2 // CH
NP = H // 2
QUAD = 32
NT = H // 4
UNITS = NT * CH
G = 4
NG = B // G
GT = G * S
F = 1024
FC = F // P
E = 8
CAP = B * S // E
STACK = 3 * QUAD
ROWS = STACK + 2
LAG = 3
PROBS = 2 * CH
VECTOR_UNITS = ((4, 6, 8, 9, 10), (6, 8, 10))
W_SCALE = 2.0 ** 6
MASKED = float(2 ** 30)
EPS = 1e-5
LARGEST = 3.0e38


class Step:

    def __init__(self, pair, slot):
        self.pair, self.slot = pair, slot
        self.value = 2 * pair + slot

    def back(self, n):
        total = self.slot - n
        pairs = total // 2
        return Step(self.pair + pairs if pairs else self.pair, total % 2)

    def exists(self, count):
        return 0 <= self.value < count if isinstance(self.value, int) else count > 1


def run_steps(eng, count, lag, body, head=4):
    for s in range(head):
        body(Step(s // 2, s % 2))
    with eng.Fori(head // 2, count // 2) as pair:
        for slot in range(2):
            body(Step(pair, slot))
    for s in range(count, count + lag):
        body(Step(s // 2, s % 2))


def wait(eng, sem, value):
    if not isinstance(value, int) or value > 0:
        eng.wait_ge(sem, value)


class Semaphores:

    def __init__(self, nc, stack):
        self.nc, self.stack, self.made = nc, stack, []

    def new(self, name):
        self.made.append(self.stack.enter_context(self.nc.semaphore(name)))
        return self.made[-1]

    def clear(self):
        with self.nc.Block() as block:
            @block.sync
            def _(sp):
                for s in self.made:
                    sp.sem_clear(s)


def flamingo_program(nc, a, out):
    def dram(name, shape, dt):
        return nc.dram_tensor(name, shape, dt, kind="Internal").ap()

    x1 = dram("x_after_attention_0", [B, S, D], F32)
    x2 = dram("x_after_ffn_0", [B, S, D], F32)
    x3 = dram("x_after_attention_1", [B, S, D], F32)
    q_split = dram("q_split", [2, 3, P, B * S], F16) 
    k_split = dram("k_split", [2, 2, 3, P, S2], F16)
    expert_in = dram("expert_in", [E * CAP, D], F32)
    expert_out = dram("expert_out", [E * CAP, D], F32)

    with ExitStack() as ctx:
        def sb(name, shape, dt):
            return ctx.enter_context(nc.sbuf_tensor(name, shape, dt))

        m = {
            "bank": [ctx.enter_context(nc.psum_tensor(f"bank{i}", [P, 512], F32)) for i in range(8)],
            "ident": sb("ident", [P, P], F32),
            "ident_h": sb("ident_h", [P, P], F16),
            "ident_b": sb("ident_b", [P, P], BF16),
            "eps": sb("eps", [P, 1], F32),
            "gate": sb("gate", [P, 4], F32),
            "ffn_scale": sb("ffn_scale", [P, 1], F32),
            "sign": sb("sign", [P, 2], F32),
            "ffn_w": [sb("ffn_w0", [P, KC, F], F16), sb("ffn_w1", [P, FC, F], F16), sb("ffn_w2", [P, FC, D], F16)],
            "wq": [sb(f"wq{n}", [P, KC, D], F32) for n in range(2)],
            "wk": [[sb(f"wk{n}_{part}", [P, KC, D], F16) for part in ("high", "low")] for n in range(2)],
            "wv": [[sb(f"wv{n}_{part}", [P, KC, D], F16) for part in ("high", "low")] for n in range(2)],
            "wo": [sb(f"wo{n}", [P, KC, D], F32) for n in range(2)],
            "bo": [sb(f"bo{n}", [S, D], F32) for n in range(2)],
        }
        m["experts_cleared"] = ctx.enter_context(nc.semaphore("experts_cleared"))
        m["zeros"] = sb("zeros", [P, CAP * E * D // P // 14], F32)
        setup_phase(nc, m, a, expert_in)
        queries_phase(nc, m, 0, a["x"], a["mask_1x1xSxS2_ik1"], q_split)
        attention_phase(nc, m, 0, a["x"], x1, a["ctx_1024"], a["mask_1x1xSxS2_ik1"], q_split, k_split)
        ffn_phase(nc, m, a, x1, x2)
        queries_phase(nc, m, 1, x2, a["mask_BxSxS2_if1"], q_split)
        attention_phase(nc, m, 1, x2, x3, a["ctx_1024"], a["mask_BxSxS2_if1"], q_split, k_split)
        moe_phases(nc, m, a, x3, expert_in, expert_out, out)


def setup_phase(nc, m, a, expert_in):
    with ExitStack() as ctx:
        sems = Semaphores(nc, ctx)
        def sem(name):
            return sems.new(name)

        raw = {(w, n): ctx.enter_context(nc.sbuf_tensor(f"raw_w{w}{n}", [P, KC, D], F32)) for w in "kv" for n in range(2)}
        k_in = [ctx.enter_context(nc.sbuf_tensor(f"k{n}_in", [P, *shape], U8))
                for n, shape in enumerate(((2 * KC, F), (FC, F), (FC, D)))]
        w0_parts = ctx.enter_context(nc.sbuf_tensor("w0_parts", [P, 2 * KC, F], F16))
        factors = ctx.enter_context(nc.sbuf_tensor("factors", [P, 4], F32))
        gin = ctx.enter_context(nc.sbuf_tensor("gate_in", [P, 4], F32))
        sin = ctx.enter_context(nc.sbuf_tensor("scale_in", [P, 3], F32))
        mag = ctx.enter_context(nc.sbuf_tensor("scale_parts", [P, 4], F32))
        small_loaded, weights_loaded, raw_loaded = sem("small_loaded"), sem("weights_loaded"), sem("raw_loaded")
        cleared, made = sem("su_cleared"), sem("su_made")
        chain, gated = sem("su_chain"), sem("su_gated")
        k_loaded, w_step, high_ready = sem("k_loaded"), sem("w_step"), sem("su_high_ready")
        factors_ready = sem("factors_ready")
        ended = ExitStack()
        block = ended.enter_context(nc.Block())

        def chunked(w):
            return w.rearrange("(c p) n -> p c n", p=P)

        @block.sync
        def _(sp):
            for n, g in enumerate((a["g_xattn"], a["g_ffn"])):
                sp.dma_start(gin[:, 2 * n:2 * n + 2], g.partition_broadcast(P)).then_inc(small_loaded, 16)
            for n in range(3):
                s = a[f"L0_ffn_s{n}"]
                sp.dma_start(sin[:, n:n + 1], s.partition_broadcast(P)).then_inc(small_loaded, 16)
            for n in range(3):
                sp.dma_start(k_in[n][:, :, :], chunked(a[f"L0_ffn_k{n}"])).then_inc(k_loaded, 16)
            for w in "kvqo":
                for n, name in enumerate((f"L0_xattn_w_{w}", f"L1_xattn_W{w}")):
                    dst = raw[w, n] if w in "kv" else m["w" + w][n]
                    sp.dma_start(dst[:, :, :], chunked(a[name])).then_inc(raw_loaded if w in "kv" else weights_loaded, 16)
            for n, b in enumerate((a["L0_xattn_b_o"], a["L1_xattn_bo"])):
                sp.dma_start(m["bo"][n][:, :], b.partition_broadcast(S)).then_inc(weights_loaded, 16)
            sp.wait_ge(cleared, 1)
            rows = expert_in.rearrange("(p f r) n -> p f (r n)", f=14, p=P)
            sp.dma_start(rows, m["zeros"][:, :].unsqueeze(1).to_broadcast([P, 14, m["zeros"].shape[1]])
                         ).then_inc(m["experts_cleared"], 16)
            sp.wait_ge(weights_loaded, 96)

        @block.gpsimd
        def _(pool):
            for t in (m["ident"], m["ident_h"], m["ident_b"]):
                pool.memset(t[:, :], 0.0).then_inc(made, 1)
            pool.wait_ge(made, 3)
            for t in (m["ident"], m["ident_h"], m["ident_b"]):
                pool.affine_select(out=t[:, :], in_=t[:, :], compare_op=ALU.not_equal, fill=1.0, base=0,
                                   pattern=[[-1, P]], channel_multiplier=1).then_inc(made, 1)

        @block.vector
        def _(dve):
            dve.memset(m["zeros"][:, :], 0.0).then_inc(cleared, 1)
            dve.memset(m["eps"][:, :], EPS)
            dve.wait_ge(small_loaded, 80)
            steps = 0

            def link(ins):
                nonlocal steps
                steps += 1
                ins.then_inc(chain, 1)
                dve.wait_ge(chain, steps)

            link(dve.tensor_scalar(m["sign"][:, :], sin[:, 0:2], 0.0, None, ALU.is_ge))
            link(dve.tensor_scalar(m["sign"][:, :], m["sign"][:, :], 2.0, -1.0, ALU.mult, ALU.add))
            link(dve.tensor_tensor(mag[:, 0:2], sin[:, 0:2], m["sign"][:, :], ALU.mult))
            link(dve.tensor_tensor(mag[:, 2:3], mag[:, 0:1], mag[:, 1:2], ALU.mult))
            link(dve.tensor_tensor(mag[:, 3:4], mag[:, 2:3], sin[:, 2:3], ALU.mult))
            dve.wait_ge(gated, 1)
            link(dve.tensor_scalar(m["ffn_scale"][:, :], mag[:, 3:4], m["gate"][:, 2:3], 4.0 * 32.0,
                                   ALU.mult, ALU.mult))
            for n, size in enumerate((1.0, 2.0 ** -5)):
                dve.tensor_scalar(factors[:, 2 * n:2 * n + 1], m["sign"][:, n:n + 1], 2.0 * size, None,
                                  ALU.mult).then_inc(w_step, 1)
                dve.tensor_scalar(factors[:, 2 * n + 1:2 * n + 2], m["sign"][:, n:n + 1], size if n == 0 else -size,
                                  None, ALU.mult).then_inc(w_step, 1)
            dve.wait_ge(w_step, 4)
            dve.sem_inc(factors_ready, 1)
            for i, ((w, n), tile) in enumerate(raw.items()):
                dve.wait_ge(high_ready, i + 1)
                dve.scalar_tensor_tensor(out=m["w" + w][n][1][:, :, :], in0=tile[:, :, :], scalar=W_SCALE,
                                         in1=m["w" + w][n][0][:, :, :], op0=ALU.mult, op1=ALU.subtract)
            w = m["ffn_w"]
            dve.wait_ge(k_loaded, 48)
            dve.tensor_scalar(w0_parts[:, :, :], k_in[0][:, :, :], factors[:, 0:1], factors[:, 1:2],
                              ALU.mult, ALU.subtract).then_inc(w_step, 1)
            dve.tensor_scalar(w[2][:, :, :], k_in[2][:, :, :], 2.0, -1.0, ALU.mult, ALU.add)
            dve.wait_ge(w_step, 5)
            dve.tensor_tensor(w[0][:, :, :], w0_parts[:, 0:KC, :], w0_parts[:, KC:2 * KC, :], ALU.subtract)

        @block.scalar
        def _(act):
            act.wait_ge(small_loaded, 80)
            act.activation(m["gate"][:, :], gin[:, :], ACT.Tanh).then_inc(gated, 1)
            act.wait_ge(raw_loaded, 64)
            for (w, n), tile in raw.items():
                act.activation(m["w" + w][n][0][:, :, :], tile[:, :, :], ACT.Copy, scale=W_SCALE).then_inc(high_ready, 1)
            act.wait_ge(k_loaded, 48)
            act.wait_ge(factors_ready, 1)
            act.activation(m["ffn_w"][1][:, :, :], k_in[1][:, :, :], ACT.Identity, bias=factors[:, 3:4],
                           scale=factors[:, 2:3])

        ended.close()
        sems.clear()


def queries_phase(nc, m, layer, x_in, mask, q_split):
    tag = f"_q{layer}"
    with ExitStack() as ctx:
        sems = Semaphores(nc, ctx)
        def sb(name, shape, dt):
            return ctx.enter_context(nc.sbuf_tensor(name + tag, shape, dt))

        def sem(name):
            return sems.new(name + tag)

        masks = G if layer else 1
        xg = [sb(f"xg{n}", [S, G, D], F32) for n in range(2)]
        mask_in = [sb(f"mask_in{n}", [S, masks, S2], I32) for n in range(2)]
        mask_f = sb("mask_f", [S, masks, S2], F32)
        seen = sb("seen", [S, masks], F32)
        stats = sb("stats", [S, G, 6], F32)
        mean_var = sb("mean_var", [S, G, 2], F32)
        dev = sb("dev", [S, G], F32)
        scale = sb("scale", [S, G], F32)
        xn = [sb(f"xn{n}", [S, G, D], F32) for n in range(2)]
        xt = [sb(f"xt{n}", [P, KC, GT], F32) for n in range(2)]
        high = [sb(f"high{n}", [P, KC, GT], F16) for n in range(2)]
        low = [sb(f"low{n}", [P, KC, GT], F16) for n in range(2)]
        x_loaded = [sem(f"x_loaded{n}") for n in range(2)]
        mask_loaded = [sem(f"mask_loaded{n}") for n in range(2)]
        dve_chain, var_ready, dev_ready, scaled = sem("dve_chain"), sem("var_ready"), sem("dev_ready"), sem("scaled")
        xn_ready, turned, xt_ready, q_ready = sem("xn_ready"), sem("turned"), sem("xt_ready"), sem("q_ready")
        high_ready, low_ready = sem("high_ready"), sem("low_ready")
        stored = [sem(f"stored{n}") for n in range(2)]
        passed = sem("passed")
        ended = ExitStack()
        block = ended.enter_context(nc.Block())
        turn_bank = [m["bank"][0:2], m["bank"][2:4]]
        q_bank = [m["bank"][4:6], m["bank"][6:8]]
        x_rows = x_in.rearrange("(g b) s d -> g s b d", b=G)
        q_out = q_split.rearrange("e w p (g t) -> w g p e t", t=GT)

        @block.sync
        def _(sp):
            if not layer:
                sp.dma_start(mask_in[0][:, 0, :], mask[0, 0, :, :]).then_inc(mask_loaded[0], 16)

            def body(s):
                if s.exists(NG):
                    wait(sp, xn_ready, s.back(2).value + 1 if s.back(2).exists(NG) else 0)
                    sp.dma_start(xg[s.slot][:, :, :], take(x_rows, s.value)).then_inc(x_loaded[s.slot], 16)
                    if layer:
                        rows = mask.rearrange("(g b) s k -> g s b k", b=G)
                        sp.dma_start(mask_in[s.slot][:, :, :],
                                     take(rows, s.value)).then_inc(mask_loaded[s.slot], 16)
                r = s.back(3)
                if r.exists(NG):
                    for g, (tile, ready) in enumerate(((high, high_ready), (high, high_ready), (low, low_ready))):
                        wait(sp, ready, KC * (r.value + 1))
                        sp.dma_start(take(q_out[g], r.value), tile[r.slot][:, :, :]).then_inc(stored[r.slot], 16)

            run_steps(sp, NG, 3, body)
            for n in range(2):
                sp.wait_ge(stored[n], 48 * NG // 2)

        @block.vector
        def _(dve):
            def see(slot, done):
                dve.tensor_scalar(mask_f[:, :, :], mask_in[slot][:, :, :], 0.0, None,
                                  ALU.not_equal).then_inc(dve_chain, 1)
                dve.wait_ge(dve_chain, done + 1)
                dve.tensor_reduce(seen[:, :], mask_f[:, :, :], AX.X, ALU.max).then_inc(dve_chain, 1)

            if not layer:
                dve.wait_ge(mask_loaded[0], 16)
                see(0, 0)
            per, first = (3, 0) if layer else (1, 2)

            def normalise(p):
                dve.wait_ge(dev_ready, p.value + 1)
                dve.reciprocal(scale[:, :], dev[:, :]).then_inc(scaled, 1)
                dve.wait_ge(scaled, 2 * p.value + 1)
                seen_all = seen[:, :] if layer else seen[:, :].to_broadcast([S, G])
                dve.tensor_tensor(scale[:, :], scale[:, :], seen_all, ALU.mult).then_inc(scaled, 1)
                dve.wait_ge(scaled, 2 * p.value + 2)
                wait(dve, turned, KC * (p.back(2).value + 1) if p.back(2).exists(NG) else 0)
                for b in range(G):
                    last = dve.tensor_scalar(xn[p.slot][:, b, :], xg[p.slot][:, b, :], mean_var[:, b, 0:1],
                                             scale[:, b:b + 1], ALU.subtract, ALU.mult)
                last.then_inc(xn_ready, 1)

            def statistics(s):
                dve.wait_ge(x_loaded[s.slot], 16 * (s.pair + 1))
                wait(dve, xn_ready, s.value)
                done = per * s.value + first
                if layer:
                    dve.wait_ge(mask_loaded[s.slot], 16 * (s.pair + 1))
                    wait(dve, dve_chain, done)
                    see(s.slot, done)
                    done = done + 2
                for b in range(G):
                    last = dve.bn_stats(stats[:, b, :], xg[s.slot][:, b, :])
                last.then_inc(dve_chain, 1)
                hold(dve, dve_chain, done + 1, passed)
                for b in range(G):
                    last = dve.bn_aggr(mean_var[:, b, :], stats[:, b, :])
                last.then_inc(var_ready, 1)

            def low_parts(q):
                wait(dve, stored[q.slot], 48 * q.pair)
                for c in range(KC):
                    dve.wait_ge(high_ready, KC * q.value + c + 1)
                    dve.tensor_tensor(low[q.slot][:, c, :], q_bank[q.slot][c][:, 0:GT],
                                      high[q.slot][:, c, :], ALU.subtract).then_inc(low_ready, 1)

            def body(s):
                p, q = s.back(1), s.back(2)
                if p.exists(NG):
                    normalise(p)
                if q.exists(NG):
                    low_parts(q)
                if s.exists(NG):
                    statistics(s)

            run_steps(dve, NG, 2, body)

        @block.scalar
        def _(act):
            def body(s):
                p, q = s.back(1), s.back(2)
                if q.exists(NG):
                    wait(act, stored[q.slot], 48 * q.pair)
                    for c in range(KC):
                        act.wait_ge(q_ready, KC * q.value + c + 1)
                        act.activation(high[q.slot][:, c, :], q_bank[q.slot][c][:, 0:GT], ACT.Copy).then_inc(high_ready, 1)
                if p.exists(NG):
                    wait(act, q_ready, KC * (p.back(2).value + 1) if p.back(2).exists(NG) else 0)
                    for c in range(KC):
                        act.wait_ge(turned, KC * p.value + c + 1)
                        act.activation(xt[p.slot][:, c, :], turn_bank[p.slot][c][:, 0:GT], ACT.Copy).then_inc(xt_ready, 1)
                if s.exists(NG):
                    act.wait_ge(var_ready, s.value + 1)
                    act.activation(dev[:, :], mean_var[:, :, 1], ACT.Sqrt, bias=m["eps"][0:S, :]).then_inc(dev_ready, 1)

            run_steps(act, NG, 2, body)

        @block.tensor
        def _(pe):
            def body(s):
                p, q = s.back(1), s.back(2)
                if q.exists(NG):
                    pe.wait_ge(xt_ready, KC * (q.value + 1))
                    wait(pe, low_ready, KC * (q.back(2).value + 1) if q.back(2).exists(NG) else 0)
                    for j in range(KC):
                        for c in range(KC):
                            last = pe.matmul(q_bank[q.slot][j][:, 0:GT], m["wq"][layer][:, c, j * P:(j + 1) * P],
                                             xt[q.slot][:, c, :], start=c == 0, stop=c == KC - 1)
                        last.then_inc(q_ready, 1)
                if p.exists(NG):
                    pe.wait_ge(xn_ready, p.value + 1)
                    wait(pe, xt_ready, KC * (p.back(2).value + 1) if p.back(2).exists(NG) else 0)
                    for c in range(KC):
                        for b in range(G):
                            last = pe.transpose(turn_bank[p.slot][c][:, b * S:(b + 1) * S],
                                                xn[p.slot][:, b, c * P:(c + 1) * P], m["ident"][0:S, 0:S])
                        last.then_inc(turned, 1)

            run_steps(pe, NG, 2, body)

        ended.close()
        sems.clear()


def hold(eng, sem, value, passed):
    if not isinstance(value, int) or value > 0:
        eng.wait_ge(sem, value)
        eng.sem_inc(passed, 1)


def take(ap, index):
    return ap[index] if isinstance(index, int) else ap[bass.ds(index, 1)].squeeze(0)


def attention_phase(nc, m, layer, x_in, x_out, context, mask, q_split, k_split):
    tag = f"_a{layer}"
    with ExitStack() as ctx:
        sems = Semaphores(nc, ctx)
        def sb(name, shape, dt):
            return ctx.enter_context(nc.sbuf_tensor(name + tag, shape, dt))

        def sem(name):
            return sems.new(name + tag)

        def two(make, name, *args):
            return [make(f"{name}{n}", *args) for n in range(2)]

        ctx_in = two(sb, "ctx_in", [P, KC, S2], F32)
        ctx_high, ctx_low = two(sb, "ctx_high", [P, KC, S2], F16), two(sb, "ctx_low", [P, KC, S2], F16)
        k_high = sb("k_high", [P, KC, S2], F16)
        k_low = sb("k_low", [P, KC, S2], F16)
        k_stack = two(sb, "k_stack", [P, NP, S2], F16)
        q_stack = two(sb, "q_stack", [P, NP, 2 * S], F16)
        values = two(sb, "values", [CK, CH, H, QUAD], F32)
        mask_in = two(sb, "mask_in", [S, S2], I32)
        mask_f = sb("mask_f", [S, S2], F32)
        seen = sb("seen", [S, 2], F32)
        mask_add = sb("mask_add", [S, S2], F32)
        mask_cut = sb("mask_cut", [S, S2], BF16)
        cut_t = two(sb, "cut_t", [CK, CH, S], BF16)
        mask_t = two(sb, "mask_t", [CK, CH, S], BF16)
        masked_scores = sb("masked_scores", [S, 2, S2], BF16)
        row_max = sb("row_max", [S, H], F32)
        max_parts = sb("max_parts", [S, 2 * H], F16)
        max_t = sb("max_t", [2 * H, S], F16)
        probs = sb("probs", [CK, PROBS, GT], F32)
        heads_t = sb("heads_t", [P, GT], F32)
        inverse = sb("inverse", [S, H], F32)
        heads_q = sb("heads_q", [S, H, DK], F32)
        heads_n = sb("heads_n", [P, KC, S], F32)
        x_old = two(sb, "x_old", [S, D], F32)
        attended = sb("attended", [S, D], F32)
        x_new = two(sb, "x_new", [S, D], F32)

        def halves(name):
            return [two(sem, f"{name}_{half}_") for half in ("first", "second")]

        ctx_loaded, q_loaded, k_loaded = two(sem, "ctx_loaded"), halves("q_loaded"), halves("k_loaded")
        mask_loaded, max_loaded, x_loaded = two(sem, "mask_loaded"), two(sem, "max_loaded"), two(sem, "x_loaded")
        k_stored, x_stored = sem("k_stored"), two(sem, "x_stored")
        zeros_set, ones_set = sem("zeros_set"), sem("ones_set")
        ctx_high_ready, ctx_low_ready = sem("ctx_high_ready"), sem("ctx_low_ready")
        k_made, k_high_ready, k_low_ready = sem("k_made"), sem("k_high_ready"), sem("k_low_ready")
        v_made, v_ready = sem("v_made"), sem("v_ready")
        mask_step, mask_made, mask_turned, mask_ready = (sem("mask_step"), sem("mask_made"), sem("mask_turned"),
                                                         sem("mask_ready"))
        rows_scored, rows_maxed = sem("rows_scored"), sem("rows_maxed")
        parts_ready, max_turned, max_ready = sem("parts_ready"), sem("max_turned"), sem("max_ready")
        scored, exped, weighted = sem("scored"), sem("exped"), sem("weighted")
        cut = sem("cut")
        heads_ready, heads_turned, inverted, normed = (sem("heads_ready"), sem("heads_turned"), sem("inverted"),
                                                       sem("normed"))
        turned_back, back_ready = sem("turned_back"), sem("back_ready")
        projected, biased, added = sem("projected"), sem("biased"), sem("added")
        passed, passed_pool = sem("passed"), sem("passed_pool")
        ended = ExitStack()
        block = ended.enter_context(nc.Block())

        row_bank = m["bank"][0:2]
        score_bank = m["bank"][2:5]
        head_bank = m["bank"][5]
        bank_a = m["bank"][6]
        bank_b = m["bank"][7]
        k_bank = (bank_b, bank_a)
        value_units, split_units = (3, 5, 7), (9, 11)
        max_t_ps = row_bank[0][:, :].bitcast(F16)[0:2 * H, 0:S]
        mask_t_ps = bank_b[:, :].bitcast(BF16)[0:CK, 0:CH * S]
        masks = B if layer else 1
        cut_units = VECTOR_UNITS[layer]
        HALF_UNITS, HALF_PAIRS = UNITS // 2, NP // 2

        ctx_rows = context.rearrange("b (c p) k -> b p c k", p=P)
        mask_rows = mask if layer else mask[0]
        q_rows = q_split.rearrange("e g (r p) (b t) -> e b (g r) p t", p=NP, t=S)
        k_rows = k_split.rearrange("s e g (r p) k -> s (e g r) p k", p=NP)
        k_save = k_split.rearrange("s e g p k -> s g p e k")
        SIDE = STACK // 2

        def load_queries(p, half):
            pairs = slice(HALF_PAIRS * half, HALF_PAIRS * (half + 1))
            for e in range(2):
                dst = q_stack[p.slot][SIDE * e:SIDE * (e + 1), pairs, e * S:(e + 1) * S]
                nc.sync.dma_start(dst, take(q_rows[e], p.value)[:, pairs, :]).then_inc(q_loaded[half][p.slot], 16)

        def load_keys(p, half):
            pairs = slice(HALF_PAIRS * half, HALF_PAIRS * (half + 1))
            nc.sync.dma_start(k_stack[p.slot][0:STACK, pairs, :],
                              k_rows[p.slot][:, pairs, :]).then_inc(k_loaded[half][p.slot], 16)

        @block.sync
        def _(sp):
            def body(s):
                p, x, d, e = (s.back(n) for n in range(1, 5))
                if e.exists(B):
                    wait(sp, added, e.back(2).value + 1 if e.back(2).exists(B) else 0)
                    sp.dma_start(x_old[e.slot][:, :], take(x_in, e.value)).then_inc(x_loaded[e.slot], 16)
                if s.exists(B):
                    wait(sp, ctx_low_ready, KC * (x.value + 1) if x.exists(B) else 0)
                    sp.dma_start(ctx_in[s.slot][:, :, :], take(ctx_rows, s.value)).then_inc(ctx_loaded[s.slot], 16)
                if p.exists(masks):
                    wait(sp, mask_step, 3 * (p.back(2).value + 1) if p.back(2).exists(masks) else 0)
                    sp.dma_start(mask_in[p.slot][:, :], take(mask_rows, p.value)).then_inc(mask_loaded[p.slot], 16)
                if p.exists(B):
                    for half in range(2):
                        hold(sp, k_loaded[half][p.slot], 16 * p.pair, passed)
                    for g, (tile, ready) in enumerate(((k_high, k_high_ready), (k_low, k_low_ready),
                                                       (k_high, k_high_ready))):
                        sp.wait_ge(ready, KC * (p.value + 1))
                        sp.dma_start(k_save[p.slot, g], tile[:, :, :]).then_inc(k_stored, 16)
                    if isinstance(p.value, int) and p.value == 0:
                        sp.wait_ge(zeros_set, 2)
                    hold(sp, scored, UNITS * d.value + HALF_UNITS if d.exists(B) else 0, passed)
                    hold(sp, k_stored, 48 * (p.value + 1), passed)
                    load_keys(p, 0)
                    load_queries(p, 0)
                if x.exists(B):
                    sp.wait_ge(max_ready, x.value + 1)
                    dst = q_stack[x.slot][STACK:ROWS, :, :].rearrange("w p t -> w (p t)")
                    sp.dma_start(dst, max_t[:, :]).then_inc(max_loaded[x.slot], 16)
                if p.exists(B):
                    hold(sp, scored, UNITS * (d.value + 1) if d.exists(B) else 0, passed)
                    load_keys(p, 1)
                    load_queries(p, 1)
                if e.exists(B):
                    sp.wait_ge(added, e.value + 1)
                    sp.dma_start(take(x_out, e.value), x_new[e.slot][:, :]).then_inc(x_stored[e.slot], 16)

            run_steps(sp, B, 4, body, 6)
            for n in range(2):
                sp.wait_ge(x_stored[n], 16 * B // 2)

        @block.gpsimd
        def _(pool):
            def body(s):
                if s.exists(B):
                    for c in range(KC):
                        hold(pool, ctx_high_ready, KC * s.value + c + 1, passed_pool)
                        pool.tensor_tensor(ctx_low[s.slot][:, c, :], ctx_in[s.slot][:, c, :], ctx_high[s.slot][:, c, :],
                                           ALU.subtract).then_inc(ctx_low_ready, 1)
                if isinstance(s.value, int) and s.value == 0:
                    pool.wait_ge(ctx_low_ready, KC)
                    for n in range(2):
                        pool.memset(k_stack[n][STACK:P, :, :], 1.0).then_inc(ones_set, 1)
                        pool.wait_ge(ones_set, 2 * n + 1)
                        pool.memset(values[n][:, :, :, DK:QUAD], 1.0).then_inc(ones_set, 1)
                        pool.wait_ge(ones_set, 2 * n + 2)

            run_steps(pool, B, 0, body, 6)

        @block.tensor
        def _(pe):
            ident, ident_h, ident_b = m["ident"], m["ident_h"], m["ident_b"]

            def make_keys(p, x, e, j):
                if j == 0:
                    pe.wait_ge(ctx_low_ready, KC * (p.value + 1))
                    if e.back(1).exists(B):
                        pe.wait_ge(biased, e.value)
                    elif x.back(1).exists(masks):
                        pe.wait_ge(mask_ready, 2 * x.value)
                    elif p.back(1).exists(B):
                        pe.wait_ge(k_low_ready, KC * (p.value - 1) + 1)
                else:
                    if x.back(1).exists(B):
                        pe.wait_ge(v_ready, CH * x.value)
                    elif p.back(1).exists(B):
                        pe.wait_ge(k_low_ready, KC * p.value)
                high, low = m["wk"][layer]
                for c in range(KC):
                    for n, (w, part) in enumerate(((high, ctx_high), (high, ctx_low), (low, ctx_high))):
                        last = pe.matmul(k_bank[j][:, 0:S2], w[:, c, j * P:(j + 1) * P], part[p.slot][:, c, :],
                                         start=c == 0 and n == 0, stop=c == KC - 1 and n == 2)
                last.then_inc(k_made, 1)

            def make_values(x, p, k):
                if k:
                    pe.wait_ge(v_ready, CH * x.value + k)
                elif p.exists(B):
                    pe.wait_ge(k_low_ready, KC * (p.value + 1))
                else:
                    wait(pe, v_ready, CH * x.value)
                high, low = m["wv"][layer]
                for c in range(KC):
                    for n, (part, w) in enumerate(((ctx_high, high), (ctx_high, low), (ctx_low, high))):
                        last = pe.matmul(bank_a[0:CK, 0:D], part[x.slot][:, c, k * CK:(k + 1) * CK], w[:, c, :],
                                         start=c == 0 and n == 0, stop=c == KC - 1 and n == 2)
                last.then_inc(v_made, 1)

            def turn_mask(x, p, e):
                pe.wait_ge(mask_step, 3 * (x.value + 1))
                if e.exists(B):
                    pe.wait_ge(back_ready, e.value + 1)
                elif p.exists(B):
                    pe.wait_ge(k_low_ready, KC * p.value + 1)
                for k in range(CH):
                    last = pe.transpose(mask_t_ps[:, k * S:(k + 1) * S], mask_cut[:, k * CK:(k + 1) * CK],
                                        ident_b[0:S, 0:S])
                last.then_inc(mask_turned, 1)

            def score_rows(x, h):
                if h % (H // 2) == 0:
                    half = h // (H // 2)
                    pe.wait_ge(q_loaded[half][x.slot], 32 * (x.pair + 1))
                    pe.wait_ge(k_loaded[half][x.slot], 16 * (x.pair + 1))
                if h == 0 and isinstance(x.value, int) and x.value == 0:
                    pe.wait_ge(ones_set, 4)
                if h == 0:
                    wait(pe, max_ready, x.value)
                elif h == 1:
                    wait(pe, rows_maxed, H * x.value)
                else:
                    pe.wait_ge(rows_maxed, H * x.value + h - 1)
                e = h % 2
                pe.matmul(row_bank[h % 2][0:S, 0:S2], q_stack[x.slot][0:STACK, h // 2, e * S:(e + 1) * S],
                          k_stack[x.slot][0:STACK, h // 2, :], start=True, stop=True).then_inc(rows_scored, 1)

            def turn_maxima(x):
                pe.wait_ge(parts_ready, 2 * (x.value + 1))
                pe.transpose(max_t_ps, max_parts[:, :], ident_h[0:S, 0:S]).then_inc(max_turned, 1)

            def score_unit(d, i):
                if i == 0:
                    pe.wait_ge(max_loaded[d.slot], 16 * (d.pair + 1))
                    if layer:
                        pe.wait_ge(mask_ready, 2 * (d.value + 1))
                    elif isinstance(d.value, int) and d.value == 0:
                        pe.wait_ge(mask_ready, 2)
                wait(pe, exped, UNITS * d.value + i - 2)
                t, k = divmod(i, CH)
                bank = score_bank[i % 3]
                by_scores = i not in cut_units
                if by_scores:
                    mask_cols = mask_t[d.slot if layer else 0][:, k, :]
                    pe.matmul(bank[0:CK, 0:GT], ident_b[0:CK, 0:CK], mask_cols.unsqueeze(1).to_broadcast([CK, 4, S]),
                              start=True, stop=True)
                for half in range(2):
                    last = pe.matmul(bank[0:CK, half * 2 * S:(half + 1) * 2 * S],
                                     k_stack[d.slot][0:ROWS, 2 * t + half, k * CK:(k + 1) * CK],
                                     q_stack[d.slot][0:ROWS, 2 * t + half, :],
                                     start=not by_scores, stop=True, skip_group_check=True)
                last.then_inc(scored, 1)

            def weigh_unit(d, i):
                t, k = divmod(i, CH)
                if i == 0:
                    pe.wait_ge(v_ready, CH * (d.value + 1))
                    wait(pe, heads_ready, d.value)
                if i in cut_units:
                    pe.wait_ge(cut, len(cut_units) * d.value + cut_units.index(i) + 1)
                else:
                    pe.wait_ge(exped, UNITS * d.value + i + 1)
                for j in range(4):
                    last = pe.matmul(head_bank[QUAD * j:QUAD * (j + 1), t * S:(t + 1) * S],
                                     values[d.slot][:, k, 4 * t + j, :], probs[:, i % PROBS, j * S:(j + 1) * S],
                                     start=k == 0, stop=k == CH - 1, tile_position=(0, QUAD * j))
                last.then_inc(weighted, 1)

            def turn_heads(e, p):
                pe.wait_ge(heads_ready, e.value + 1)
                if p.exists(B):
                    pe.wait_ge(k_low_ready, KC * p.value + 1)
                else:
                    wait(pe, biased, e.value)
                for t in range(NT):
                    last = pe.transpose(bank_b[0:S, t * P:(t + 1) * P], heads_t[:, t * S:(t + 1) * S], ident[:, :])
                last.then_inc(heads_turned, 1)

            def turn_heads_back(e):
                pe.wait_ge(normed, e.value + 1)
                for c in range(KC):
                    last = pe.transpose(bank_b[:, c * S:(c + 1) * S],
                                        heads_q[:, :, :].rearrange("q h r -> q (h r)")[:, c * P:(c + 1) * P],
                                        ident[0:S, 0:S])
                last.then_inc(turned_back, 1)

            def project(x, e):
                pe.wait_ge(back_ready, e.value + 1)
                if x.exists(masks):
                    pe.wait_ge(mask_ready, 2 * (x.value + 1))
                for c in range(KC):
                    last = pe.matmul(bank_b[0:S, 0:D], heads_n[:, c, :], m["wo"][layer][:, c, :],
                                     start=c == 0, stop=c == KC - 1)
                last.then_inc(projected, 1)

            def body(s):
                p, x, d, e = (s.back(n) for n in range(1, 5))
                for i in range(UNITS):
                    if d.exists(B):
                        score_unit(d, i)
                    if x.exists(B) and i < H // 2:
                        score_rows(x, 2 * i)
                    if d.exists(B) and i >= LAG:
                        weigh_unit(d, i - LAG)
                    if x.exists(B) and i < H // 2:
                        score_rows(x, 2 * i + 1)
                    if p.exists(B) and i in (0, 1):
                        make_keys(p, x, e, i)
                    if e.exists(B) and i == 2:
                        turn_heads(e, p)
                    if e.exists(B) and i == 4:
                        turn_heads_back(e)
                    if x.exists(B) and i in value_units:
                        make_values(x, p, value_units.index(i))
                    if x.exists(masks) and i == 8:
                        turn_mask(x, p, e)
                    if x.exists(B) and i == 9:
                        turn_maxima(x)
                for i in range(UNITS - LAG, UNITS):
                    if e.exists(B) and i == UNITS - 2:
                        project(x, e)
                    if d.exists(B):
                        weigh_unit(d, i)

            run_steps(pe, B, 4, body, 6)

        @block.scalar
        def _(act):
            def body(s):
                p, x, d, e = (s.back(n) for n in range(1, 5))
                if e.exists(B):
                    act.wait_ge(weighted, UNITS * (e.value + 1))
                    wait(act, heads_turned, e.value)
                    act.activation(heads_t[:, :], head_bank[:, 0:GT], ACT.Copy).then_inc(heads_ready, 1)
                for i in range(UNITS):
                    if d.exists(B):
                        act.wait_ge(scored, UNITS * d.value + i + 1)
                        wait(act, weighted, UNITS * d.value + i + 1 - PROBS)
                        act.activation(probs[:, i % PROBS, :], score_bank[i % 3][0:CK, 0:GT], ACT.Exp,
                                       scale=DK ** -0.5).then_inc(exped, 1)
                    if p.exists(B) and i in (0, 1):
                        wait(act, k_stored, 48 * p.value)
                        act.wait_ge(k_made, KC * p.value + i + 1)
                        act.activation(k_high[:, i, :], k_bank[i][:, 0:S2], ACT.Copy,
                                       scale=1 / W_SCALE).then_inc(k_high_ready, 1)
                    if e.exists(B) and i == 4:
                        act.wait_ge(turned_back, e.value + 1)
                        wait(act, projected, e.value)
                        act.activation(heads_n[:, :, :], bank_b[:, 0:KC * S].rearrange("p (c t) -> p c t", c=KC),
                                       ACT.Copy).then_inc(back_ready, 1)
                    if x.exists(B) and i in value_units:
                        k = value_units.index(i)
                        act.wait_ge(v_made, CH * x.value + k + 1)
                        act.activation(values[x.slot][:, k, :, 0:DK],
                                       bank_a[0:CK, 0:D].rearrange("p (h r) -> p h r", r=DK),
                                       ACT.Copy, scale=1 / W_SCALE).then_inc(v_ready, 1)
                    if x.exists(B) and i == 9:
                        act.wait_ge(max_turned, x.value + 1)
                        w = x.back(1)
                        if w.exists(B):
                            act.wait_ge(max_loaded[w.slot], 16 * (w.pair + 1))
                        act.activation(max_t[:, :], max_t_ps, ACT.Copy).then_inc(max_ready, 1)
                    if s.exists(B) and i in split_units:
                        c = split_units.index(i)
                        act.wait_ge(ctx_loaded[s.slot], 16 * (s.pair + 1))
                        act.activation(ctx_high[s.slot][:, c, :], ctx_in[s.slot][:, c, :],
                                       ACT.Copy).then_inc(ctx_high_ready, 1)

            run_steps(act, B, 4, body, 6)

        @block.vector
        def _(dve):
            for n in range(2):
                dve.memset(q_stack[n][0:STACK, :, :], 0.0).then_inc(zeros_set, 1)

            def read_mask(p):
                dve.wait_ge(mask_loaded[p.slot], 16 * (p.pair + 1))
                dve.tensor_scalar(mask_f[:, :], mask_in[p.slot][:, :], 0.0, None, ALU.not_equal).then_inc(mask_step, 1)
                dve.wait_ge(mask_step, 3 * p.value + 1)
                dve.tensor_reduce(seen[:, 0:1], mask_f[:, :], AX.X, ALU.max).then_inc(mask_step, 1)
                dve.wait_ge(mask_step, 3 * p.value + 2)
                dve.tensor_scalar(seen[:, 1:2], seen[:, 0:1], MASKED, None, ALU.mult).then_inc(mask_made, 1)

            def split_mask(p):
                dve.wait_ge(mask_made, 2 * p.value + 1)
                dve.tensor_scalar(mask_add[:, :], mask_f[:, :], 1.0, seen[:, 1:2], ALU.subtract,
                                  ALU.mult).then_inc(mask_made, 1)
                wait(dve, mask_turned, p.value)
                dve.wait_ge(mask_made, 2 * p.value + 2)
                dve.tensor_scalar(mask_cut[:, :], mask_add[:, :], MASKED, None, ALU.add).then_inc(mask_step, 1)

            def copy_mask(x):
                dve.wait_ge(mask_turned, x.value + 1)
                w = x.back(2)
                wait(dve, cut, len(cut_units) * (w.value + 1) if w.exists(B) else 0)
                wait(dve, scored, UNITS * (w.value + 1) if w.exists(B) else 0)
                turned_cut = mask_t_ps.rearrange("p (k q) -> p k q", k=CH)
                dve.tensor_copy(cut_t[x.slot][:, :, :], turned_cut).then_inc(mask_ready, 1)
                dve.tensor_scalar(mask_t[x.slot][:, :, :], turned_cut, MASKED, None, ALU.subtract).then_inc(mask_ready, 1)

            def reduce_row(x, h):
                hold(dve, rows_scored, H * x.value + h + 1, passed)
                dve.tensor_tensor_reduce(masked_scores[:, h % 2, :], row_bank[h % 2][0:S, 0:S2], mask_add[:, :],
                                         1.0, -LARGEST, ALU.add, ALU.max,
                                         row_max[:, h:h + 1]).then_inc(rows_maxed, 1)

            def split_maxima(x):
                dve.wait_ge(rows_maxed, H * (x.value + 1))
                wait(dve, max_turned, x.value)
                dve.tensor_scalar(max_parts[:, 0:H], row_max[:, :], -1.0, None, ALU.mult).then_inc(parts_ready, 1)
                dve.wait_ge(parts_ready, 2 * x.value + 1)
                dve.scalar_tensor_tensor(out=max_parts[:, H:2 * H], in0=row_max[:, :], scalar=-1.0,
                                         in1=max_parts[:, 0:H], op0=ALU.mult, op1=ALU.subtract).then_inc(parts_ready, 1)

            def normalise(e):
                dve.wait_ge(heads_turned, e.value + 1)
                heads = bank_b[0:S, 0:H * QUAD].rearrange("q (h r) -> q h r", r=QUAD)
                dve.reciprocal(inverse[:, :], heads[:, :, DK]).then_inc(inverted, 1)
                dve.wait_ge(inverted, e.value + 1)
                wait(dve, turned_back, e.value)
                dve.tensor_tensor(heads_q[:, :, :], heads[:, :, 0:DK],
                                  inverse[:, :].unsqueeze(2).to_broadcast([S, H, DK]), ALU.mult).then_inc(normed, 1)

            def add_output(e):
                dve.wait_ge(projected, e.value + 1)
                dve.tensor_tensor(attended[:, :], bank_b[0:S, 0:D], m["bo"][layer][:, :], ALU.add).then_inc(biased, 1)
                dve.wait_ge(biased, e.value + 1)
                dve.wait_ge(x_loaded[e.slot], 16 * (e.pair + 1))
                wait(dve, x_stored[e.slot], 16 * e.pair)
                dve.scalar_tensor_tensor(out=x_new[e.slot][:, :], in0=attended[:, :],
                                         scalar=m["gate"][0:S, layer:layer + 1], in1=x_old[e.slot][:, :],
                                         op0=ALU.mult, op1=ALU.add).then_inc(added, 1)

            def cut_weights(d, i):
                dve.wait_ge(exped, UNITS * d.value + i + 1)
                weights = probs[:, i % PROBS, :].rearrange("p (j t) -> p j t", j=4)
                mask_cols = cut_t[d.slot if layer else 0][:, i % CH, :].unsqueeze(1).to_broadcast([CK, 4, S])
                dve.tensor_tensor(weights, weights, mask_cols, ALU.min).then_inc(cut, 1)

            def low_keys(p, j):
                wait(dve, k_stored, 48 * p.value)
                dve.wait_ge(k_high_ready, KC * p.value + j + 1)
                dve.scalar_tensor_tensor(out=k_low[:, j, :], in0=k_bank[j][:, 0:S2], scalar=1 / W_SCALE,
                                         in1=k_high[:, j, :], op0=ALU.mult, op1=ALU.subtract).then_inc(k_low_ready, 1)

            def body(s):
                p, x, d, e = (s.back(n) for n in range(1, 5))
                for i in range(H // 2):
                    if x.exists(B):
                        reduce_row(x, 2 * i)
                        reduce_row(x, 2 * i + 1)
                    if d.exists(B) and i in cut_units:
                        cut_weights(d, i)
                    if p.exists(B) and i in (1, 2):
                        low_keys(p, i - 1)
                    if e.exists(B) and i == 3:
                        normalise(e)
                    if p.exists(masks) and i == 4:
                        read_mask(p)
                if x.exists(B):
                    split_maxima(x)
                if x.exists(masks):
                    copy_mask(x)
                for i in cut_units:
                    if d.exists(B) and i >= H // 2:
                        cut_weights(d, i)
                if p.exists(masks):
                    split_mask(p)
                if e.exists(B):
                    add_output(e)

            run_steps(dve, B, 4, body, 6)

        ended.close()
        sems.clear()


def ffn_phase(nc, m, a, x_in, x_out):
    with ExitStack() as ctx:
        sems = Semaphores(nc, ctx)
        def sb(name, shape, dt):
            return ctx.enter_context(nc.sbuf_tensor(name + "_f", shape, dt))

        def sem(name):
            return sems.new(name + "_f")

        def two(make, name, *args):
            return [make(f"{name}{n}", *args) for n in range(2)]

        w = m["ffn_w"]
        xg = two(sb, "xg", [S, G, D], F32)
        stats = sb("stats", [S, G, 6], F32)
        mean_var = sb("mean_var", [S, G, 2], F32)
        dev = sb("dev", [S, G], F32)
        scale = sb("scale", [S, G], F32)
        xn = sb("xn", [S, G, D], F32)
        xh, xl = two(sb, "xh", [P, KC, GT], F16), two(sb, "xl", [P, KC, GT], F16)
        h = [[sb(f"h{n}{part}", [P, FC, GT], F16) for part in "hl"] for n in range(2)]
        y = two(sb, "y", [S, G, D], F32)

        x_loaded, stored = two(sem, "x_loaded"), two(sem, "stored")
        stats_ready, var_ready, dev_ready, scaled = sem("stats_ready"), sem("var_ready"), sem("dev_ready"), sem("scaled")
        xn_ready, turned, xh_ready, xl_ready = sem("xn_ready"), sem("turned"), sem("xh_ready"), sem("xl_ready")
        z_made, h_high_ready, h_low_ready = sem("z_made"), sem("h_high_ready"), sem("h_low_ready")
        y_made, y_ready = sem("y_made"), sem("y_ready")
        passed = sem("passed")
        ended = ExitStack()
        block = ended.enter_context(nc.Block())

        z_bank, y_bank, turn_bank = m["bank"][0:4], m["bank"][4:6], m["bank"][6:8]
        x_rows = x_in.rearrange("(g b) s d -> g s b d", b=G)
        out_rows = x_out.rearrange("(g b) s d -> g s b d", b=G)
        ZS = 2 * FC

        @block.sync
        def _(sp):
            def body(s):
                if s.exists(NG):
                    wait(sp, y_ready, G * (s.back(2).value + 1) if s.back(2).exists(NG) else 0)
                    sp.dma_start(xg[s.slot][:, :, :], take(x_rows, s.value)).then_inc(x_loaded[s.slot], 16)

            run_steps(sp, NG, 1, body)

        @block.gpsimd
        def _(pool):
            def body(s):
                p = s.back(1)
                if p.exists(NG):
                    hold(pool, y_ready, G * (p.value + 1), passed)
                    pool.dma_start(take(out_rows, p.value), y[p.slot][:, :, :]).then_inc(stored[p.slot], 16)

            run_steps(pool, NG, 1, body)
            for n in range(2):
                pool.wait_ge(stored[n], 16 * NG // 2)

        @block.vector
        def _(dve):
            def normalise(s):
                dve.wait_ge(x_loaded[s.slot], 16 * (s.pair + 1))
                for b in range(G):
                    last = dve.bn_stats(stats[:, b, :], xg[s.slot][:, b, :])
                last.then_inc(stats_ready, 1)
                hold(dve, stats_ready, s.value + 1, passed)
                for b in range(G):
                    last = dve.bn_aggr(mean_var[:, b, :], stats[:, b, :])
                last.then_inc(var_ready, 1)

            def normalise_end(s):
                dve.wait_ge(dev_ready, s.value + 1)
                dve.reciprocal(scale[:, :], dev[:, :]).then_inc(scaled, 1)
                dve.wait_ge(scaled, s.value + 1)
                wait(dve, turned, KC * s.value)
                for b in range(G):
                    last = dve.tensor_scalar(xn[:, b, :], xg[s.slot][:, b, :], mean_var[:, b, 0:1],
                                             scale[:, b:b + 1], ALU.subtract, ALU.mult)
                last.then_inc(xn_ready, 1)

            def low_rows(s):
                for c in range(KC):
                    dve.wait_ge(xh_ready, KC * s.value + c + 1)
                    dve.tensor_tensor(xl[s.slot][:, c, :], turn_bank[c][:, 0:GT], xh[s.slot][:, c, :],
                                      ALU.subtract).then_inc(xl_ready, 1)

            def low_hidden(p, z):
                dve.wait_ge(h_high_ready, ZS * p.value + z + 1)
                layer, j = divmod(z, FC)
                high, low = h[layer]
                dve.scalar_tensor_tensor(out=low[:, j, :], in0=z_bank[z % 4][:, 0:GT], scalar=0.0,
                                         in1=high[:, j, :], op0=ALU.max, op1=ALU.subtract).then_inc(h_low_ready, 1)

            def add(p, b):
                dve.wait_ge(y_made, G * p.value + b + 1)
                if b == 0:
                    wait(dve, stored[p.slot], 16 * p.pair)
                dve.scalar_tensor_tensor(out=y[p.slot][:, b, :], in0=y_bank[b % 2][0:S, 0:D],
                                         scalar=m["ffn_scale"][0:S, 0:1], in1=xg[p.slot][:, b, :],
                                         op0=ALU.mult, op1=ALU.add).then_inc(y_ready, 1)

            def body(s):
                p = s.back(1)
                for z in range(ZS):
                    if p.exists(NG):
                        low_hidden(p, z)
                    if s.exists(NG):
                        if z == 4:
                            normalise(s)
                        if z == 6:
                            normalise_end(s)
                        if z == 12:
                            low_rows(s)
                if p.exists(NG):
                    for b in range(G):
                        add(p, b)

            run_steps(dve, NG, 1, body)

        @block.scalar
        def _(act):
            def body(s):
                p = s.back(1)
                for z in range(ZS):
                    if p.exists(NG):
                        act.wait_ge(z_made, ZS * p.value + z + 1)
                        layer, j = divmod(z, FC)
                        act.activation(h[layer][0][:, j, :], z_bank[z % 4][:, 0:GT], ACT.Relu).then_inc(h_high_ready, 1)
                    if s.exists(NG):
                        if z == 5:
                            act.wait_ge(var_ready, s.value + 1)
                            act.activation(dev[:, :], mean_var[:, :, 1], ACT.Sqrt, bias=m["eps"][0:S, :]).then_inc(dev_ready, 1)
                        if z == 12:
                            for c in range(KC):
                                act.wait_ge(turned, KC * s.value + c + 1)
                                act.activation(xh[s.slot][:, c, :], turn_bank[c][:, 0:GT], ACT.Copy).then_inc(xh_ready, 1)

            run_steps(act, NG, 1, body)

        @block.tensor
        def _(pe):
            def turn(s):
                pe.wait_ge(xn_ready, s.value + 1)
                wait(pe, xl_ready, KC * s.value)
                for c in range(KC):
                    for b in range(G):
                        last = pe.transpose(turn_bank[c][:, b * S:(b + 1) * S], xn[:, b, c * P:(c + 1) * P],
                                            m["ident"][0:S, 0:S])
                    last.then_inc(turned, 1)

            def hidden(p, z):
                layer, j = divmod(z, FC)
                wait(pe, h_low_ready, ZS * p.value + z - 3)
                if z == 0:
                    pe.wait_ge(xl_ready, KC * (p.value + 1))
                parts = h[0] if layer else [xh[p.slot], xl[p.slot]]
                chunks = FC if layer else KC
                for c in range(chunks):
                    if z == FC:
                        pe.wait_ge(h_low_ready, ZS * p.value + c + 1)
                    for n, part in enumerate(parts):
                        last = pe.matmul(z_bank[z % 4][:, 0:GT], w[layer][:, c, j * P:(j + 1) * P], part[:, c, :],
                                         start=c == 0 and n == 0, stop=c == chunks - 1 and n == 1)
                last.then_inc(z_made, 1)

            def output(p, b):
                wait(pe, y_ready, G * p.value + b - 1)
                for c in range(FC):
                    if b == 0:
                        pe.wait_ge(h_low_ready, ZS * p.value + FC + c + 1)
                    for n, part in enumerate(h[1]):
                        last = pe.matmul(y_bank[b % 2][0:S, 0:D], part[:, c, b * S:(b + 1) * S], w[2][:, c, :],
                                         start=c == 0 and n == 0, stop=c == FC - 1 and n == 1)
                last.then_inc(y_made, 1)

            def body(s):
                p = s.back(1)
                for z in range(ZS):
                    if p.exists(NG):
                        hidden(p, z)
                    if s.exists(NG) and z == 11:
                        turn(s)
                if p.exists(NG):
                    for b in range(G):
                        output(p, b)

            run_steps(pe, NG, 1, body)

        ended.close()
        sems.clear()


def moe_phases(nc, m, a, x_in, expert_in, expert_out, out):
    with ExitStack() as ctx:
        def sb(name, shape, dt):
            return ctx.enter_context(nc.sbuf_tensor(name + "_r", shape, dt))

        route = {
            "logits": sb("logits", [S, B, E], F32),
            "put": sb("put", [S, B], U32),
            "get": sb("get", [S, B], U32),
            "weight": sb("weight", [S, B], F32),
        }
        with nc.sbuf_tensor("x_normed", [S, B, D], F32) as x_normed:
            logits_phase(nc, m, a, x_in, x_normed, route)
            ranks_phase(nc, m, route)
            experts_phase(nc, m, a, x_normed, route, expert_in, expert_out)
        combine_phase(nc, route, x_in, expert_out, out)


def logits_phase(nc, m, a, x_in, x_normed, route):
    with ExitStack() as ctx:
        sems = Semaphores(nc, ctx)
        def sb(name, shape, dt):
            return ctx.enter_context(nc.sbuf_tensor(name + "_l", shape, dt))

        def sem(name):
            return sems.new(name + "_l")

        def two(make, name, *args):
            return [make(f"{name}{n}", *args) for n in range(2)]

        wr = sb("wr", [P, KC, E], F32)
        xg = two(sb, "xg", [S, G, D], F32)
        stats = sb("stats", [S, G, 6], F32)
        mean_var = sb("mean_var", [S, G, 2], F32)
        dev = sb("dev", [S, G], F32)
        scale = sb("scale", [S, G], F32)
        xn = two(sb, "xn", [S, G, D], F32)
        xt = two(sb, "xt", [P, KC, GT], F32)
        wr_loaded, x_loaded = sem("wr_loaded"), two(sem, "x_loaded")
        stats_ready, var_ready, dev_ready, scaled = sem("stats_ready"), sem("var_ready"), sem("dev_ready"), sem("scaled")
        xn_ready, kept_rows = sem("xn_ready"), sem("kept_rows")
        turned, xt_ready, made, kept = sem("turned"), sem("xt_ready"), sem("made"), sem("kept")
        passed = sem("passed")
        ended = ExitStack()
        block = ended.enter_context(nc.Block())
        turn_bank = [m["bank"][0:2], m["bank"][2:4]]
        logit_bank = m["bank"][4:6]
        x_rows = x_in.rearrange("(g b) s d -> g s b d", b=G)

        @block.sync
        def _(sp):
            sp.dma_start(wr[:, :, :], a["L1_ffn_Wr"].rearrange("(c p) e -> p c e", p=P)).then_inc(wr_loaded, 16)

            def body(s):
                if s.exists(NG):
                    wait(sp, xn_ready, s.back(2).value + 1 if s.back(2).exists(NG) else 0)
                    sp.dma_start(xg[s.slot][:, :, :], take(x_rows, s.value)).then_inc(x_loaded[s.slot], 16)

            run_steps(sp, NG, 0, body)

        @block.tensor
        def _(pe):
            pe.wait_ge(wr_loaded, 16)

            def body(s):
                p, q = s.back(1), s.back(2)
                if q.exists(NG):
                    pe.wait_ge(xt_ready, KC * (q.value + 1))
                    wait(pe, kept, q.back(2).value + 1 if q.back(2).exists(NG) else 0)
                    for b in range(G):
                        for c in range(KC):
                            last = pe.matmul(logit_bank[q.slot][0:S, b * E:(b + 1) * E], xt[q.slot][:, c, b * S:(b + 1) * S],
                                             wr[:, c, :], start=c == 0, stop=c == KC - 1)
                    last.then_inc(made, 1)
                if p.exists(NG):
                    pe.wait_ge(xn_ready, p.value + 1)
                    wait(pe, xt_ready, KC * (p.back(2).value + 1) if p.back(2).exists(NG) else 0)
                    for c in range(KC):
                        for b in range(G):
                            last = pe.transpose(turn_bank[p.slot][c][:, b * S:(b + 1) * S],
                                                xn[p.slot][:, b, c * P:(c + 1) * P], m["ident"][0:S, 0:S])
                        last.then_inc(turned, 1)

            run_steps(pe, NG, 2, body)

        @block.gpsimd
        def _(pool):
            groups = x_normed[:, :, :].rearrange("s (g b) d -> s g (b d)", b=G)

            def body(s):
                hold(pool, xn_ready, s.value + 1, passed)
                at = groups[:, s.value, :] if isinstance(s.value, int) else groups[:, bass.ds(s.value, 1), :].squeeze(1)
                pool.tensor_copy(at, xn[s.slot][:, :, :].rearrange("s b d -> s (b d)")).then_inc(kept_rows, 1)

            run_steps(pool, NG, 0, body)

        @block.scalar
        def _(act):
            def body(s):
                p = s.back(1)
                if s.exists(NG):
                    act.wait_ge(var_ready, s.value + 1)
                    act.activation(dev[:, :], mean_var[:, :, 1], ACT.Sqrt, bias=m["eps"][0:S, :]).then_inc(dev_ready, 1)
                if p.exists(NG):
                    wait(act, made, p.back(2).value + 1 if p.back(2).exists(NG) else 0)
                    for c in range(KC):
                        act.wait_ge(turned, KC * p.value + c + 1)
                        act.activation(xt[p.slot][:, c, :], turn_bank[p.slot][c][:, 0:GT], ACT.Copy).then_inc(xt_ready, 1)

            run_steps(act, NG, 1, body)

        @block.vector
        def _(dve):
            def body(s):
                p, q = s.back(1), s.back(2)
                if p.exists(NG):
                    dve.wait_ge(dev_ready, p.value + 1)
                    dve.reciprocal(scale[:, :], dev[:, :]).then_inc(scaled, 1)
                    dve.wait_ge(scaled, p.value + 1)
                    wait(dve, turned, KC * (p.back(2).value + 1) if p.back(2).exists(NG) else 0)
                    wait(dve, kept_rows, p.back(2).value + 1 if p.back(2).exists(NG) else 0)
                    for b in range(G):
                        last = dve.tensor_scalar(xn[p.slot][:, b, :], xg[p.slot][:, b, :], mean_var[:, b, 0:1],
                                                 scale[:, b:b + 1], ALU.subtract, ALU.mult)
                    last.then_inc(xn_ready, 1)
                if s.exists(NG):
                    dve.wait_ge(x_loaded[s.slot], 16 * (s.pair + 1))
                    wait(dve, xn_ready, s.value)
                    for b in range(G):
                        last = dve.bn_stats(stats[:, b, :], xg[s.slot][:, b, :])
                    last.then_inc(stats_ready, 1)
                    hold(dve, stats_ready, s.value + 1, passed)
                    for b in range(G):
                        last = dve.bn_aggr(mean_var[:, b, :], stats[:, b, :])
                    last.then_inc(var_ready, 1)
                if q.exists(NG):
                    dve.wait_ge(made, q.value + 1)
                    dst = route["logits"][:, :, :].rearrange("s (g b) e -> s g (b e)", b=G)
                    at = dst[:, q.value, :] if isinstance(q.value, int) else dst[:, bass.ds(q.value, 1), :].squeeze(1)
                    dve.tensor_scalar(at, logit_bank[q.slot][0:S, 0:G * E], 1.0, None, ALU.mult).then_inc(kept, 1)

            run_steps(dve, NG, 2, body)

        ended.close()
        sems.clear()


def ranks_phase(nc, m, route):
    with ExitStack() as ctx:
        sems = Semaphores(nc, ctx)
        def sb(name, shape=(S, B, E), dt=F32):
            return ctx.enter_context(nc.sbuf_tensor(name + "_k", list(shape), dt))

        def sem(name):
            return sems.new(name + "_k")

        before = sb("before", (S, S))
        ones = sb("ones", (S, S))
        number = sb("number")
        top, first, prob, rank, kept, base = (sb(n, (S, B)) for n in ("top", "first", "prob", "rank", "kept", "base"))
        shifted, power, equal, chosen, counts, total = (sb(n) for n in ("shifted", "power", "equal", "chosen", "counts", "total"))
        sums = [sb(f"sums{n}") for n in range(2)]
        step, made, product, powered = sem("step"), sem("made"), sem("product"), sem("powered")
        passed = sem("passed")
        ended = ExitStack()
        block = ended.enter_context(nc.Block())
        rank_bank, count_bank = m["bank"][0], m["bank"][1]

        @block.gpsimd
        def _(pool):
            pool.memset(before[:, :], 0.0).then_inc(made, 1)
            pool.memset(ones[:, :], 1.0).then_inc(made, 1)
            pool.wait_ge(made, 2)
            pool.affine_select(out=before[:, :], in_=before[:, :], compare_op=ALU.is_ge, fill=1.0, base=0,
                               pattern=[[-1, S]], channel_multiplier=1).then_inc(made, 1)
            for e in range(E):
                pool.memset(number[:, :, e], float(e - E)).then_inc(made, 1)

        @block.scalar
        def _(act):
            act.wait_ge(step, 2)
            act.activation(power[:, :, :], shifted[:, :, :], ACT.Exp).then_inc(powered, 1)

        @block.tensor
        def _(pe):
            pe.wait_ge(made, 3)
            pe.wait_ge(step, 6)
            pe.matmul(rank_bank[0:S, 0:B * E], before[:, :], chosen[:, :, :].rearrange("s b e -> s (b e)"),
                      start=True, stop=True).then_inc(product, 1)
            pe.matmul(count_bank[0:S, 0:B * E], ones[:, :], chosen[:, :, :].rearrange("s b e -> s (b e)"),
                      start=True, stop=True).then_inc(product, 1)

        @block.vector
        def _(dve):
            done = 0

            def link(ins):
                nonlocal done
                done += 1
                ins.then_inc(step, 1)
                dve.wait_ge(step, done)

            def wide(t):
                return t[:, :].unsqueeze(2).to_broadcast([S, B, E])

            logits = route["logits"]
            link(dve.tensor_reduce(top[:, :], logits[:, :, :], AX.X, ALU.max))
            link(dve.tensor_tensor(shifted[:, :, :], logits[:, :, :], wide(top), ALU.subtract))
            link(dve.tensor_scalar(equal[:, :, :], shifted[:, :, :], 0.0, None, ALU.is_equal))
            dve.wait_ge(made, 3 + E)
            link(dve.tensor_tensor(equal[:, :, :], equal[:, :, :], number[:, :, :], ALU.mult))
            link(dve.tensor_reduce(first[:, :], equal[:, :, :], AX.X, ALU.min))
            link(dve.tensor_tensor(chosen[:, :, :], number[:, :, :], wide(first), ALU.is_equal))
            dve.wait_ge(powered, 1)
            link(dve.tensor_reduce(prob[:, :], power[:, :, :], AX.X, ALU.add))
            link(dve.reciprocal(prob[:, :], prob[:, :]))
            dve.wait_ge(product, 2)
            link(dve.tensor_copy(counts[:, :, :].rearrange("s b e -> s (b e)"), count_bank[0:S, 0:B * E]))
            old = counts
            shift, turn = 1, 0
            while shift < B:
                new = sums[turn]
                link(dve.tensor_copy(new[:, 0:shift, :], old[:, 0:shift, :]))
                link(dve.tensor_tensor(new[:, shift:B, :], old[:, shift:B, :], old[:, 0:B - shift, :], ALU.add))
                old, shift, turn = new, 2 * shift, 1 - turn
            link(dve.tensor_tensor(total[:, :, :], old[:, :, :], counts[:, :, :], ALU.subtract))
            link(dve.tensor_tensor(total[:, :, :].rearrange("s b e -> s (b e)"), rank_bank[0:S, 0:B * E],
                                   total[:, :, :].rearrange("s b e -> s (b e)"), ALU.add))
            link(dve.tensor_tensor(total[:, :, :], total[:, :, :], chosen[:, :, :], ALU.mult))
            link(dve.tensor_reduce(rank[:, :], total[:, :, :], AX.X, ALU.add))
            link(dve.tensor_scalar(kept[:, :], rank[:, :], float(CAP), None, ALU.is_lt))
            link(dve.tensor_scalar(base[:, :], first[:, :], float(CAP), float(E * CAP), ALU.mult, ALU.add))
            link(dve.tensor_scalar(rank[:, :], rank[:, :], float(CAP - 1), None, ALU.min))
            link(dve.tensor_tensor(base[:, :], base[:, :], rank[:, :], ALU.add))
            link(dve.tensor_copy(route["get"][:, :], base[:, :]))
            link(dve.tensor_scalar(rank[:, :], kept[:, :], -float(2 * E * CAP), float(2 * E * CAP), ALU.mult, ALU.add))
            link(dve.tensor_tensor(route["put"][:, :], base[:, :], rank[:, :], ALU.add))
            link(dve.tensor_tensor(prob[:, :], prob[:, :], kept[:, :], ALU.mult))
            link(dve.tensor_scalar(route["weight"][:, :], prob[:, :], m["gate"][0:S, 3:4], None, ALU.mult))

        ended.close()
        sems.clear()


def copy_index(dve, slot, table, s):
    groups = table[:, :].rearrange("s (g b) -> s g b", b=G)
    at = groups[:, s.value, :] if isinstance(s.value, int) else groups[:, bass.ds(s.value, 1), :].squeeze(1)
    return dve.tensor_scalar(slot[:, :], at, 0.0, None, ALU.add)


def experts_phase(nc, m, a, x_normed, route, expert_in, expert_out):
    with ExitStack() as ctx:
        sems = Semaphores(nc, ctx)
        def sb(name, shape, dt):
            return ctx.enter_context(nc.sbuf_tensor(name + "_e", shape, dt))

        def sem(name):
            return sems.new(name + "_e")

        def two(make, name, *args):
            return [make(f"{name}{n}", *args) for n in range(2)]

        w1_in, w2_in = two(sb, "w1_in", [P, KC, F], F32), two(sb, "w2_in", [P, FC, D], F32)
        w1 = [two(sb, f"w1_{part}", [P, KC, F], F16) for part in ("high", "low")]
        w2 = [two(sb, f"w2_{part}", [P, FC, D], F16) for part in ("high", "low")]
        xg = two(sb, "xg", [S, G, D], F32)
        x_high, x_low = sb("x_high", [P, KC, GT], F16), sb("x_low", [P, KC, GT], F16)
        h_high, h_low = sb("h_high", [P, FC, GT], F16), sb("h_low", [P, FC, GT], F16)
        y = two(sb, "y", [S, G, D], F32)
        x_loaded, w_loaded, stored = two(sem, "x_loaded"), two(sem, "w_loaded"), two(sem, "stored")
        w_high_ready, w_low_ready = sem("w_high_ready"), sem("w_low_ready")
        turned, x_high_ready, x_low_ready = sem("turned"), sem("x_high_ready"), sem("x_low_ready")
        z_made, h_high_ready, h_low_ready, y_made = sem("z_made"), sem("h_high_ready"), sem("h_low_ready"), sem("y_made")
        y_even_ready, y_odd_ready, put = sem("y_even_ready"), sem("y_odd_ready"), sem("put")
        passed = sem("passed")
        ended = ExitStack()
        block = ended.enter_context(nc.Block())
        z_bank, y_bank, turn_bank = m["bank"][0:4], m["bank"][4:6], m["bank"][6:8]
        in_rows = expert_in.rearrange("(e t s) d -> e s t d", e=E, s=S)
        out_rows = expert_out.rearrange("(e t s) d -> e s t d", e=E, s=S)
        w1_rows = a["L1_ffn_W1"].rearrange("e (c p) f -> e p c f", p=P)
        w2_rows = a["L1_ffn_W2"].rearrange("e (c p) d -> e p c d", p=P)
        HG = G // 2
        PIECES = FC

        def piece(first, second, n):
            half = PIECES // 2
            if n < half:
                c, part = divmod(n, half // KC)
                width = F * KC // half
                return first[:, c, part * width:(part + 1) * width]
            rows = FC // half
            return second[:, (n - half) * rows:(n - half + 1) * rows, :]

        @block.sync
        def _(sp):
            def body(s):
                if s.exists(E):
                    wait(sp, w_low_ready, PIECES * (s.back(2).value + 1) if s.back(2).exists(E) else 0)
                    sp.dma_start(w1_in[s.slot][:, :, :], take(w1_rows, s.value)).then_inc(w_loaded[s.slot], 16)
                    sp.dma_start(w2_in[s.slot][:, :, :], take(w2_rows, s.value)).then_inc(w_loaded[s.slot], 16)
                    if isinstance(s.value, int) and s.value == 0:
                        sp.wait_ge(put, 16 * B)
                    wait(sp, turned, KC * (s.back(2).value + 1) if s.back(2).exists(E) else 0)
                    sp.dma_start(xg[s.slot][:, :, :], take(in_rows, s.value)).then_inc(x_loaded[s.slot], 16)

            run_steps(sp, E, 1, body)

        @block.gpsimd
        def _(pool):
            def body(s):
                p = s.back(1)
                if p.exists(E):
                    pool.wait_ge(y_even_ready, HG * (p.value + 1))
                    hold(pool, y_odd_ready, HG * (p.value + 1), passed)
                    pool.dma_start(take(out_rows, p.value), y[p.slot][:, :, :]).then_inc(stored[p.slot], 16)

            pool.wait_ge(m["experts_cleared"], 16)
            for b in range(B):
                pool.indirect_dma_start(expert_in[:, :], bass.IndirectOffsetOnAxis(route["put"][:, b:b + 1], 0),
                                        x_normed[:, b, :], None, bounds_check=E * CAP - 1,
                                        oob_is_err=False).then_inc(put, 16)
            run_steps(pool, E, 1, body)
            for n in range(2):
                pool.wait_ge(stored[n], 16 * E // 2)

        @block.tensor
        def _(pe):
            def turn(s):
                pe.wait_ge(x_loaded[s.slot], 16 * (s.pair + 1))
                wait(pe, x_low_ready, KC * s.value)
                for c in range(KC):
                    for b in range(G):
                        last = pe.transpose(turn_bank[c][:, b * S:(b + 1) * S], xg[s.slot][:, b, c * P:(c + 1) * P],
                                            m["ident"][0:S, 0:S])
                    last.then_inc(turned, 1)

            def body(s):
                p = s.back(1)
                for j in range(FC):
                    if p.exists(E):
                        if j == 0:
                            pe.wait_ge(w_low_ready, PIECES * (p.value + 1))
                            pe.wait_ge(x_low_ready, KC * (p.value + 1))
                        wait(pe, h_low_ready, FC * p.value + j - 3)
                        cols = slice(j * P, (j + 1) * P)
                        (high, low), slot = w1, p.slot
                        for c in range(KC):
                            for n, (w, x) in enumerate(((high, x_high), (high, x_low), (low, x_high))):
                                last = pe.matmul(z_bank[j % 4][:, 0:GT], w[slot][:, c, cols], x[:, c, :],
                                                 start=c == 0 and n == 0, stop=c == KC - 1 and n == 2)
                        last.then_inc(z_made, 1)
                    if s.exists(E) and j == FC - 1:
                        turn(s)
                if p.exists(E):
                    (high, low), slot = w2, p.slot
                    for b in range(G):
                        wait(pe, (y_even_ready, y_odd_ready)[b % 2], HG * p.value + b // 2)
                        for c in range(FC):
                            if b == 0:
                                pe.wait_ge(h_low_ready, FC * p.value + c + 1)
                            for n, (h, w) in enumerate(((h_high, high), (h_high, low), (h_low, high))):
                                last = pe.matmul(y_bank[b % 2][0:S, 0:D], h[:, c, b * S:(b + 1) * S], w[slot][:, c, :],
                                                 start=c == 0 and n == 0, stop=c == FC - 1 and n == 2)
                        last.then_inc(y_made, 1)

            run_steps(pe, E, 1, body)

        @block.scalar
        def _(act):
            def split_piece(s, n):
                if n == 0:
                    act.wait_ge(w_loaded[s.slot], 32 * (s.pair + 1))
                    wait(act, y_made, G * (s.back(2).value + 1) if s.back(2).exists(E) else 0)
                act.activation(piece(w1[0][s.slot], w2[0][s.slot], n), piece(w1_in[s.slot], w2_in[s.slot], n),
                               ACT.Copy, scale=W_SCALE).then_inc(w_high_ready, 1)

            def second_half(s, now):
                for n in range(PIECES // 2, PIECES):
                    if now and s.exists(E):
                        split_piece(s, n)

            def body(s):
                p = s.back(1)
                if p.exists(E):
                    wait(act, y_made, G * p.value)
                for j in range(FC):
                    if p.exists(E):
                        act.wait_ge(z_made, FC * p.value + j + 1)
                        act.activation(h_high[:, j, :], z_bank[j % 4][:, 0:GT], ACT.Relu).then_inc(h_high_ready, 1)
                    if s.exists(E) and j % 2:
                        split_piece(s, j // 2)
                second_half(s, not p.exists(E))
                if s.exists(E):
                    for c in range(KC):
                        act.wait_ge(turned, KC * s.value + c + 1)
                        act.activation(x_high[:, c, :], turn_bank[c][:, 0:GT], ACT.Copy).then_inc(x_high_ready, 1)
                if p.exists(E):
                    wait(act, stored[p.slot], 16 * p.pair)
                for b in range(G):
                    if s.exists(E) and p.exists(E):
                        split_piece(s, PIECES // 2 + b)
                    if p.exists(E) and b % 2 == 0:
                        act.wait_ge(y_made, G * p.value + b + 1)
                        act.activation(y[p.slot][:, b, :], y_bank[0][0:S, 0:D], ACT.Copy,
                                       scale=W_SCALE ** -2).then_inc(y_even_ready, 1)

            run_steps(act, E, 1, body)

        @block.vector
        def _(dve):
            def split_piece(s, n):
                dve.wait_ge(w_high_ready, PIECES * s.value + n + 1)
                dve.scalar_tensor_tensor(out=piece(w1[1][s.slot], w2[1][s.slot], n),
                                         in0=piece(w1_in[s.slot], w2_in[s.slot], n), scalar=W_SCALE,
                                         in1=piece(w1[0][s.slot], w2[0][s.slot], n),
                                         op0=ALU.mult, op1=ALU.subtract).then_inc(w_low_ready, 1)

            def second_half(s, now):
                for n in range(PIECES // 2, PIECES):
                    if now and s.exists(E):
                        split_piece(s, n)

            def body(s):
                p = s.back(1)
                for j in range(FC):
                    if p.exists(E):
                        dve.wait_ge(h_high_ready, FC * p.value + j + 1)
                        dve.scalar_tensor_tensor(out=h_low[:, j, :], in0=z_bank[j % 4][:, 0:GT], scalar=0.0,
                                                 in1=h_high[:, j, :], op0=ALU.max, op1=ALU.subtract).then_inc(h_low_ready, 1)
                    if s.exists(E) and j % 2:
                        split_piece(s, j // 2)
                second_half(s, not p.exists(E))
                if s.exists(E):
                    for c in range(KC):
                        dve.wait_ge(x_high_ready, KC * s.value + c + 1)
                        dve.tensor_tensor(x_low[:, c, :], turn_bank[c][:, 0:GT], x_high[:, c, :],
                                          ALU.subtract).then_inc(x_low_ready, 1)
                if p.exists(E):
                    wait(dve, stored[p.slot], 16 * p.pair)
                for b in range(G):
                    if s.exists(E) and p.exists(E):
                        split_piece(s, PIECES // 2 + b)
                    if p.exists(E) and b % 2:
                        dve.wait_ge(y_made, G * p.value + b + 1)
                        dve.tensor_scalar(y[p.slot][:, b, :], y_bank[1][0:S, 0:D], W_SCALE ** -2, None,
                                          ALU.mult).then_inc(y_odd_ready, 1)

            run_steps(dve, E, 1, body)

        ended.close()
        sems.clear()


def combine_phase(nc, route, x_in, expert_out, out):
    with ExitStack() as ctx:
        sems = Semaphores(nc, ctx)
        def sb(name, shape, dt):
            return ctx.enter_context(nc.sbuf_tensor(name + "_c", shape, dt))

        def sem(name):
            return sems.new(name + "_c")

        def two(make, name, *args):
            return [make(f"{name}{n}", *args) for n in range(2)]

        xg, y, total = (two(sb, name, [S, G, D], F32) for name in ("xg", "y", "total"))
        index = two(sb, "index", [S, G], U32)
        weight = sb("weight", [S, G], F32)
        x_loaded, got, stored = two(sem, "x_loaded"), two(sem, "got"), two(sem, "stored")
        index_ready, weight_ready, added = sem("index_ready"), sem("weight_ready"), sem("added")
        passed = sem("passed")
        ended = ExitStack()
        block = ended.enter_context(nc.Block())
        x_rows = x_in.rearrange("(g b) s d -> g s b d", b=G)
        out_rows = out.rearrange("(g b) s d -> g s b d", b=G)

        @block.sync
        def _(sp):
            def body(s):
                p = s.back(1)
                if s.exists(NG):
                    wait(sp, added, s.back(2).value + 1 if s.back(2).exists(NG) else 0)
                    sp.dma_start(xg[s.slot][:, :, :], take(x_rows, s.value)).then_inc(x_loaded[s.slot], 16)
                if p.exists(NG):
                    sp.wait_ge(added, p.value + 1)
                    sp.dma_start(take(out_rows, p.value), total[p.slot][:, :, :]).then_inc(stored[p.slot], 16)

            run_steps(sp, NG, 1, body)
            for n in range(2):
                sp.wait_ge(stored[n], 16 * NG // 2)

        @block.gpsimd
        def _(pool):
            def body(s):
                if s.exists(NG):
                    pool.wait_ge(index_ready, s.value + 1)
                    hold(pool, added, s.back(2).value + 1 if s.back(2).exists(NG) else 0, passed)
                    for b in range(G):
                        pool.indirect_dma_start(y[s.slot][:, b, :], None, expert_out[:, :],
                                                bass.IndirectOffsetOnAxis(index[s.slot][:, b:b + 1], 0)
                                                ).then_inc(got[s.slot], 16)

            run_steps(pool, NG, 1, body)

        @block.vector
        def _(dve):
            def body(s):
                p = s.back(1)
                if s.exists(NG):
                    wait(dve, got[s.slot], 16 * G * s.pair)
                    copy_index(dve, index[s.slot], route["get"], s).then_inc(index_ready, 1)
                if p.exists(NG):
                    wait(dve, added, p.value)
                    copy_index(dve, weight, route["weight"], p).then_inc(weight_ready, 1)
                    dve.wait_ge(weight_ready, p.value + 1)
                    dve.wait_ge(x_loaded[p.slot], 16 * (p.pair + 1))
                    dve.wait_ge(got[p.slot], 16 * G * (p.pair + 1))
                    wait(dve, stored[p.slot], 16 * p.pair)
                    for b in range(G):
                        last = dve.scalar_tensor_tensor(out=total[p.slot][:, b, :], in0=y[p.slot][:, b, :],
                                                        scalar=weight[:, b:b + 1], in1=xg[p.slot][:, b, :],
                                                        op0=ALU.mult, op1=ALU.add)
                    last.then_inc(added, 1)

            run_steps(dve, NG, 1, body)

        ended.close()
        sems.clear()


_INS = ["x", "ctx_1024", "mask_1x1xSxS2_ik1", "mask_BxSxS2_if1", "g_xattn", "g_ffn",
        "L0_xattn_w_q", "L0_xattn_w_k", "L0_xattn_w_v", "L0_xattn_w_o", "L0_xattn_b_o",
        "L0_ffn_k0", "L0_ffn_k1", "L0_ffn_k2", "L0_ffn_s0", "L0_ffn_s1", "L0_ffn_s2",
        "L1_xattn_Wq", "L1_xattn_Wk", "L1_xattn_Wv", "L1_xattn_Wo", "L1_xattn_bo",
        "L1_ffn_Wr", "L1_ffn_W1", "L1_ffn_W2"]


def laid_out(name, a):
    if name == "ctx_1024":
        a = a.transpose(0, 2, 1)
    if name.startswith("L1_xattn_W"):
        a = a.T
    if name[-1] in "qk" and "xattn" in name and a.ndim == 2:
        a = a.reshape(D, NP, 2, DK).transpose(0, 2, 3, 1).reshape(D, D)
    return a


def kernel(**inputs):
    import numpy as _np
    import concourse.bacc as _bacc
    from concourse import mybir as _mybir
    from concourse.bass_utils import run_bass_kernel_spmd as _run

    nc = _bacc.Bacc("TRN2", target_bir_lowering=False, num_devices=1)
    arrays, args = {}, {}
    for name in _INS:
        a = _np.ascontiguousarray(laid_out(name, _np.asarray(inputs[name])))
        if a.ndim == 0:
            a = a.reshape(1)
        arrays[f"in_{name}_dram"] = a
        args[name] = nc.dram_tensor(f"in_{name}_dram", a.shape, _mybir.dt.from_np(a.dtype), kind="ExternalInput").ap()
    out = nc.dram_tensor("out_0_dram", (B, S, D), F32, kind="ExternalOutput").ap()
    flamingo_program(nc, args, out)
    r = _run(nc, [arrays], core_ids=[0])
    return r.results[0]["out_0_dram"]
```
